# Optimizing a Trainium2 kernel written in Bass

```python
import numpy as np
import jax
import jax.numpy as jnp

def _softmax(x, axis=-1):
    return jax.nn.softmax(x, axis=axis)

def _gelu(x):
    return jax.nn.gelu(x, approximate=True)

def _silu(x):
    return jax.nn.silu(x)

def _sigmoid(x):
    return jax.nn.sigmoid(x)

def _layernorm(x, axis=-1, eps=1e-05):
    m = jnp.mean(x, axis=axis, keepdims=True)
    v = jnp.var(x, axis=axis, keepdims=True)
    return (x - m) / jnp.sqrt(v + eps)

def _scatter_add(tgt, idx, src, axis=0):
    return tgt.at[idx].add(src)

def _segment_sum(src, seg, n):
    return jax.ops.segment_sum(src, seg, n)
kernel_name = 'mk_decoder_preln_d1_seqx_r8_0eb1ec'

def setup_inputs(seed: int=0):
    np.random.seed(seed)
    _w = jnp.asarray

    def _rec_inputs():
        import jax
        import jax.numpy as jnp
        _rk = jax.random.key(seed)
        x = -0.0002928 + 1 * jax.random.normal(jax.random.fold_in(_rk, 1), (32, 56, 128), jnp.float32)
        _lenS = 56 - jax.random.randint(jax.random.fold_in(_rk, 7), (32,), 0, max(1, 56 // 4) + 1, jnp.int32)
        _lenS2 = 1500 - jax.random.randint(jax.random.fold_in(_rk, 8), (32,), 0, max(1, 1500 // 4) + 1, jnp.int32)
        _ctx_1024P = jax.random.normal(jax.random.fold_in(_rk, 11), (32, 16, 128), jnp.float32)
        _ctx_1024c = jax.random.dirichlet(jax.random.fold_in(_rk, 511), 0.3 * jnp.ones((16,), jnp.float32), (32, 1500))
        _ctx_1024t = jnp.einsum('bsk,bkd->bsd', _ctx_1024c, _ctx_1024P)
        _ctx_1024t = _ctx_1024t * jax.lax.rsqrt(jnp.mean(jnp.square(_ctx_1024t)) + 1e-12) * 0.953939
        ctx_1024 = -1.39393e-06 + 0.999914 * (_ctx_1024t + 0.3 * jax.random.normal(jax.random.fold_in(_rk, 611), (32, 1500, 128), jnp.float32))
        return (x, ctx_1024)
    x, ctx_1024 = _rec_inputs()

    def _L0_attn_setup():
        import jax, jax.numpy as jnp
        import numpy as np
        from jax import lax
        B, S, D = (16, 128, 128)
        PE = 20
        NB = 3
        EPS = 1e-12

        def _lstm(x, W_ih, W_hh, b_ih, b_hh):
            b, _, _ = x.shape
            H = W_hh.shape[1]
            xg = jnp.einsum('bsd,gd->bsg', x, W_ih) + b_ih + b_hh

            def step(carry, xg_t):
                h, c = carry
                g = xg_t + h @ W_hh.T
                i, f, gg, o = jnp.split(g, 4, axis=-1)
                c = jax.nn.sigmoid(f) * c + jax.nn.sigmoid(i) * jnp.tanh(gg)
                h = jax.nn.sigmoid(o) * jnp.tanh(c)
                return ((h, c), h)
            init = (jnp.zeros((b, H), x.dtype), jnp.zeros((b, H), x.dtype))
            _, hs = lax.scan(step, init, xg.transpose(1, 0, 2))
            return hs.transpose(1, 0, 2)

        def _forward(x, W_ih, W_hh, b_ih, b_hh, W_mu, b_mu, W_sig, b_sig):
            b, s, d = x.shape
            pw = _lstm(x, W_ih, W_hh, b_ih, b_hh)
            mu_w = jax.nn.relu(jnp.einsum('bsp,np->bsn', pw, W_mu) + b_mu)
            sigma = jax.nn.sigmoid(jnp.einsum('bsp,op->bso', pw, W_sig) + b_sig)[..., 0]
            j_idx = jnp.arange(s, dtype=x.dtype)

            def mu_step(prev_mu, inputs):
                w_t, j = inputs
                mu = w_t[:, 0] * prev_mu + w_t[:, 1] / s + w_t[:, 2] * (j + 1.0) / s
                return (mu, mu)
            _, mus = lax.scan(mu_step, jnp.zeros((b,), x.dtype), (mu_w.transpose(1, 0, 2), j_idx))
            mu = mus.T
            i_idx = jnp.arange(s, dtype=x.dtype)
            rel = i_idx[None, :] / (j_idx[:, None] + 1.0)
            mask = i_idx[None, :] <= j_idx[:, None]
            w = jnp.exp(-(rel[None] - mu[:, :, None]) ** 2 / (2.0 * sigma[:, :, None] ** 2))
            w = jnp.where(mask[None], w, 0.0)
            norm = jnp.sqrt(jnp.sum(w * w, axis=-1, keepdims=True))
            w = w / jnp.maximum(norm, EPS)
            context = jnp.einsum('bji,bid->bjd', w, x)
            return context
        key = jax.random.key(seed)
        ks = jax.random.split(key, 10)
        s = lambda *sh: 0.05
        inp = {'x': jax.random.normal(ks[0], (B, S, D), dtype=jnp.float32), 'W_ih': jax.random.normal(ks[1], (4 * PE, D), dtype=jnp.float32) * 0.02, 'W_hh': jax.random.normal(ks[2], (4 * PE, PE), dtype=jnp.float32) * 0.02, 'b_ih': jax.random.normal(ks[3], (4 * PE,), dtype=jnp.float32) * 0.02, 'b_hh': jax.random.normal(ks[4], (4 * PE,), dtype=jnp.float32) * 0.02, 'W_mu': jax.random.normal(ks[5], (NB, PE), dtype=jnp.float32) * 0.1, 'b_mu': jax.random.normal(ks[6], (NB,), dtype=jnp.float32) * 0.1, 'W_sig': jax.random.normal(ks[7], (1, PE), dtype=jnp.float32) * 0.1, 'b_sig': jax.random.normal(ks[8], (1,), dtype=jnp.float32) * 0.1}
        return inp
    _L0_attn_all = _L0_attn_setup()
    _L0_attn_in = {k: v for k, v in _L0_attn_all.items() if k in ('W_ih', 'W_hh', 'b_ih', 'b_hh', 'W_mu', 'b_mu', 'W_sig', 'b_sig')}
    del _L0_attn_all

    def _L0_xattn_setup():
        import jax, jax.numpy as jnp
        import numpy as np
        import math
        D_MODEL = 128
        HEADS = 16
        DK = 64
        DV = 64
        key = jax.random.key(seed)
        ks = jax.random.split(key, 8)
        N, QL, KL = (2, 256, 256)
        s = 1.0 / math.sqrt(D_MODEL)
        return {'Q': jax.random.normal(ks[0], (N, QL, D_MODEL), jnp.float32), 'K': jax.random.normal(ks[1], (N, KL, D_MODEL), jnp.float32), 'V': jax.random.normal(ks[2], (N, KL, D_MODEL), jnp.float32), 'WQ': jax.random.normal(ks[3], (D_MODEL, HEADS * DK), jnp.float32) * s, 'WK': jax.random.normal(ks[4], (D_MODEL, HEADS * DK), jnp.float32) * s, 'WV': jax.random.normal(ks[5], (D_MODEL, HEADS * DV), jnp.float32) * s, 'WO': jax.random.normal(ks[6], (HEADS * DV, D_MODEL), jnp.float32) * (1.0 / math.sqrt(HEADS * DV)), 'bO': jnp.zeros((D_MODEL,), jnp.float32)}
    _L0_xattn_all = _L0_xattn_setup()
    _L0_xattn_in = {k: v for k, v in _L0_xattn_all.items() if k in ('WQ', 'WK', 'WV', 'WO', 'bO')}
    del _L0_xattn_all

    def _L0_ffn_setup():
        import jax, jax.numpy as jnp
        import numpy as np
        H = 128
        I = 512
        E = 4
        LN_EPS = 1e-12

        def _layer_norm(x, gamma, beta, eps=LN_EPS):
            mu = jnp.mean(x, axis=-1, keepdims=True)
            var = jnp.mean(jnp.square(x - mu), axis=-1, keepdims=True)
            return (x - mu) * jax.lax.rsqrt(var + eps) * gamma + beta
        key = jax.random.key(seed)
        ks = jax.random.split(key, 8)
        B, S = (4, 64)
        scale = 0.02
        return {'hidden_states': jax.random.normal(ks[0], (B, S, H), jnp.float32), 'W_router': jax.random.normal(ks[1], (H, E), jnp.float32) * scale, 'W1': jax.random.normal(ks[2], (E, H, I), jnp.float32) * scale, 'b1': jax.random.normal(ks[3], (E, I), jnp.float32) * scale, 'Wo': jax.random.normal(ks[4], (I, H), jnp.float32) * scale, 'bo': jax.random.normal(ks[5], (H,), jnp.float32) * scale, 'ln_gamma': jnp.ones((H,), jnp.float32), 'ln_beta': jnp.zeros((H,), jnp.float32)}
    _L0_ffn_all = _L0_ffn_setup()
    _L0_ffn_in = {k: v for k, v in _L0_ffn_all.items() if k in ('W_router', 'W1', 'b1', 'Wo', 'bo', 'ln_gamma', 'ln_beta')}
    del _L0_ffn_all
    return {'x': x, 'ctx_1024': ctx_1024, 'L0_attn_W_ih': _L0_attn_in['W_ih'], 'L0_attn_W_hh': _L0_attn_in['W_hh'], 'L0_attn_b_ih': _L0_attn_in['b_ih'], 'L0_attn_b_hh': _L0_attn_in['b_hh'], 'L0_attn_W_mu': _L0_attn_in['W_mu'], 'L0_attn_b_mu': _L0_attn_in['b_mu'], 'L0_attn_W_sig': _L0_attn_in['W_sig'], 'L0_attn_b_sig': _L0_attn_in['b_sig'], 'L0_xattn_WQ': _L0_xattn_in['WQ'], 'L0_xattn_WK': _L0_xattn_in['WK'], 'L0_xattn_WV': _L0_xattn_in['WV'], 'L0_xattn_WO': _L0_xattn_in['WO'], 'L0_xattn_bO': _L0_xattn_in['bO'], 'L0_ffn_W_router': _L0_ffn_in['W_router'], 'L0_ffn_W1': _L0_ffn_in['W1'], 'L0_ffn_b1': _L0_ffn_in['b1'], 'L0_ffn_Wo': _L0_ffn_in['Wo'], 'L0_ffn_bo': _L0_ffn_in['bo'], 'L0_ffn_ln_gamma': _L0_ffn_in['ln_gamma'], 'L0_ffn_ln_beta': _L0_ffn_in['ln_beta']}

def reference(x, ctx_1024, L0_attn_W_ih, L0_attn_W_hh, L0_attn_b_ih, L0_attn_b_hh, L0_attn_W_mu, L0_attn_b_mu, L0_attn_W_sig, L0_attn_b_sig, L0_xattn_WQ, L0_xattn_WK, L0_xattn_WV, L0_xattn_WO, L0_xattn_bO, L0_ffn_W_router, L0_ffn_W1, L0_ffn_b1, L0_ffn_Wo, L0_ffn_bo, L0_ffn_ln_gamma, L0_ffn_ln_beta):
    import jax
    import jax.numpy as jnp

    def _L0_attn_ref(x, W_ih, W_hh, b_ih, b_hh, W_mu, b_mu, W_sig, b_sig):
        import jax, jax.numpy as jnp
        import numpy as np
        from jax import lax
        B, S, D = (16, 128, 128)
        PE = 20
        NB = 3
        EPS = 1e-12

        def _lstm(x, W_ih, W_hh, b_ih, b_hh):
            b, _, _ = x.shape
            H = W_hh.shape[1]
            xg = jnp.einsum('bsd,gd->bsg', x, W_ih) + b_ih + b_hh

            def step(carry, xg_t):
                h, c = carry
                g = xg_t + h @ W_hh.T
                i, f, gg, o = jnp.split(g, 4, axis=-1)
                c = jax.nn.sigmoid(f) * c + jax.nn.sigmoid(i) * jnp.tanh(gg)
                h = jax.nn.sigmoid(o) * jnp.tanh(c)
                return ((h, c), h)
            init = (jnp.zeros((b, H), x.dtype), jnp.zeros((b, H), x.dtype))
            _, hs = lax.scan(step, init, xg.transpose(1, 0, 2))
            return hs.transpose(1, 0, 2)

        def _forward(x, W_ih, W_hh, b_ih, b_hh, W_mu, b_mu, W_sig, b_sig):
            b, s, d = x.shape
            pw = _lstm(x, W_ih, W_hh, b_ih, b_hh)
            mu_w = jax.nn.relu(jnp.einsum('bsp,np->bsn', pw, W_mu) + b_mu)
            sigma = jax.nn.sigmoid(jnp.einsum('bsp,op->bso', pw, W_sig) + b_sig)[..., 0]
            j_idx = jnp.arange(s, dtype=x.dtype)

            def mu_step(prev_mu, inputs):
                w_t, j = inputs
                mu = w_t[:, 0] * prev_mu + w_t[:, 1] / s + w_t[:, 2] * (j + 1.0) / s
                return (mu, mu)
            _, mus = lax.scan(mu_step, jnp.zeros((b,), x.dtype), (mu_w.transpose(1, 0, 2), j_idx))
            mu = mus.T
            i_idx = jnp.arange(s, dtype=x.dtype)
            rel = i_idx[None, :] / (j_idx[:, None] + 1.0)
            mask = i_idx[None, :] <= j_idx[:, None]
            w = jnp.exp(-(rel[None] - mu[:, :, None]) ** 2 / (2.0 * sigma[:, :, None] ** 2))
            w = jnp.where(mask[None], w, 0.0)
            norm = jnp.sqrt(jnp.sum(w * w, axis=-1, keepdims=True))
            w = w / jnp.maximum(norm, EPS)
            context = jnp.einsum('bji,bid->bjd', w, x)
            return context
        return _forward(x, W_ih, W_hh, b_ih, b_hh, W_mu, b_mu, W_sig, b_sig)

    def _L0_xattn_ref(Q, K, V, WQ, WK, WV, WO, bO):
        import jax, jax.numpy as jnp
        import numpy as np
        import math
        D_MODEL = 128
        HEADS = 16
        DK = 64
        DV = 64
        N, ql, _ = Q.shape
        kl = K.shape[1]
        q = (Q @ WQ).reshape(N, ql, HEADS, DK)
        k = (K @ WK).reshape(N, kl, HEADS, DK)
        v = (V @ WV).reshape(N, kl, HEADS, DV)
        compat = jnp.einsum('nqhk,nlhk->nhql', q, k) / math.sqrt(DK)
        weights = jax.nn.softmax(compat, axis=3)
        attn = jnp.einsum('nhqk,nkhv->nqhv', weights, v).reshape(N, ql, HEADS * DV)
        return attn @ WO + bO

    def _L0_ffn_ref(hidden_states, W_router, W1, b1, Wo, bo, ln_gamma, ln_beta):
        import jax, jax.numpy as jnp
        import numpy as np
        H = 128
        I = 512
        E = 4
        LN_EPS = 1e-12

        def _layer_norm(x, gamma, beta, eps=LN_EPS):
            mu = jnp.mean(x, axis=-1, keepdims=True)
            var = jnp.mean(jnp.square(x - mu), axis=-1, keepdims=True)
            return (x - mu) * jax.lax.rsqrt(var + eps) * gamma + beta
        B, S, _ = hidden_states.shape
        x = hidden_states.reshape(-1, H)
        logits = x @ W_router
        expert_idx = jnp.argmax(logits, axis=-1)
        h = jnp.einsum('th,ehi->tei', x, W1) + b1
        h = jax.nn.gelu(h, approximate=False)
        onehot = jax.nn.one_hot(expert_idx, E, dtype=x.dtype)
        intermediate = jnp.einsum('te,tei->ti', onehot, h)
        y = intermediate @ Wo + bo + x
        y = _layer_norm(y, ln_gamma, ln_beta)
        return y.reshape(B, S, H)
    x = x + _L0_attn_ref(_layernorm(x, axis=-1), L0_attn_W_ih, L0_attn_W_hh, L0_attn_b_ih, L0_attn_b_hh, L0_attn_W_mu, L0_attn_b_mu, L0_attn_W_sig, L0_attn_b_sig)
    x = x + _L0_xattn_ref(_layernorm(x, axis=-1), ctx_1024, ctx_1024, L0_xattn_WQ, L0_xattn_WK, L0_xattn_WV, L0_xattn_WO, L0_xattn_bO)
    x = x + _L0_ffn_ref(_layernorm(x, axis=-1), L0_ffn_W_router, L0_ffn_W1, L0_ffn_b1, L0_ffn_Wo, L0_ffn_bo, L0_ffn_ln_gamma, L0_ffn_ln_beta)
    return x

_drawn_inputs = setup_inputs


def setup_inputs(seed=0):
    import zlib

    import numpy as np

    out = dict(_drawn_inputs(seed))
    spreads = {'L0_xattn_bO': (0.0, 0.1), 'L0_ffn_ln_gamma': (1.0, 0.2), 'L0_ffn_ln_beta': (0.0, 0.1)}
    factors = {'L0_attn_W_ih': 4.667,
     'L0_attn_W_hh': 8.0,
     'L0_attn_b_ih': 8.0,
     'L0_attn_b_hh': 8.0,
     'L0_attn_W_mu': 6.05,
     'L0_attn_b_mu': 2.804,
     'L0_attn_W_sig': 8.0,
     'L0_ffn_W_router': 2.995,
     'L0_ffn_W1': 2.717,
     'L0_ffn_b1': 27.617,
     'L0_ffn_bo': 5.965}
    for name, (base, spread) in spreads.items():
        noise = np.random.default_rng([zlib.crc32(name.encode()), seed]).standard_normal(out[name].shape)
        drawn = base * np.exp(spread * noise) if base else spread * noise
        out[name] = jnp.asarray(drawn.astype(out[name].dtype))
    for name, factor in factors.items():
        out[name] = (out[name] * factor).astype(out[name].dtype)
    return out
```

```python
from contextlib import ExitStack

import concourse.bass as bass
from concourse import mybir

F32 = mybir.dt.float32
F32R = mybir.dt.float32r
I32 = mybir.dt.int32
ALU = mybir.AluOpType
ACT = mybir.ActivationFunctionType
AX = mybir.AxisListType


def decoder_layer(nc, x, ctx_1024, W_ih, W_hh, b_ih, b_hh, W_mu, b_mu, W_sig, b_sig,
                  WQ, WK, WV, WO, bO, W_router, W1, b1, Wo, bo, ln_gamma, ln_beta, out):
    B, S, D = x.shape
    L = ctx_1024.shape[1]
    PE = W_hh.shape[1]
    NB = W_mu.shape[0]
    E, _, FF = W1.shape
    DK = 64
    H = WQ.shape[1] // DK
    TOK = 2 * S
    PAIRS = B // 2
    CH = 12
    CR = L // CH
    HQ = H * S
    HALF = HQ // 2
    HB = H // 2
    RB = HQ // 128
    MP = 3
    MC = L // MP
    TG = CH // MP
    SCALE = 1.0 / DK ** 0.5
    G4 = 4
    MB = FF // 128
    GROUPS = PAIRS // G4
    GT = G4 * TOK
    U8 = 2 * G4
    ONEHOT_STEPS = 5 + 2 * (E - 1) - 1
    assert CR * CH == L and RB * 128 == HQ and PAIRS % G4 == 0 and S % U8 == 0

    with ExitStack() as stack:
        def sb(name, shape, dt=F32):
            return stack.enter_context(nc.sbuf_tensor(name, shape, dt))

        ps = stack.enter_context(nc.psum_tensor("ps", [128, 8, 512], F32))
        score_ps = [ps[0:CR, 2 * n:2 * n + 2, 0:HALF] for n in range(2)]
        usum_ps = ps[:, 4:6, 0:HALF]
        SIDE = 6

        resid = sb("resid", [TOK, PAIRS * D])
        resid_k = resid[:].rearrange("p (k d) -> p k d", k=PAIRS)
        xnorm = sb("xnorm", [TOK, PAIRS, D])
        xT = sb("xT", [D, PAIRS, TOK])
        ident = sb("ident", [128, 128])
        ones = sb("ones", [128, 128])
        ones_r = sb("ones_r", [128, 128], F32R)
        qk_w = sb("qk_w", [D, H, D])
        vo_w = sb("vo_w", [D, H, D])
        bO_row = sb("bO_row", [1, D])
        w1_sb = sb("w1_sb", [D, E, FF])
        b1_sb = sb("b1_sb", [E, FF])
        wo_sb = sb("wo_sb", [128, MB, D])
        rows_sb = sb("rows_sb", [1, 3, D])
        wr_sb = sb("wr_sb", [D, E])
        stats = sb("stats", [TOK, PAIRS, 6])
        meanvar = sb("meanvar", [TOK, PAIRS, 2])
        veps = sb("veps", [TOK, PAIRS])
        rstd = sb("rstd", [TOK, PAIRS])
        minus_half = sb("minus_half", [TOK, PAIRS])

        ctx_raw = [sb(f"ctx_raw{n}", [128, CH * D]) for n in range(2)]
        ctx_in = [r[0:CR, :].rearrange("p (c d) -> p c d", c=CH) for r in ctx_raw]
        ctx_hi = [sb(f"ctx_hi{n}", [CR, CH, D], F32R) for n in range(2)]
        ctx_lo = [sb(f"ctx_lo{n}", [CR, CH, D], F32R) for n in range(2)]
        ctxT_hi = [sb(f"ctxT_hi{n}", [D, L], F32R) for n in range(2)]
        ctxT_lo = [sb(f"ctxT_lo{n}", [D, L], F32R) for n in range(2)]
        q_hi = [sb(f"q_hi{n}", [D, HQ], F32R) for n in range(2)]
        q_lo = [sb(f"q_lo{n}", [D, HQ], F32R) for n in range(2)]
        p_hi = [sb(f"p_hi{n}", [CR, 2, HALF], F32R) for n in range(3)]
        p_lo = [sb(f"p_lo{n}", [CR, 2, HALF], F32R) for n in range(3)]
        max_diag = sb("max_diag", [128, HQ], F32R)
        max_parts = sb("max_parts", [128, RB * MP])
        max_all = sb("max_all", [128, RB])
        sum_recip = sb("sum_recip", [128, HALF])
        wo_raw = sb("wo_raw", [128, H // 2, D])

        ARENA = 12 * HQ
        arena = sb("arena", [128, ARENA])
        at = [0]

        def cut(size, parts=128):
            at[0] += size
            assert at[0] <= ARENA
            return arena[0:parts, at[0] - size:at[0]]

        neg_max = [cut(HQ).rearrange("p (a b) -> p a b", a=2) for n in range(2)]
        probs = [cut(HQ, CR).rearrange("p (a b) -> p a b", a=2) for n in range(3)]
        prob_sum = [cut(HQ, CR).rearrange("p (a b) -> p a b", a=2) for n in range(2)]
        u_raw = cut(HQ).rearrange("p (a b) -> p a b", a=2)
        u_norm = cut(2 * HQ).rearrange("p (h b q) -> p h b q", h=H, b=2)
        q_stage = cut(2 * HQ).rearrange("p (b h q) -> p b h q", b=2, h=H)

        at[0] = 0
        W = PAIRS * TOK
        gauss_d = cut(W, TOK).rearrange("p (k i) -> p k i", k=PAIRS)
        gauss_w = cut(W, TOK).rearrange("p (k i) -> p k i", k=PAIRS)
        gauss_wT = cut(W, TOK).rearrange("p (k j) -> p k j", k=PAIRS)
        lstm_h = cut(U8 * B).rearrange("p (u b) -> p u b", u=U8)
        w_in = cut(D)
        w_hh_in = cut(PE)
        w_head_in = cut(PE)
        wihT = cut(4 * PE)
        whhT = cut(4 * PE)
        headT = cut(NB + 1)
        gate_act = cut(4 * B, PE).rearrange("p (g b) -> p g b", g=4)
        cell = cut(B, PE)
        cell_f = cut(B, PE)
        cell_i = cut(B, PE)
        cell_t = cut(B, PE)
        mu_w = cut(U8 * NB, B).rearrange("p (t n) -> p t n", n=NB)
        mu_t = cut(U8, B)
        mu_b = cut(U8, B)
        mu = cut(S + 1, B)
        sig = cut(S, B)
        sig2 = cut(S, B)
        inv2s = cut(S, B)
        jp1 = cut(S, B)
        pick_b = cut(TOK, B).rearrange("p (b j) -> p b j", b=2)
        pick_k = cut(PAIRS, B)
        mu_l = cut(TOK, B).rearrange("p (b j) -> p b j", b=2)
        inv_l = cut(TOK, B).rearrange("p (b j) -> p b j", b=2)
        mu_tok = cut(2 * PAIRS, TOK).rearrange("p (a k) -> p a k", a=2)
        rel = cut(TOK, TOK)
        causal = cut(TOK, TOK)
        i_idx = cut(TOK, TOK)
        pos = cut(4, TOK)
        wsum = cut(PAIRS, TOK)
        jp1_int = cut(S, B).bitcast(I32)
        idx_int = cut(TOK, TOK).bitcast(I32)
        p_int = cut(1, TOK).bitcast(I32)

        wq_raw = ctx_raw[1][:, 0:H * DK]
        wk_raw = w1_sb[:].rearrange("p e f -> p (e f)")[:, 0:H * DK]
        wv_raw = w1_sb[:].rearrange("p e f -> p (e f)")[:, H * DK:2 * H * DK]
        wT_sb = sb("wT_sb", [128, 2, 3, D])

        at[0] = 0
        experts_in = cut(2 * E * D, TOK).rearrange("p (n e d) -> p n e d", n=2, e=E)
        expertsT = [cut(E * GT).rearrange("p (e k t) -> p e k t", e=E, k=G4) for n in range(2)]
        inter = [cut(MB * GT).rearrange("p (m t) -> p m t", m=MB) for n in range(2)]
        onehotT = cut(PAIRS * TOK, E)
        seen = cut(PAIRS, TOK)
        best = cut(PAIRS, TOK)
        logits = cut(PAIRS * E, TOK).rearrange("p (k e) -> p k e", e=E)
        is_best = cut(PAIRS * E, TOK).rearrange("p (k e) -> p k e", e=E)
        onehot = cut(PAIRS * E, TOK)
        onehot_k = onehot.rearrange("p (k e) -> p k e", e=E)
        rows_b = cut(3 * D, TOK).rearrange("p (n d) -> p n d", n=3)
        y_sb = ctx_raw[0][0:TOK, 0:2 * G4 * D].rearrange("p (n k d) -> p n k d", n=2, k=G4)
        o_sb = ctx_raw[1][0:TOK, 0:2 * G4 * D].rearrange("p (n k d) -> p n k d", n=2, k=G4)

        s = {name: stack.enter_context(nc.semaphore("s_" + name)) for name in (
            "x_in lstm_w_in bias_in attn_w_in ffn_w_in ctx_in0 ctx_in1 out_stored0 out_stored1 "
            "identity_made ones_made minus_made indices_made rel_made causal_made picks_made zeros_made "
            "biased_cleared lstm_w_ps lstm_w_sb "
            "ln_step ln_var rstd_done ln_done xT_ps xT_sb ones_r_made "
            "gates_ready sig_ready tanhg_ready cell_step tanhc_ready h_ready head_ready mu_step "
            "head_read sigma_done pick_ps gauss_step gauss_exp gauss_ready norm_in norm_done gaussT_ps gaussT_sb self_attn_ps "
            "turned_w turned_w_sb folded folded_sb bits_set "
            "ctx_hi_done ctx_lo_done ctxT_ps ctxT_hi_done ctxT_lo_done q_ps q_staged q_hi_done q_lo_done "
            "max_ps max_read max_found diag_done spread_ps neg_done seeded scored prob_done prob_hi_done "
            "prob_lo_done prob_added weighted u_act u_dve sums_ps recip_done u_normed projected x2_done "
            "rows_ps rows_copied logit_ps onehot_step onehotT_ps onehotT_sb masked expT_ps expT_sb hid_ps hid_act "
            "y_ps y_added y_step y_var y_pow out_made"
        ).split()}

        def need(eng, name, value):
            if not isinstance(value, int) or value > 0:
                eng.wait_ge(s[name], value)

        def side_work(i, k):
            first = isinstance(i, int) and i == 0
            last = isinstance(i, int) and i == PAIRS - 1
            work = {}
            if not (last and k == 1):
                work.update({(0, 0): ("turn", 0), (0, 2): ("turn", 1), (1, 0): ("turn", 2)})
                free = [(1, 1), (1, 3), (2, 3)] + [(j, p) for j in range(3, 9) for p in (0, 1, 3)]
                work.update({place: ("max", n) for n, place in enumerate(free)})
                work.update({(9, 1): ("spread", 0), (9, 2): ("spread", 1)})
            if not (first and k == 0):
                work.update({(2, 0): ("sums", 0), (2, 1): ("sums", 1)})
            if k == 0 and not first:
                work[9, 3] = ("project", 0)
            if k == 0 and not last:
                work.update({place: ("query", u) for u, place in enumerate([(10, 1), (10, 3), (11, 1), (11, 3)])})
            return [(place, *work[place], SIDE + n % 2) for n, place in enumerate(sorted(work))]

        def bank_read(what, which, i, k):
            nb = 2 * i + k + 1
            return {"turn": ("ctxT_lo_done", MP * nb + which + 1), "max": ("max_read", RB * MP * nb + which + 1),
                    "spread": ("neg_done", 2 * nb + which + 1), "sums": ("recip_done", 2 * (nb - 2) + which + 1),
                    "project": ("x2_done", i), "query": ("q_staged", 4 * (i + 1) + which + 1)}[what]

        def side_banks(i, k):
            if isinstance(i, int) and i == 0 and k == 0:
                before = {SIDE + 1: ("neg_done", 1), SIDE: ("neg_done", 2)}
            else:
                pi, pk = (i, 0) if k else (i - 1, 1)
                before = {bank: bank_read(what, which, pi, pk) for _, what, which, bank in side_work(pi, pk)}
            rows = []
            for place, what, which, bank in side_work(i, k):
                rows.append((place, what, which, bank, before[bank]))
                before[bank] = bank_read(what, which, i, k)
            return rows

        def slot_work(i, k, j):
            return [(what, which, bank) for (slot, _), what, which, bank in side_work(i, k) if slot == j]

        def sequence(eng, period):
            for k in range(2):
                period(0, k)
            with eng.Fori(1, PAIRS - 1) as i:
                for k in range(2):
                    period(i, k)
            for k in range(2):
                period(PAIRS - 1, k)

        FOLD_BANK = (4, 0)
        SELF_BANK = (4, 5, 0, 1)

        block = stack.enter_context(nc.Block())

        @block.sync
        def _(sp):
            sp.dma_start(resid_k, x.rearrange("b s d -> (b s) d").rearrange("(k p) d -> p k d", p=TOK)).then_inc(s["x_in"], 16)
            sp.dma_start(w_in[0:4 * PE, :], W_ih).then_inc(s["lstm_w_in"], 16)
            sp.dma_start(w_hh_in[0:4 * PE, :], W_hh).then_inc(s["lstm_w_in"], 16)
            sp.dma_start(w_head_in[0:NB, :], W_mu).then_inc(s["lstm_w_in"], 16)
            sp.dma_start(w_head_in[NB:NB + 1, :], W_sig).then_inc(s["lstm_w_in"], 16)
            need(sp, "biased_cleared", 2)
            sp.dma_start(headT[PE:PE + 1, 0:NB], b_mu.rearrange("(a n) -> a n", a=1)).then_inc(s["bias_in"], 16)
            sp.dma_start(headT[PE:PE + 1, NB:NB + 1], b_sig.rearrange("(a n) -> a n", a=1)).then_inc(s["bias_in"], 16)
            sp.dma_start(whhT[PE:PE + 1, :], b_ih.rearrange("(a n) -> a n", a=1)).then_inc(s["bias_in"], 16)
            sp.dma_start(whhT[PE + 1:PE + 2, :], b_hh.rearrange("(a n) -> a n", a=1)).then_inc(s["bias_in"], 16)
            sp.dma_start(wq_raw, WQ).then_inc(s["attn_w_in"], 16)
            sp.dma_start(wk_raw, WK).then_inc(s["attn_w_in"], 16)
            sp.dma_start(wv_raw, WV).then_inc(s["attn_w_in"], 16)
            sp.dma_start(wo_raw[:], WO.rearrange("(c p) n -> p c n", p=128)).then_inc(s["attn_w_in"], 16)
            sp.dma_start(bO_row[:], bO.rearrange("(a n) -> a n", a=1)).then_inc(s["attn_w_in"], 16)
            sp.dma_start(ctx_in[0], ctx_1024[0].rearrange("(p c) d -> p c d", p=CR)).then_inc(s["ctx_in0"], 16)
            sp.dma_start(b1_sb[:], b1).then_inc(s["ffn_w_in"], 16)
            sp.dma_start(wo_sb[:], Wo.rearrange("(m p) n -> p m n", p=128)).then_inc(s["ffn_w_in"], 16)
            sp.dma_start(wr_sb[:], W_router).then_inc(s["ffn_w_in"], 16)
            for n, row in enumerate((bo, ln_gamma, ln_beta)):
                sp.dma_start(rows_sb[:, n, :], row.rearrange("(a n) -> a n", a=1)).then_inc(s["ffn_w_in"], 16)
            need(sp, "folded", H // 2)
            sp.dma_start(ctx_in[1], ctx_1024[1].rearrange("(p c) d -> p c d", p=CR)).then_inc(s["ctx_in1"], 16)
            sp.dma_start(w1_sb[:], W1.rearrange("e h i -> h e i")).then_inc(s["ffn_w_in"], 16)
            out_k = out.rearrange("b s d -> (b s) d").rearrange("(k p) d -> p k d", p=TOK)
            for g in range(GROUPS):
                need(sp, "out_made", g + 1)
                sp.dma_start(out_k[:, G4 * g:G4 * g + G4, :], o_sb[:, g % 2]).then_inc(s[f"out_stored{g % 2}"], 16)
            for n in range(2):
                sp.wait_ge(s[f"out_stored{n}"], 16 * (GROUPS // 2))

        @block.gpsimd
        def _(pool):
            g = nc.gpsimd
            g.memset(headT, 0.0).then_inc(s["biased_cleared"], 1)
            g.memset(whhT, 0.0).then_inc(s["biased_cleared"], 1)
            g.memset(lstm_h, 1.0).then_inc(s["zeros_made"], 1)
            g.memset(cell, 0.0).then_inc(s["zeros_made"], 1)
            g.memset(mu[:, 0:1], 0.0).then_inc(s["zeros_made"], 1)
            pool.wait_ge(s["zeros_made"], 1)
            g.memset(lstm_h[0:PE, U8 - 1, :], 0.0).then_inc(s["zeros_made"], 1)
            g.memset(ident[:], 0.0).then_inc(s["identity_made"], 1)
            pool.wait_ge(s["identity_made"], 1)
            g.affine_select(out=ident[:], in_=ident[:], compare_op=ALU.not_equal, fill=1.0, base=0,
                            pattern=[[-1, 128]], channel_multiplier=1).then_inc(s["identity_made"], 1)
            g.memset(ones[:], 1.0).then_inc(s["ones_made"], 1)
            g.memset(minus_half[:], -0.5).then_inc(s["minus_made"], 1)

            def power(count):
                pool.wait_ge(s["ln_var"], count)
                g.tensor_tensor(rstd[:], veps[:], minus_half[:], ALU.pow).then_inc(s["rstd_done"], 1)

            pool.wait_ge(s["minus_made"], 1)
            power(1)
            g.iota(jp1_int, [[1, S]], base=1, channel_multiplier=0).then_inc(s["indices_made"], 1)
            g.iota(idx_int.rearrange("p (b i) -> p b i", b=2), [[0, 2], [1, S]], base=0, channel_multiplier=0).then_inc(s["indices_made"], 1)
            g.iota(p_int, [[0, 1]], base=1, channel_multiplier=1).then_inc(s["indices_made"], 1)
            g.memset(pos[:, 1:2], -float(S)).then_inc(s["rel_made"], 1)
            pool.wait_ge(s["rel_made"], 1)
            g.affine_select(out=pos[:, 1:2], in_=pos[:, 1:2], compare_op=ALU.is_ge, fill=0.0, base=-S,
                            pattern=[[0, 1]], channel_multiplier=1).then_inc(s["rel_made"], 1)
            causal_v = causal.rearrange("p (b i) -> p b i", b=2)
            g.memset(causal, 1.0).then_inc(s["causal_made"], 1)
            pool.wait_ge(s["causal_made"], 1)
            g.affine_select(out=causal_v, in_=causal_v, compare_op=ALU.is_ge, fill=0.0, base=0,
                            pattern=[[-S, 2], [-1, S]], channel_multiplier=1).then_inc(s["causal_made"], 1)
            pool.wait_ge(s["causal_made"], 2)
            g.affine_select(out=causal_v, in_=causal_v, compare_op=ALU.is_ge, fill=0.0, base=S - 1,
                            pattern=[[S, 2], [0, S]], channel_multiplier=-1).then_inc(s["causal_made"], 1)
            g.memset(pick_b, 1.0).then_inc(s["picks_made"], 1)
            g.memset(pick_k, 0.0).then_inc(s["picks_made"], 1)
            pool.wait_ge(s["picks_made"], 2)
            g.affine_select(out=pick_b, in_=pick_b, compare_op=ALU.is_ge, fill=0.0, base=0,
                            pattern=[[-PAIRS, 2], [0, S]], channel_multiplier=1).then_inc(s["picks_made"], 1)
            g.affine_select(out=pick_k, in_=pick_k, compare_op=ALU.not_equal, fill=1.0, base=0,
                            pattern=[[-1, PAIRS]], channel_multiplier=1).then_inc(s["picks_made"], 1)
            pool.wait_ge(s["picks_made"], 4)
            g.affine_select(out=pick_b, in_=pick_b, compare_op=ALU.is_ge, fill=0.0, base=PAIRS - 1,
                            pattern=[[PAIRS, 2], [0, S]], channel_multiplier=-1).then_inc(s["picks_made"], 1)
            g.affine_select(out=pick_k, in_=pick_k, compare_op=ALU.not_equal, fill=1.0, base=-PAIRS,
                            pattern=[[-1, PAIRS]], channel_multiplier=1).then_inc(s["picks_made"], 1)

            def low_half(i, k):
                need(pool, "ctx_hi_done", 2 * i + k + 1)
                g.tensor_tensor(ctx_lo[k][:], ctx_in[k], ctx_hi[k][:].bitcast(F32), ALU.subtract).then_inc(s["ctx_lo_done"], 1)

            low_half(0, 0)
            pool.wait_ge(s["norm_in"], 1)
            g.tensor_tensor(wsum, wsum, minus_half[:], ALU.pow).then_inc(s["norm_done"], 1)
            power(2)

            def period(i, k):
                b = 2 * i + k
                for j in range(1, CH):
                    need(pool, "prob_done", CH * b + j + 1)
                    if j == 1:
                        need(pool, "sums_ps", 2 * (b - 1))
                        g.tensor_tensor(prob_sum[k], probs[0], probs[1], ALU.add).then_inc(s["prob_added"], 1)
                    else:
                        need(pool, "prob_added", (CH - 1) * b + j - 1)
                        g.tensor_tensor(prob_sum[k], prob_sum[k], probs[j % 3], ALU.add).then_inc(s["prob_added"], 1)
                    if j == 4 and not (isinstance(i, int) and i == PAIRS - 1 and k == 1):
                        low_half(i + k, 1 - k)

            sequence(pool, period)

            power(3)
            for n in range(GROUPS):
                pool.wait_ge(s["y_var"], n + 1)
                g.tensor_tensor(rstd[:, G4 * n:G4 * n + G4], veps[:, G4 * n:G4 * n + G4], minus_half[:, 0:G4],
                                ALU.pow).then_inc(s["y_pow"], 1)

        @block.tensor
        def _(pe):
            mm, tr = nc.tensor.matmul, nc.tensor.transpose

            pe.wait_ge(s["identity_made"], 2)
            pe.wait_ge(s["lstm_w_in"], 64)
            tr(ps[:, 3, 0:4 * PE], w_in[0:4 * PE, :], ident[0:4 * PE, 0:4 * PE])
            tr(ps[0:PE, 3, 128:128 + 4 * PE], w_hh_in[0:4 * PE, :], ident[0:4 * PE, 0:4 * PE])
            tr(ps[0:PE, 3, 256:256 + NB + 1], w_head_in[0:NB + 1, :], ident[0:NB + 1, 0:NB + 1]).then_inc(s["lstm_w_ps"], 1)

            def turn_tokens(first_bank, count):
                pe.wait_ge(s["ln_done"], count)
                for q in range(GROUPS):
                    for t in range(G4):
                        m = tr(ps[:, first_bank + q, t * TOK:(t + 1) * TOK], xnorm[:, G4 * q + t, :], ident[0:TOK, 0:TOK])
                    m.then_inc(s["xT_ps"], 1)

            turn_tokens(4, 1)

            GATE = (0, 1, 3, 2)
            xT_steps = xT[:].rearrange("d k (b t) -> d t b k", b=2)
            pe.wait_ge(s["xT_sb"], 4)
            pe.wait_ge(s["lstm_w_sb"], 3)
            pe.wait_ge(s["bias_in"], 64)
            pe.wait_ge(s["zeros_made"], 4)

            def input_part(bank, gate, t0):
                mm(ps[0:PE, bank, gate * 128:(gate + 1) * 128], wihT[:, GATE[gate] * PE:(GATE[gate] + 1) * PE],
                   xT_steps[:, bass.ds(t0, G4), :, :], start=(gate == 0), stop=False, skip_group_check=True)

            def head(u):
                return mm(ps[0:B, 2, u * (NB + 1):(u + 1) * (NB + 1)], lstm_h[:, u, :], headT, start=True, stop=True)

            def lstm_steps(it, last):
                for u in range(U8):
                    bank, v = u // G4, u % G4
                    need(pe, "h_ready", U8 * it + u)
                    for gate in range(4):
                        m = mm(ps[0:PE, bank, gate * 128 + v * B:gate * 128 + (v + 1) * B],
                               whhT[:, GATE[gate] * PE:(GATE[gate] + 1) * PE], lstm_h[:, (u - 1) % U8, :],
                               start=False, stop=True, skip_group_check=True)
                    m.then_inc(s["gates_ready"], 1)
                    if u == 1:
                        need(pe, "head_read", it)
                    if u:
                        head(u - 1)
                    if bank == 0:
                        input_part(1, v, U8 * it + G4)
                    elif not last:
                        input_part(0, v, U8 * it + U8)
                need(pe, "h_ready", U8 * it + U8)
                head(U8 - 1).then_inc(s["head_ready"], 1)

            for gate in range(4):
                input_part(0, gate, 0)
            lstm_steps(0, False)
            with pe.Fori(1, S // U8 - 1) as it:
                lstm_steps(it, False)
            lstm_steps(S // U8 - 1, True)

            pe.wait_ge(s["gauss_ready"], 1)
            pe.wait_ge(s["picks_made"], 6)
            mm(ps[0:TOK, 3, 0:PAIRS], mu_l.rearrange("p b j -> p (b j)"), pick_k, start=True, stop=True)
            mm(ps[0:TOK, 3, PAIRS:2 * PAIRS], inv_l.rearrange("p b j -> p (b j)"), pick_k, start=True, stop=True).then_inc(s["pick_ps"], 1)

            def turn_weights(f):
                need(pe, "turned_w_sb", f - 1)
                for n, w in enumerate((wq_raw, wk_raw, wv_raw)):
                    m = tr(ps[:, SIDE + f % 2, n * D:(n + 1) * D], w[:, f * D:(f + 1) * D], ident[:])
                m.then_inc(s["turned_w"], 1)

            pe.wait_ge(s["attn_w_in"], 80)
            turn_weights(0)
            for f in range(H // 2):
                if f + 1 < H // 2:
                    turn_weights(f + 1)
                need(pe, "turned_w_sb", f + 1)
                need(pe, "folded_sb", 2 * (f - 1))
                for n in range(2):
                    part = slice(DK * n, DK * n + DK)
                    mm(ps[:, FOLD_BANK[f % 2] + n, 0:D], wT_sb[part, f % 2, 0, :], wT_sb[part, f % 2, 1, :], start=True, stop=True)
                    m = mm(ps[:, FOLD_BANK[f % 2] + n, D:2 * D], wT_sb[part, f % 2, 2, :], wo_raw[part, f, :], start=True, stop=True)
                m.then_inc(s["folded"], 1)

            def side(what, which, bank, i, k):
                nk, nb = 1 - k, 2 * i + k + 1
                if what == "turn":
                    if which == 0:
                        need(pe, f"ctx_in{nk}", 16 * (i + k + 1))
                    for c in range(TG):
                        m = tr(ps[:, bank, c * CR:(c + 1) * CR], ctx_in[nk][:, which * TG + c, :], ident[0:CR, 0:CR])
                    m.then_inc(s["ctxT_ps"], 1)
                elif what == "max":
                    block_, part = which // MP, which % MP
                    if which == 0:
                        need(pe, "q_hi_done", nb + 1)
                    if which < MP:
                        need(pe, "ctxT_hi_done", MP * nb + part + 1)
                    mm(ps[:, bank, 0:MC], q_hi[nk][:, block_ * 128:(block_ + 1) * 128], ctxT_hi[nk][:, part * MC:(part + 1) * MC],
                       start=True, stop=True).then_inc(s["max_ps"], 1)
                elif what == "spread":
                    if which == 0:
                        need(pe, "diag_done", nb + 1)
                    mm(ps[:, bank, 0:HALF], ones_r[:], max_diag[:, which * HALF:(which + 1) * HALF],
                       start=True, stop=True).then_inc(s["spread_ps"], 1)
                elif what == "sums":
                    if which == 0:
                        need(pe, "prob_added", (CH - 1) * (nb - 1))
                    mm(ps[:, bank, 0:HALF], ones[0:CR, :], prob_sum[nk][:, which, :], start=True, stop=True).then_inc(s["sums_ps"], 1)
                elif what == "project":
                    need(pe, "u_normed", 4 * i)
                    mm(ps[0:TOK, bank, 0:D], ones[0:1, 0:TOK], bO_row[:], start=True, stop=False)
                    for h in range(H):
                        m = mm(ps[0:TOK, bank, 0:D], u_norm[:, h].rearrange("p b q -> p (b q)"), vo_w[:, h, :], start=False, stop=(h == H - 1))
                    m.then_inc(s["projected"], 1)
                elif what == "query":
                    for n in range(4):
                        m = mm(ps[:, bank, n * TOK:(n + 1) * TOK], qk_w[:, 4 * which + n, :],
                               xT[:, bass.ds(i + 1, 1), :].rearrange("p k t -> p (k t)"), start=True, stop=True)
                    m.then_inc(s["q_ps"], 1)

            need(pe, "folded_sb", 2 * (H // 2))
            for q in range(GROUPS):
                pe.wait_ge(s["gauss_ready"], 2)
                for t in range(G4):
                    m = tr(ps[0:TOK, q, t * TOK:(t + 1) * TOK], gauss_w[:, G4 * q + t, :], ident[0:TOK, 0:TOK])
                m.then_inc(s["gaussT_ps"], 1)
            need(pe, "folded_sb", 2 * (H // 2))
            for q in range(GROUPS):
                pe.wait_ge(s["gaussT_sb"], max(q + 1, SELF_BANK[q] + 1 if SELF_BANK[q] < 4 else 0))
                for t in range(G4):
                    m = mm(ps[0:TOK, SELF_BANK[q], t * D:(t + 1) * D], gauss_wT[:, G4 * q + t, :], xnorm[:, G4 * q + t, :], start=True, stop=True)
                m.then_inc(s["self_attn_ps"], 1)

            need(pe, "turned_w_sb", H // 2)
            for n in range(2):
                side("turn", n, SIDE + n, -1, 1)
            turn_tokens(0, 2)
            need(pe, "ctxT_lo_done", 1)
            side("turn", 2, SIDE, -1, 1)
            pe.wait_ge(s["xT_sb"], 8)
            for bank in range(4):
                m = mm(ps[0:CR, bank, :], ones[:, 0:CR], xT[:].rearrange("d k t -> d (k t)")[:, 0:512], start=True, stop=True)
            m.then_inc(s["bits_set"], 1)
            need(pe, "folded_sb", 2 * (H // 2))
            for u in range(4):
                need(pe, "ctxT_lo_done", MP)
                if u > 1:
                    need(pe, "q_staged", u - 1)
                side("query", u, SIDE + u % 2, -1, 0)
            for n in range(RB * MP):
                if n < 2:
                    need(pe, "q_staged", 4)
                else:
                    need(pe, "max_read", n - 1)
                side("max", n, SIDE + n % 2, -1, 1)
            for n in range(2):
                need(pe, "max_read", RB * MP)
                side("spread", n, SIDE + (n + 1) % 2, -1, 1)

            def scores(b, k, j, half):
                if half == 0:
                    if j == 0:
                        need(pe, "q_lo_done", b + 1)
                        need(pe, "ctxT_lo_done", MP * (b + 1))
                    need(pe, "seeded", CH * b + j + 1)
                rows, cols = slice(j * CR, (j + 1) * CR), slice(half * HALF, (half + 1) * HALF)
                for cx, q in ((ctxT_hi, q_hi), (ctxT_hi, q_lo), (ctxT_lo, q_hi)):
                    m = mm(score_ps[j % 2][:, half, :], cx[k][:, rows], q[k][:, cols], start=False, stop=True, skip_group_check=True)
                if half == 1:
                    m.then_inc(s["scored"], 1)

            def weigh(b, k, j, half):
                if half == 0:
                    if j == 0:
                        need(pe, "u_act", b)
                        need(pe, "u_dve", b)
                        need(pe, "ctx_lo_done", b + 1)
                    need(pe, "prob_lo_done", CH * b + j + 1)
                for n, (cx, p) in enumerate(((ctx_hi, p_hi), (ctx_hi, p_lo), (ctx_lo, p_hi))):
                    m = mm(usum_ps[:, half, :], cx[k][:, j, :], p[j % 3][:, half, :], start=(j == 0 and n == 0), stop=(j == CH - 1 and n == 2))
                if half == 1:
                    m.then_inc(s["weighted"], 1)

            for half in range(2):
                scores(0, 0, 0, half)

            def period(i, k):
                b = 2 * i + k
                last = isinstance(i, int) and i == PAIRS - 1 and k == 1
                work = {(j, p): row for (j, p), *row in side_banks(i, k)}

                def beside(j, p):
                    if (j, p) in work:
                        what, which, bank, (name, value) = work[j, p]
                        need(pe, name, value)
                        side(what, which, bank, i, k)

                for j in range(CH):
                    ahead = (b, k, j + 1) if j + 1 < CH else (b + 1, 1 - k, 0)
                    for half in range(2):
                        if j + 1 < CH or not last:
                            scores(*ahead, half)
                        beside(j, half)
                    for half in range(2):
                        weigh(b, k, j, half)
                        beside(j, 2 + half)

            sequence(pe, period)

            for n in range(2):
                need(pe, "recip_done", 2 * (B - 1))
                side("sums", n, SIDE + n, PAIRS, 0)
            need(pe, "recip_done", 2 * B)
            side("project", 0, SIDE, PAIRS, 0)

            pe.wait_ge(s["ffn_w_in"], 16 * 7)
            mm(ps[0:TOK, 5, 0:3 * D], ones[0:1, 0:TOK], rows_sb[:].rearrange("p n d -> p (n d)"), start=True, stop=True).then_inc(s["rows_ps"], 1)
            turn_tokens(0, 3)
            for t in range(PAIRS):
                if t % G4 == 0:
                    pe.wait_ge(s["xT_sb"], 8 + t // G4 + 1)
                m = mm(ps[0:TOK, 4, t * E:(t + 1) * E], xT[:, t, :], wr_sb[:], start=True, stop=True)
            m.then_inc(s["logit_ps"], 1)
            pe.wait_ge(s["onehot_step"], ONEHOT_STEPS)
            for q in range(GROUPS):
                for t in range(G4):
                    m = tr(ps[0:E, q, t * TOK:(t + 1) * TOK], onehot[:, (G4 * q + t) * E:(G4 * q + t + 1) * E], ident[0:TOK, 0:TOK])
                m.then_inc(s["onehotT_ps"], 1)

            def turn_experts(n):
                for t in range(G4):
                    tile = G4 * n + t
                    need(pe, "masked", tile + 1)
                    need(pe, "expT_sb", tile - 1)
                    for e in range(E):
                        m = tr(ps[:, SIDE + t % 2, e * TOK:(e + 1) * TOK], experts_in[:, t % 2, e, :], ident[0:TOK, 0:TOK])
                    m.then_inc(s["expT_ps"], 1)

            turn_experts(0)
            pe.wait_ge(s["onehotT_sb"], GROUPS)
            for n in range(GROUPS):
                if n + 1 < GROUPS:
                    turn_experts(n + 1)
                need(pe, "expT_sb", G4 * (n + 1))
                for m_ in range(MB):
                    need(pe, "hid_act", MB * (n - 1) + m_ + 1)
                    o_ps, cols = ps[:, m_, 0:GT], slice(m_ * 128, (m_ + 1) * 128)
                    mm(o_ps, b1_sb[:, cols], onehotT[:, n * GT:(n + 1) * GT], start=True, stop=False)
                    for e in range(E):
                        m = mm(o_ps, w1_sb[:, e, cols], expertsT[n % 2][:, e].rearrange("p k t -> p (k t)"), start=False, stop=(e == E - 1))
                    m.then_inc(s["hid_ps"], 1)
                need(pe, "y_added", n - 1)
                for t in range(G4):
                    for m_ in range(MB):
                        if t == 0:
                            need(pe, "hid_act", MB * n + m_ + 1)
                        m = mm(ps[0:TOK, 4 + n % 2, t * D:(t + 1) * D], inter[n % 2][:, m_, t * TOK:(t + 1) * TOK], wo_sb[:, m_, :],
                               start=(m_ == 0), stop=(m_ == MB - 1))
                m.then_inc(s["y_ps"], 1)

        @block.scalar
        def _(act):
            a = nc.scalar.activation
            ctx_pairs = ctx_1024.rearrange("(i n) (p c) d -> n p i (c d)", n=2, p=CR)

            def load_context(i, k):
                need(act, "ctx_lo_done", 2 * i + k + 1)
                need(act, "ctxT_ps", MP * (2 * i + k + 1))
                act.dma_start(ctx_raw[k][0:CR, :], ctx_pairs[k, :, bass.ds(i + 1, 1), :].rearrange("p i c -> p (i c)")).then_inc(
                    s[f"ctx_in{k}"], 16)

            def copy_tokens(first_bank, count):
                for q in range(GROUPS):
                    need(act, "xT_ps", 4 * (count - 1) + q + 1)
                    a(xT[:, G4 * q:G4 * q + G4, :].rearrange("d k t -> d (k t)"), ps[:, first_bank + q, 0:GT], ACT.Copy).then_inc(s["xT_sb"], 1)

            act.wait_ge(s["lstm_w_ps"], 1)
            need(act, "biased_cleared", 2)
            a(wihT, ps[:, 3, 0:4 * PE], ACT.Copy).then_inc(s["lstm_w_sb"], 1)
            a(whhT[0:PE, :], ps[0:PE, 3, 128:128 + 4 * PE], ACT.Copy).then_inc(s["lstm_w_sb"], 1)
            a(headT[0:PE, :], ps[0:PE, 3, 256:256 + NB + 1], ACT.Copy).then_inc(s["lstm_w_sb"], 1)
            act.wait_ge(s["ones_made"], 1)
            a(ones_r[:], ones[:], ACT.Copy).then_inc(s["ones_r_made"], 1)
            copy_tokens(4, 1)

            def lstm_steps(it):
                for u in range(U8):
                    t = U8 * it + u
                    gates = ps[0:PE, u // G4, :].rearrange("p (g t b) -> p g t b", g=4, t=G4)[:, :, u % G4, :]
                    need(act, "gates_ready", t + 1)
                    a(gate_act[:, 0:3, :], gates[:, 0:3, :], ACT.Sigmoid).then_inc(s["sig_ready"], 1)
                    a(gate_act[:, 3, :], gates[:, 3, :], ACT.Tanh).then_inc(s["tanhg_ready"], 1)
                    need(act, "cell_step", 3 * t + 3)
                    a(cell_t, cell, ACT.Tanh).then_inc(s["tanhc_ready"], 1)

            with act.Fori(0, S // U8) as it:
                lstm_steps(it)

            need(act, "head_read", S // U8)
            a(sig, sig, ACT.Sigmoid).then_inc(s["sigma_done"], 1)

            def fold_out(f):
                need(act, "folded", f + 1)
                a(qk_w[:, 2 * f:2 * f + 2, :], folded_ps(f, 0), ACT.Copy).then_inc(s["folded_sb"], 1)
                a(vo_w[:, 2 * f:2 * f + 2, :], folded_ps(f, 1), ACT.Copy).then_inc(s["folded_sb"], 1)

            def folded_ps(f, side_):
                return ps[:, FOLD_BANK[f % 2]:FOLD_BANK[f % 2] + 2, side_ * D:(side_ + 1) * D]

            for f in range(H // 2):
                need(act, "turned_w", f + 1)
                need(act, "folded", f - 1)
                a(wT_sb[:, f % 2].rearrange("p n d -> p (n d)"), ps[:, SIDE + f % 2, 0:3 * D], ACT.Copy).then_inc(s["turned_w_sb"], 1)
                if f:
                    fold_out(f - 1)
            fold_out(H // 2 - 1)

            act.wait_ge(s["gauss_exp"], 1)
            a(gauss_w, gauss_d, ACT.Exp, scale=-1.0).then_inc(s["gauss_exp"], 1)

            def turned_hi(i, k, which, bank):
                nk, nb = 1 - k, 2 * i + k + 1
                need(act, "ctxT_ps", MP * nb + which + 1)
                a(ctxT_hi[nk][:, which * MC:(which + 1) * MC], ps[:, bank, 0:MC], ACT.Copy).then_inc(s["ctxT_hi_done"], 1)

            def context_hi(i, k):
                nk, nb = 1 - k, 2 * i + k + 1
                need(act, f"ctx_in{nk}", 16 * (i + k + 1))
                need(act, "weighted", CH * (nb - 1))
                a(ctx_hi[nk][:], ctx_in[nk], ACT.Copy).then_inc(s["ctx_hi_done"], 1)

            def stage_query(i, which, bank):
                need(act, "q_ps", 4 * (i + 1) + which + 1)
                need(act, "q_lo_done", 2 * (i + 1))
                a(q_stage[:, :, 4 * which:4 * which + 4, :], ps[:, bank, 0:4 * TOK].rearrange("p (h b q) -> p b h q", h=4, b=2),
                  ACT.Copy).then_inc(s["q_staged"], 1)

            def query_hi(i, k):
                nk, nb = 1 - k, 2 * i + k + 1
                need(act, "q_staged", 4 * (i + k + 1))
                a(q_hi[nk][:].rearrange("p (h q) -> p h q", h=H), q_stage[:, nk], ACT.Copy).then_inc(s["q_hi_done"], 1)

            def negate_max(i, k, which, bank):
                nk, nb = 1 - k, 2 * i + k + 1
                need(act, "spread_ps", 2 * nb + which + 1)
                need(act, "seeded", CH * (nb - 1))
                a(neg_max[nk][:, which, :], ps[:, bank, 0:HALF], ACT.Copy, scale=-1.0).then_inc(s["neg_done"], 1)

            def seed(b, k, j):
                need(act, "prob_hi_done", CH * b + j - 1)
                need(act, "neg_done", 2 * (b + 1))
                a(score_ps[j % 2], neg_max[k][0:CR], ACT.Copy).then_inc(s["seeded"], 1)

            for q in range(GROUPS):
                need(act, "gaussT_ps", q + 1)
                a(gauss_wT[:, G4 * q:G4 * q + G4, :].rearrange("p k t -> p (k t)"), ps[0:TOK, q, 0:GT], ACT.Copy).then_inc(s["gaussT_sb"], 1)
            context_hi(-1, 1)
            turned_hi(-1, 1, 0, SIDE)
            turned_hi(-1, 1, 1, SIDE + 1)
            copy_tokens(0, 2)
            turned_hi(-1, 1, 2, SIDE)
            for u in range(4):
                stage_query(-1, u, SIDE + u % 2)
            query_hi(-1, 1)
            for n in range(2):
                negate_max(-1, 1, n, SIDE + (n + 1) % 2)
            act.wait_ge(s["bits_set"], 1)
            seed(0, 0, 0)
            seed(0, 0, 1)

            def take_u(b):
                need(act, "weighted", CH * (b + 1))
                need(act, "u_normed", 2 * b)
                a(u_raw[:, 0, :], usum_ps[:, 0, :], ACT.Copy).then_inc(s["u_act"], 1)

            def period(i, k):
                b = 2 * i + k
                first = isinstance(i, int) and i == 0 and k == 0
                last = isinstance(i, int) and i == PAIRS - 1 and k == 1
                for j in range(CH):
                    c = CH * b + j
                    need(act, "scored", c + 1)
                    need(act, "prob_lo_done", c - 2)
                    need(act, "prob_added", (CH - 1) * b + (max(j - 3, 1) if j >= 3 else j - 2))
                    a(probs[j % 3], score_ps[j % 2], ACT.Exp, scale=SCALE).then_inc(s["prob_done"], 1)
                    need(act, "weighted", c - 2)
                    a(p_hi[j % 3][:], score_ps[j % 2], ACT.Exp, scale=SCALE).then_inc(s["prob_hi_done"], 1)
                    if j == 0 and not first:
                        take_u(b - 1)
                    if j + 2 < CH:
                        seed(b, k, j + 2)
                    elif not last:
                        need(act, "prob_hi_done", c + 1)
                        seed(b + 1, 1 - k, j + 2 - CH)
                    if j == 0 and not last:
                        query_hi(i, k)
                    if j == 2 and not (isinstance(i, int) and i == PAIRS - 1):
                        load_context(i, k)
                    if j == 3 and not last:
                        context_hi(i, k)
                    for what, which, bank in slot_work(i, k, j):
                        if what == "turn":
                            turned_hi(i, k, which, bank)
                        elif what == "spread":
                            negate_max(i, k, which, bank)
                        elif what == "query":
                            stage_query(i, which, bank)

            sequence(act, period)
            take_u(B - 1)

            copy_tokens(0, 3)
            for q in range(GROUPS):
                need(act, "onehotT_ps", q + 1)
                a(onehotT[:, q * GT:(q + 1) * GT], ps[0:E, q, 0:GT], ACT.Copy).then_inc(s["onehotT_sb"], 1)

            def copy_experts(n):
                need(act, "hid_ps", MB * (n - 1))
                for t in range(G4):
                    need(act, "expT_ps", G4 * n + t + 1)
                    a(expertsT[n % 2][:, :, t, :], ps[:, SIDE + t % 2, 0:E * TOK].rearrange("p (e t) -> p e t", e=E),
                      ACT.Copy).then_inc(s["expT_sb"], 1)

            copy_experts(0)
            for n in range(GROUPS):
                if n + 1 < GROUPS:
                    copy_experts(n + 1)
                need(act, "y_ps", n - 1)
                for m_ in range(MB):
                    need(act, "hid_ps", MB * n + m_ + 1)
                    a(inter[n % 2][:, m_, :], ps[:, m_, 0:GT], ACT.Gelu).then_inc(s["hid_act"], 1)

        @block.vector
        def _(dve):
            v = nc.vector

            def layer_norm(count):
                need(dve, "ln_done", count - 1)
                for k in range(PAIRS):
                    m = v.bn_stats(stats[:, k, :], resid_k[:, k, :])
                m.then_inc(s["ln_step"], 1)
                dve.wait_ge(s["ln_step"], 2 * count - 1)
                for k in range(PAIRS):
                    m = v.bn_aggr(meanvar[:, k, :], stats[:, k, :])
                m.then_inc(s["ln_step"], 1)
                dve.wait_ge(s["ln_step"], 2 * count)
                v.tensor_scalar(veps[:], meanvar[:, :, 1], 1e-5, None, ALU.add).then_inc(s["ln_var"], 1)
                dve.wait_ge(s["rstd_done"], count)
                for k in range(PAIRS):
                    m = v.tensor_scalar(xnorm[:, k, :], resid_k[:, k, :], meanvar[:, k, 0:1], rstd[:, k:k + 1], ALU.subtract, ALU.mult)
                m.then_inc(s["ln_done"], 1)

            dve.wait_ge(s["x_in"], 16)
            layer_norm(1)

            gauss_count = [0]

            def then(m):
                gauss_count[0] += 1
                m.then_inc(s["gauss_step"], 1)
                dve.wait_ge(s["gauss_step"], gauss_count[0])

            dve.wait_ge(s["indices_made"], 3)
            v.tensor_copy(jp1, jp1_int)
            v.tensor_copy(i_idx, idx_int)
            then(v.tensor_copy(pos[:, 0:1], p_int))
            dve.wait_ge(s["rel_made"], 2)
            then(v.tensor_tensor(pos[:, 2:3], pos[:, 0:1], pos[:, 1:2], ALU.add))
            then(v.reciprocal(pos[:, 3:4], pos[:, 2:3]))
            then(v.tensor_scalar(rel, i_idx, pos[:, 3:4], None, ALU.mult))

            dve.wait_ge(s["zeros_made"], 4)

            def lstm_steps(it):
                for u in range(U8):
                    t = U8 * it + u
                    need(dve, "sig_ready", t + 1)
                    need(dve, "cell_step", 3 * t)
                    v.tensor_tensor(cell_f, gate_act[:, 1, :], cell, ALU.mult).then_inc(s["cell_step"], 1)
                    need(dve, "tanhg_ready", t + 1)
                    v.tensor_tensor(cell_i, gate_act[:, 0, :], gate_act[:, 3, :], ALU.mult).then_inc(s["cell_step"], 1)
                    need(dve, "cell_step", 3 * t + 2)
                    v.tensor_tensor(cell, cell_f, cell_i, ALU.add).then_inc(s["cell_step"], 1)
                    need(dve, "tanhc_ready", t + 1)
                    v.tensor_tensor(lstm_h[0:PE, u, :], gate_act[:, 2, :], cell_t, ALU.mult).then_inc(s["h_ready"], 1)
                heads = ps[0:B, 2, 0:U8 * (NB + 1)].rearrange("p (t n) -> p t n", n=NB + 1)
                steps = U8 + 3
                need(dve, "head_ready", it + 1)
                need(dve, "mu_step", steps * it)
                v.tensor_scalar(mu_w, heads[:, :, 0:NB], 0.0, None, ALU.max).then_inc(s["mu_step"], 1)
                v.tensor_copy(sig[:, bass.ds(U8 * it, U8)], heads[:, :, NB]).then_inc(s["head_read"], 1)
                need(dve, "mu_step", steps * it + 1)
                v.scalar_tensor_tensor(mu_t, mu_w[:, :, 2], 1.0 / S, jp1[:, bass.ds(U8 * it, U8)], ALU.mult, ALU.mult).then_inc(s["mu_step"], 1)
                need(dve, "mu_step", steps * it + 2)
                v.scalar_tensor_tensor(mu_b, mu_w[:, :, 1], 1.0 / S, mu_t, ALU.mult, ALU.add).then_inc(s["mu_step"], 1)
                for u in range(U8):
                    need(dve, "mu_step", steps * it + 3 + u)
                    v.scalar_tensor_tensor(mu[:, bass.ds(U8 * it + u + 1, 1)], mu_w[:, u, 0:1], mu[:, bass.ds(U8 * it + u, 1)],
                                           mu_b[:, u:u + 1], ALU.mult, ALU.add).then_inc(s["mu_step"], 1)

            lstm_steps(0)
            with dve.Fori(1, S // U8) as it:
                lstm_steps(it)
            need(dve, "mu_step", (U8 + 3) * (S // U8))

            def over_k(ap):
                return ap[:, None, :].to_broadcast((TOK, PAIRS, TOK))

            def over_i(ap):
                return ap[:, :, None].to_broadcast((TOK, PAIRS, TOK))

            def over_b(ap):
                return ap[:, None, :].to_broadcast((B, 2, S))

            dve.wait_ge(s["sigma_done"], 1)
            dve.wait_ge(s["picks_made"], 6)
            then(v.scalar_tensor_tensor(sig2, sig, 2.0, sig, ALU.mult, ALU.mult))
            then(v.reciprocal(inv2s, sig2))
            v.tensor_tensor(mu_l, over_b(mu[:, 1:S + 1]), pick_b, ALU.mult)
            v.tensor_tensor(inv_l, over_b(inv2s), pick_b, ALU.mult).then_inc(s["gauss_ready"], 1)
            dve.wait_ge(s["pick_ps"], 1)
            then(v.tensor_copy(mu_tok.rearrange("p a k -> p (a k)"), ps[0:TOK, 3, 0:2 * PAIRS]))
            then(v.tensor_tensor(gauss_d, over_k(rel), over_i(mu_tok[:, 0, :]), ALU.subtract))
            then(v.tensor_tensor(gauss_w, gauss_d, gauss_d, ALU.mult))
            v.tensor_tensor(gauss_d, gauss_w, over_i(mu_tok[:, 1, :]), ALU.mult).then_inc(s["gauss_exp"], 1)
            dve.wait_ge(s["gauss_exp"], 2)
            dve.wait_ge(s["causal_made"], 3)
            v.tensor_tensor(gauss_w, gauss_w, over_k(causal), ALU.mult).then_inc(s["gauss_ready"], 1)
            dve.wait_ge(s["gauss_ready"], 2)
            then(v.tensor_tensor(gauss_d, gauss_w, gauss_w, ALU.mult))
            then(v.tensor_reduce(wsum, gauss_d, AX.X, ALU.add))
            v.tensor_scalar(wsum, wsum, 1e-24, None, ALU.max).then_inc(s["norm_in"], 1)
            dve.wait_ge(s["norm_done"], 1)
            for t in range(PAIRS):
                if t % G4 == 0:
                    dve.wait_ge(s["self_attn_ps"], t // G4 + 1)
                q = t % G4
                m = v.scalar_tensor_tensor(resid_k[:, t, :], ps[0:TOK, SELF_BANK[t // G4], q * D:(q + 1) * D], wsum[:, t:t + 1],
                                           resid_k[:, t, :], ALU.mult, ALU.add)
            then(m)
            layer_norm(2)

            def turned_lo(i, k, which, bank):
                nk, nb = 1 - k, 2 * i + k + 1
                part = slice(which * MC, (which + 1) * MC)
                need(dve, "ctxT_hi_done", MP * nb + which + 1)
                v.tensor_tensor(ctxT_lo[nk][:, part], ps[:, bank, 0:MC], ctxT_hi[nk][:, part].bitcast(F32), ALU.subtract).then_inc(s["ctxT_lo_done"], 1)

            def query_lo(i, k):
                nk, nb = 1 - k, 2 * i + k + 1
                need(dve, "q_hi_done", nb + 1)
                v.tensor_tensor(q_lo[nk][:].rearrange("p (h q) -> p h q", h=H), q_stage[:, nk],
                                q_hi[nk][:].bitcast(F32).rearrange("p (h q) -> p h q", h=H), ALU.subtract).then_inc(s["q_lo_done"], 1)

            def read_max(i, k, which, bank):
                nb = 2 * i + k + 1
                need(dve, "max_ps", RB * MP * nb + which + 1)
                if which == 0:
                    need(dve, "max_found", nb)
                v.tensor_reduce(max_parts[:, which:which + 1], ps[:, bank, 0:MC], AX.X, ALU.max).then_inc(s["max_read"], 1)
                if which == RB * MP - 1:
                    need(dve, "max_read", RB * MP * (nb + 1))
                    need(dve, "diag_done", nb)
                    v.tensor_reduce(max_all[:], max_parts[:].rearrange("p (r m) -> p r m", m=MP), AX.X, ALU.max).then_inc(s["max_found"], 1)
                    need(dve, "max_found", nb + 1)
                    need(dve, "spread_ps", 2 * nb)
                    v.tensor_tensor(max_diag[:].rearrange("p (r c) -> p r c", r=RB), ident[:, None, :].to_broadcast((128, RB, 128)),
                                    max_all[:, :, None].to_broadcast((128, RB, 128)), ALU.mult).then_inc(s["diag_done"], 1)

            def take_u(b):
                need(dve, "weighted", CH * (b + 1))
                need(dve, "u_normed", 2 * b)
                v.tensor_copy(u_raw[:, 1, :], usum_ps[:, 1, :]).then_inc(s["u_dve"], 1)

            def normalise(b, kb, pair, which, bank):
                need(dve, "sums_ps", 2 * b + which + 1)
                need(dve, "u_normed", 2 * b + which)
                v.reciprocal(sum_recip[:], ps[:, bank, 0:HALF]).then_inc(s["recip_done"], 1)
                need(dve, "recip_done", 2 * b + which + 1)
                need(dve, "u_dve" if which else "u_act", b + 1)
                need(dve, "projected", pair)
                v.tensor_tensor(u_norm[:, HB * which:HB * which + HB, kb, :], u_raw[:, which, :].rearrange("p (h q) -> p h q", h=HB),
                                sum_recip[:].rearrange("p (h q) -> p h q", h=HB), ALU.mult).then_inc(s["u_normed"], 1)

            def add_attention(pair, bank):
                need(dve, "projected", pair + 1)
                tile = resid[:, bass.ds(pair * D, D)]
                v.tensor_tensor(tile, tile, ps[0:TOK, bank, 0:D], ALU.add).then_inc(s["x2_done"], 1)

            for n in range(MP):
                turned_lo(-1, 1, n, SIDE + n % 2)
            query_lo(-1, 1)
            for n in range(RB * MP):
                read_max(-1, 1, n, SIDE + n % 2)

            def period(i, k):
                b = 2 * i + k
                first = isinstance(i, int) and i == 0 and k == 0
                last = isinstance(i, int) and i == PAIRS - 1 and k == 1
                for j in range(CH):
                    c = CH * b + j
                    if j == 0 and not first:
                        take_u(b - 1)
                    need(dve, "prob_hi_done", c + 1)
                    need(dve, "weighted", c - 2)
                    v.tensor_tensor(p_lo[j % 3][:], probs[j % 3], p_hi[j % 3][:].bitcast(F32), ALU.subtract).then_inc(s["prob_lo_done"], 1)
                    if j == 0 and not last:
                        query_lo(i, k)
                    for what, which, bank in slot_work(i, k, j):
                        if what == "turn":
                            turned_lo(i, k, which, bank)
                        elif what == "max":
                            read_max(i, k, which, bank)
                        elif what == "sums":
                            normalise(b - 1, 1 - k, i if k else i - 1, which, bank)
                        elif what == "project":
                            add_attention(i - 1, bank)

            sequence(dve, period)
            take_u(B - 1)
            for n in range(2):
                normalise(B - 1, 1, PAIRS - 1, n, SIDE + n)
            add_attention(PAIRS - 1, SIDE)

            need(dve, "x2_done", PAIRS)
            dve.wait_ge(s["rows_ps"], 1)
            v.tensor_copy(rows_b.rearrange("p n d -> p (n d)"), ps[0:TOK, 5, 0:3 * D]).then_inc(s["rows_copied"], 1)
            layer_norm(3)
            route_count = [0]

            def route(m):
                route_count[0] += 1
                m.then_inc(s["onehot_step"], 1)
                dve.wait_ge(s["onehot_step"], route_count[0])

            dve.wait_ge(s["logit_ps"], 1)
            route(v.tensor_copy(logits.rearrange("p k e -> p (k e)"), ps[0:TOK, 4, 0:PAIRS * E]))
            route(v.tensor_reduce(best, logits, AX.X, ALU.max))
            route(v.tensor_tensor(is_best, logits, best[:, :, None].to_broadcast((TOK, PAIRS, E)), ALU.is_equal))
            route(v.tensor_copy(seen, is_best[:, :, 0]))
            route(v.tensor_copy(onehot_k[:, :, 0], is_best[:, :, 0]))
            for e in range(1, E):
                route(v.scalar_tensor_tensor(onehot_k[:, :, e], seen, 0.5, is_best[:, :, e], ALU.is_lt, ALU.mult))
                if e + 1 < E:
                    route(v.tensor_tensor(seen, seen, is_best[:, :, e], ALU.max))
            assert route_count[0] == ONEHOT_STEPS

            def mask_experts(n):
                for t in range(G4):
                    tile = G4 * n + t
                    need(dve, "expT_ps", tile - 1)
                    v.tensor_tensor(experts_in[:, t % 2], xnorm[:, tile, None, :].to_broadcast((TOK, E, D)),
                                    onehot_k[:, tile, :, None].to_broadcast((TOK, E, D)), ALU.mult).then_inc(s["masked"], 1)

            y_count = [0]

            def step(m):
                y_count[0] += 1
                m.then_inc(s["y_step"], 1)
                dve.wait_ge(s["y_step"], y_count[0])

            def over_t(n):
                return rows_b[:, n, None, :].to_broadcast((TOK, G4, D))

            dve.wait_ge(s["rows_copied"], 1)
            mask_experts(0)
            for n in range(GROUPS):
                if n + 1 < GROUPS:
                    mask_experts(n + 1)
                tiles = slice(G4 * n, G4 * n + G4)
                y, o = y_sb[:, n % 2], o_sb[:, n % 2]
                need(dve, "y_ps", n + 1)
                v.tensor_tensor(y, ps[0:TOK, 4 + n % 2, :].rearrange("p (k d) -> p k d", k=G4), xnorm[:, tiles, :], ALU.add).then_inc(s["y_added"], 1)
                dve.wait_ge(s["y_added"], n + 1)
                step(v.tensor_tensor(y, y, over_t(0), ALU.add))
                for t in range(G4):
                    m = v.bn_stats(stats[:, t, :], y[:, t, :])
                step(m)
                for t in range(G4):
                    m = v.bn_aggr(meanvar[:, t, :], stats[:, t, :])
                step(m)
                v.tensor_scalar(veps[:, tiles], meanvar[:, 0:G4, 1], 1e-12, None, ALU.add).then_inc(s["y_var"], 1)
                dve.wait_ge(s["y_pow"], n + 1)
                for t in range(G4):
                    m = v.tensor_scalar(y[:, t, :], y[:, t, :], meanvar[:, t, 0:1], rstd[:, G4 * n + t:G4 * n + t + 1], ALU.subtract, ALU.mult)
                step(m)
                step(v.tensor_tensor(y, y, over_t(1), ALU.mult))
                step(v.tensor_tensor(y, y, over_t(2), ALU.add))
                need(dve, f"out_stored{n % 2}", 16 * (n // 2))
                v.tensor_tensor(o, y, resid_k[:, tiles, :], ALU.add).then_inc(s["out_made"], 1)


_INS = ["x", "ctx_1024", "L0_attn_W_ih", "L0_attn_W_hh", "L0_attn_b_ih", "L0_attn_b_hh", "L0_attn_W_mu", "L0_attn_b_mu",
        "L0_attn_W_sig", "L0_attn_b_sig", "L0_xattn_WQ", "L0_xattn_WK", "L0_xattn_WV", "L0_xattn_WO", "L0_xattn_bO",
        "L0_ffn_W_router", "L0_ffn_W1", "L0_ffn_b1", "L0_ffn_Wo", "L0_ffn_bo", "L0_ffn_ln_gamma", "L0_ffn_ln_beta"]


def kernel(**inputs):
    import numpy as _np
    import concourse.bacc as _bacc
    from concourse import mybir as _mybir
    from concourse.bass_utils import run_bass_kernel_spmd as _run

    nc = _bacc.Bacc("TRN2", target_bir_lowering=False, num_devices=1)
    arrays, args = {}, []
    for name in _INS:
        a = _np.ascontiguousarray(inputs[name])
        arrays[f"in_{name}_dram"] = a
        args.append(nc.dram_tensor(f"in_{name}_dram", a.shape, _mybir.dt.from_np(a.dtype), kind="ExternalInput").ap())
    out = nc.dram_tensor("out_0_dram", inputs["x"].shape, _mybir.dt.float32, kind="ExternalOutput").ap()
    decoder_layer(nc, *args, out)
    r = _run(nc, [arrays], core_ids=[0])
    return r.results[0]["out_0_dram"]
```

```python
from contextlib import ExitStack

import concourse.bass as bass
from concourse import mybir

F32 = mybir.dt.float32
F32R = mybir.dt.float32r
I32 = mybir.dt.int32
ALU = mybir.AluOpType
ACT = mybir.ActivationFunctionType
AX = mybir.AxisListType


def decoder_layer(nc, x, ctx_1024, W_ih, W_hh, b_ih, b_hh, W_mu, b_mu, W_sig, b_sig,
                  WQ, WK, WV, WO, bO, W_router, W1, b1, Wo, bo, ln_gamma, ln_beta, out):
    B, S, D = x.shape
    L = ctx_1024.shape[1]
    PE = W_hh.shape[1]
    NB = W_mu.shape[0]
    E, _, FF = W1.shape
    DK = 64
    H = WQ.shape[1] // DK
    TOK = 2 * S
    PAIRS = B // 2
    CH = 12
    CR = L // CH
    HQ = H * S
    HALF = HQ // 2
    HB = H // 2
    RB = HQ // 128
    MP = 3
    MC = L // MP
    TG = CH // MP
    SCALE = 1.0 / DK ** 0.5
    G4 = 4
    MB = FF // 128
    GROUPS = PAIRS // G4
    GT = G4 * TOK
    U8 = 2 * G4
    ITERS = S // U8
    ONEHOT_STEPS = 5 + 2 * (E - 1) - 1
    assert CR * CH == L and RB * 128 == HQ and PAIRS % G4 == 0 and S % U8 == 0

    with ExitStack() as stack:
        def sb(name, shape, dt=F32):
            return stack.enter_context(nc.sbuf_tensor(name, shape, dt))

        ps = stack.enter_context(nc.psum_tensor("ps", [128, 8, 512], F32))
        score_ps = [ps[0:CR, 2 * n:2 * n + 2, 0:HALF] for n in range(2)]
        usum_ps = ps[:, 4:6, 0:HALF]
        SIDE = 6

        resid = sb("resid", [TOK, PAIRS * D])
        resid_k = resid[:].rearrange("p (k d) -> p k d", k=PAIRS)
        xnorm = sb("xnorm", [TOK, PAIRS, D])
        xT = sb("xT", [D, PAIRS, TOK])
        ident = sb("ident", [128, 128])
        ones = sb("ones", [128, 128])
        ones_r = sb("ones_r", [128, 128], F32R)
        qk_w = sb("qk_w", [D, H, D])
        vo_w = sb("vo_w", [D, H, D])
        bO_row = sb("bO_row", [1, D])
        w1_sb = sb("w1_sb", [D, E, FF])
        b1_sb = sb("b1_sb", [E, FF])
        wo_sb = sb("wo_sb", [128, MB, D])
        rows_sb = sb("rows_sb", [1, 3, D])
        wr_sb = sb("wr_sb", [D, E])
        stats = sb("stats", [TOK, PAIRS, 6])
        meanvar = sb("meanvar", [TOK, PAIRS, 2])
        veps = sb("veps", [TOK, PAIRS])
        rstd = sb("rstd", [TOK, PAIRS])
        minus_half = sb("minus_half", [TOK, PAIRS])

        ctx_raw = [sb(f"ctx_raw{n}", [128, CH * D]) for n in range(2)]
        ctx_in = [r[0:CR, :].rearrange("p (c d) -> p c d", c=CH) for r in ctx_raw]
        ctx_hi = [sb(f"ctx_hi{n}", [CR, CH, D], F32R) for n in range(2)]
        ctx_lo = [sb(f"ctx_lo{n}", [CR, CH, D], F32R) for n in range(2)]
        ctxT_hi = [sb(f"ctxT_hi{n}", [D, L], F32R) for n in range(2)]
        ctxT_lo = [sb(f"ctxT_lo{n}", [D, L], F32R) for n in range(2)]
        q_hi = [sb(f"q_hi{n}", [D, HQ], F32R) for n in range(2)]
        q_lo = [sb(f"q_lo{n}", [D, HQ], F32R) for n in range(2)]
        p_hi = [sb(f"p_hi{n}", [CR, 2, HALF], F32R) for n in range(3)]
        p_lo = [sb(f"p_lo{n}", [CR, 2, HALF], F32R) for n in range(3)]
        max_diag = sb("max_diag", [128, HQ], F32R)
        max_parts = sb("max_parts", [128, RB * MP])
        max_all = sb("max_all", [128, RB])
        sum_recip = sb("sum_recip", [TOK, H])
        odd_heads = sb("odd_heads", [TOK, D])
        bO_b = sb("bO_b", [TOK, D])
        wo_raw = sb("wo_raw", [128, H // 2, D])

        ARENA = 12 * HQ
        arena = sb("arena", [128, ARENA])
        at = [0]

        def cut(size, parts=128):
            at[0] += size
            assert at[0] <= ARENA
            return arena[0:parts, at[0] - size:at[0]]

        neg_max = [cut(HQ).rearrange("p (a b) -> p a b", a=2) for n in range(2)]
        probs = [cut(HQ, CR).rearrange("p (a b) -> p a b", a=2) for n in range(3)]
        prob_sum = cut(2 * HQ, CR).rearrange("p (h b q) -> p h b q", h=H, b=2)
        u_sum = cut(2 * HQ).rearrange("p (h b q) -> p h b q", h=H, b=2)
        q_stage = cut(2 * HQ).rearrange("p (b h q) -> p b h q", b=2, h=H)

        at[0] = 0
        W = PAIRS * TOK
        gauss_d = cut(W, TOK).rearrange("p (k i) -> p k i", k=PAIRS)
        gauss_w = cut(W, TOK).rearrange("p (k i) -> p k i", k=PAIRS)
        gauss_wT = cut(W, TOK).rearrange("p (k j) -> p k j", k=PAIRS)
        lstm_h = cut(U8 * B).rearrange("p (u b) -> p u b", u=U8)
        w_in = cut(D)
        w_hh_in = cut(PE)
        w_head_in = cut(PE)
        wihT = cut(4 * PE)
        whhT = cut(4 * PE)
        headT = cut(NB + 1)
        gate_act = cut(4 * B, PE).rearrange("p (g b) -> p g b", g=4)
        cell = cut(B, PE)
        cell_f = cut(B, PE)
        cell_i = cut(B, PE)
        cell_t = cut(B, PE)
        mu_w = cut(NB * S, B).rearrange("p (n t) -> p n t", n=NB)
        mu_t = cut(S, B)
        mu_b = cut(S, B)
        mu = cut(S, B)
        sig = cut(S, B)
        sig2 = cut(S, B)
        inv2s = cut(S, B)
        jp1 = cut(S, B)
        pick_b = cut(TOK, B).rearrange("p (b j) -> p b j", b=2)
        pick_k = cut(PAIRS, B)
        mu_l = cut(TOK, B).rearrange("p (b j) -> p b j", b=2)
        inv_l = cut(TOK, B).rearrange("p (b j) -> p b j", b=2)
        mu_tok = cut(2 * PAIRS, TOK).rearrange("p (a k) -> p a k", a=2)
        rel = cut(TOK, TOK)
        causal = cut(TOK, TOK)
        i_idx = cut(TOK, TOK)
        pos = cut(4, TOK)
        wsum = cut(PAIRS, TOK)
        jp1_int = cut(S, B).bitcast(I32)
        idx_int = cut(TOK, TOK).bitcast(I32)
        p_int = cut(1, TOK).bitcast(I32)

        wq_raw = ctx_raw[1][:, 0:H * DK]
        wk_raw = w1_sb[:].rearrange("p e f -> p (e f)")[:, 0:H * DK]
        wv_raw = w1_sb[:].rearrange("p e f -> p (e f)")[:, H * DK:2 * H * DK]
        wT_sb = sb("wT_sb", [128, 2, 3, D])

        at[0] = 0
        experts_in = cut(2 * E * D, TOK).rearrange("p (n e d) -> p n e d", n=2, e=E)
        expertsT = [cut(E * GT).rearrange("p (e k t) -> p e k t", e=E, k=G4) for n in range(2)]
        inter = [cut(MB * GT).rearrange("p (m t) -> p m t", m=MB) for n in range(2)]
        onehotT = cut(PAIRS * TOK, E)
        seen = cut(PAIRS, TOK)
        best = cut(PAIRS, TOK)
        logits = cut(PAIRS * E, TOK).rearrange("p (k e) -> p k e", e=E)
        is_best = cut(PAIRS * E, TOK).rearrange("p (k e) -> p k e", e=E)
        onehot = cut(PAIRS * E, TOK)
        onehot_k = onehot.rearrange("p (k e) -> p k e", e=E)
        rows_b = cut(3 * D, TOK).rearrange("p (n d) -> p n d", n=3)
        y_sb = ctx_raw[0][0:TOK, 0:2 * G4 * D].rearrange("p (n k d) -> p n k d", n=2, k=G4)
        o_sb = ctx_raw[1][0:TOK, 0:2 * G4 * D].rearrange("p (n k d) -> p n k d", n=2, k=G4)

        s = {name: stack.enter_context(nc.semaphore("s_" + name)) for name in (
            "x_in lstm_w_in bias_in attn_w_in ffn_w_in ctx_in0 ctx_in1 out_stored0 out_stored1 "
            "identity_made ones_made minus_made indices_made rel_made causal_made picks_made zeros_made "
            "biased_cleared lstm_w_ps lstm_w_sb "
            "ln_step ln_var rstd_done ln_done xT_ps xT_sb ones_r_made "
            "gates_ready sig_ready tanhg_ready cell_step tanhc_ready h_ready head_ready head_read "
            "sigma_done pick_ps picks_read gauss_step rows_picked gauss_diff gauss_sq gauss_arg gauss_exp gauss_ready gauss_w2 "
            "norm_in norm_done gaussT_ps gaussT_sb self_attn_ps x1_done bO_added "
            "turned_w turned_w_sb folded folded_sb bits_set "
            "ctx_hi_done ctx_lo_done ctxT_ps ctxT_hi_done ctxT_lo_done q_ps q_staged q_hi_done q_lo_done "
            "max_ps max_read max_found diag_done spread_ps neg_done seeded scored prob_done prob_hi_done "
            "prob_lo_done prob_added weighted u_act u_dve sums_ps recip_done projected head_added x2_done "
            "rows_ps rows_copied logit_ps onehot_step onehotT_ps onehotT_sb masked expT_ps expT_sb hid_ps hid_act "
            "y_ps y_added y_step y_var y_pow out_made"
        ).split()}

        def need(eng, name, value):
            if not isinstance(value, int) or value > 0:
                eng.wait_ge(s[name], value)

        MAX_UNITS_0 = (3, 3, 2, 2, 2, 2, 3, 3, 1)
        MAX_UNITS_1 = (3, 3, 3, 2, 2, 2, 2, 2, 2)
        assert sum(MAX_UNITS_0) == sum(MAX_UNITS_1) == RB * MP
        CP = 4
        PC = CH // CP

        def side_work(i, k):
            first = isinstance(i, int) and i == 0
            last = isinstance(i, int) and i == PAIRS - 1
            work, per_slot = {}, (MAX_UNITS_0 if k == 0 else MAX_UNITS_1)
            if not (last and k == 1):
                free = [(j, p) for j, count in enumerate(per_slot) for p in (0, 1, 3)[:count]]
                work.update({place: ("max", n) for n, place in enumerate(free)})
                work.update({(9, 2): ("spread", 0), (9, 3): ("spread", 1)})
            if not last:
                work.update({(9, 0): ("turn", 0), (10, 0): ("turn", 1), (11, 0): ("turn", 2)})
            if k == 0 and not first:
                work[1, 2] = ("sums", 0)
                work.update({(2 + n, 2): ("project", n) for n in range(4)})
            if k == 0 and not last:
                work.update({place: ("query", u) for u, place in enumerate([(6, 2), (7, 2), (8, 2), (9, 1)])})
            return [(place, *work[place], SIDE + n % 2) for n, place in enumerate(sorted(work))]

        def bank_read(what, which, i, k):
            nb = 2 * i + k + 1
            return {"turn": ("ctxT_lo_done", MP * (nb + 1) + which + 1), "max": ("max_read", RB * MP * nb + which + 1),
                    "spread": ("neg_done", 2 * nb + which + 1), "sums": ("recip_done", i),
                    "project": ("head_added", H * (i - 1) + 4 * (which + 1)), "query": ("q_staged", 4 * (i + 1) + which + 1)}[what]

        def side_banks(i, k):
            if isinstance(i, int) and i == 0 and k == 0:
                before = {SIDE + 1: ("neg_done", 1), SIDE: ("neg_done", 2)}
            else:
                pi, pk = (i, 0) if k else (i - 1, 1)
                before = {bank: bank_read(what, which, pi, pk) for _, what, which, bank in side_work(pi, pk)}
            rows = []
            for place, what, which, bank in side_work(i, k):
                rows.append((place, what, which, bank, before[bank]))
                before[bank] = bank_read(what, which, i, k)
            return rows

        def slot_work(i, k, j):
            return [(what, which, bank) for (slot, _), what, which, bank in side_work(i, k) if slot == j]

        def sequence(eng, period):
            for k in range(2):
                period(0, k)
            with eng.Fori(1, PAIRS - 1) as i:
                for k in range(2):
                    period(i, k)
            for k in range(2):
                period(PAIRS - 1, k)

        FOLD_BANK = 4
        SELF_BANK = (4, 5, 0, 1)
        TOKEN_BANKS = ((4, 5, 6, 7), (2, 3, 4, 5), (0, 1, 2, 3))

        block = stack.enter_context(nc.Block())

        @block.sync
        def _(sp):
            sp.dma_start(resid_k, x.rearrange("b s d -> (b s) d").rearrange("(k p) d -> p k d", p=TOK)).then_inc(s["x_in"], 16)
            sp.dma_start(w_in[0:4 * PE, :], W_ih).then_inc(s["lstm_w_in"], 16)
            sp.dma_start(w_hh_in[0:4 * PE, :], W_hh).then_inc(s["lstm_w_in"], 16)
            sp.dma_start(w_head_in[0:NB, :], W_mu).then_inc(s["lstm_w_in"], 16)
            sp.dma_start(w_head_in[NB:NB + 1, :], W_sig).then_inc(s["lstm_w_in"], 16)
            need(sp, "biased_cleared", 2)
            sp.dma_start(headT[PE:PE + 1, 0:NB], b_mu.rearrange("(a n) -> a n", a=1)).then_inc(s["bias_in"], 16)
            sp.dma_start(headT[PE:PE + 1, NB:NB + 1], b_sig.rearrange("(a n) -> a n", a=1)).then_inc(s["bias_in"], 16)
            sp.dma_start(whhT[PE:PE + 1, :], b_ih.rearrange("(a n) -> a n", a=1)).then_inc(s["bias_in"], 16)
            sp.dma_start(whhT[PE + 1:PE + 2, :], b_hh.rearrange("(a n) -> a n", a=1)).then_inc(s["bias_in"], 16)
            sp.dma_start(wq_raw, WQ).then_inc(s["attn_w_in"], 16)
            sp.dma_start(wk_raw, WK).then_inc(s["attn_w_in"], 16)
            sp.dma_start(wv_raw, WV).then_inc(s["attn_w_in"], 16)
            sp.dma_start(wo_raw[:], WO.rearrange("(c p) n -> p c n", p=128)).then_inc(s["attn_w_in"], 16)
            sp.dma_start(bO_row[:], bO.rearrange("(a n) -> a n", a=1)).then_inc(s["attn_w_in"], 16)
            sp.dma_start(ctx_in[0], ctx_1024[0].rearrange("(p c) d -> p c d", p=CR)).then_inc(s["ctx_in0"], 16)
            sp.dma_start(b1_sb[:], b1).then_inc(s["ffn_w_in"], 16)
            sp.dma_start(wo_sb[:], Wo.rearrange("(m p) n -> p m n", p=128)).then_inc(s["ffn_w_in"], 16)
            sp.dma_start(wr_sb[:], W_router).then_inc(s["ffn_w_in"], 16)
            for n, row in enumerate((bo, ln_gamma, ln_beta)):
                sp.dma_start(rows_sb[:, n, :], row.rearrange("(a n) -> a n", a=1)).then_inc(s["ffn_w_in"], 16)
            need(sp, "turned_w", H // 2)
            sp.dma_start(ctx_in[1], ctx_1024[1].rearrange("(p c) d -> p c d", p=CR)).then_inc(s["ctx_in1"], 16)
            sp.dma_start(w1_sb[:], W1.rearrange("e h i -> h e i")).then_inc(s["ffn_w_in"], 16)
            out_k = out.rearrange("b s d -> (b s) d").rearrange("(k p) d -> p k d", p=TOK)
            for g in range(GROUPS):
                need(sp, "out_made", g + 1)
                sp.dma_start(out_k[:, G4 * g:G4 * g + G4, :], o_sb[:, g % 2]).then_inc(s[f"out_stored{g % 2}"], 16)
            for n in range(2):
                sp.wait_ge(s[f"out_stored{n}"], 16 * (GROUPS // 2))

        @block.gpsimd
        def _(pool):
            g = nc.gpsimd
            g.memset(headT, 0.0).then_inc(s["biased_cleared"], 1)
            g.memset(whhT, 0.0).then_inc(s["biased_cleared"], 1)
            g.memset(lstm_h, 1.0).then_inc(s["zeros_made"], 1)
            g.memset(cell, 0.0).then_inc(s["zeros_made"], 1)
            pool.wait_ge(s["zeros_made"], 1)
            g.memset(lstm_h[0:PE, U8 - 1, :], 0.0).then_inc(s["zeros_made"], 1)
            g.memset(ident[:], 0.0).then_inc(s["identity_made"], 1)
            pool.wait_ge(s["identity_made"], 1)
            g.affine_select(out=ident[:], in_=ident[:], compare_op=ALU.not_equal, fill=1.0, base=0,
                            pattern=[[-1, 128]], channel_multiplier=1).then_inc(s["identity_made"], 1)
            g.memset(ones[:], 1.0).then_inc(s["ones_made"], 1)
            g.memset(minus_half[:], -0.5).then_inc(s["minus_made"], 1)

            def powers(count):
                for q in range(GROUPS):
                    tiles = slice(G4 * q, G4 * q + G4)
                    pool.wait_ge(s["ln_var"], GROUPS * (count - 1) + q + 1)
                    g.tensor_tensor(rstd[:, tiles], veps[:, tiles], minus_half[:, tiles], ALU.pow).then_inc(s["rstd_done"], 1)

            pool.wait_ge(s["minus_made"], 1)
            powers(1)
            g.iota(jp1_int, [[1, S]], base=1, channel_multiplier=0).then_inc(s["indices_made"], 1)
            g.iota(idx_int.rearrange("p (b i) -> p b i", b=2), [[0, 2], [1, S]], base=0, channel_multiplier=0).then_inc(s["indices_made"], 1)
            g.iota(p_int, [[0, 1]], base=1, channel_multiplier=1).then_inc(s["indices_made"], 1)
            g.memset(pos[:, 1:2], -float(S)).then_inc(s["rel_made"], 1)
            pool.wait_ge(s["rel_made"], 1)
            g.affine_select(out=pos[:, 1:2], in_=pos[:, 1:2], compare_op=ALU.is_ge, fill=0.0, base=-S,
                            pattern=[[0, 1]], channel_multiplier=1).then_inc(s["rel_made"], 1)
            causal_v = causal.rearrange("p (b i) -> p b i", b=2)
            g.memset(causal, 1.0).then_inc(s["causal_made"], 1)
            pool.wait_ge(s["causal_made"], 1)
            g.affine_select(out=causal_v, in_=causal_v, compare_op=ALU.is_ge, fill=0.0, base=0,
                            pattern=[[-S, 2], [-1, S]], channel_multiplier=1).then_inc(s["causal_made"], 1)
            pool.wait_ge(s["causal_made"], 2)
            g.affine_select(out=causal_v, in_=causal_v, compare_op=ALU.is_ge, fill=0.0, base=S - 1,
                            pattern=[[S, 2], [0, S]], channel_multiplier=-1).then_inc(s["causal_made"], 1)
            g.memset(pick_b, 1.0).then_inc(s["picks_made"], 1)
            g.memset(pick_k, 0.0).then_inc(s["picks_made"], 1)
            pool.wait_ge(s["picks_made"], 2)
            g.affine_select(out=pick_b, in_=pick_b, compare_op=ALU.is_ge, fill=0.0, base=0,
                            pattern=[[-PAIRS, 2], [0, S]], channel_multiplier=1).then_inc(s["picks_made"], 1)
            g.affine_select(out=pick_k, in_=pick_k, compare_op=ALU.not_equal, fill=1.0, base=0,
                            pattern=[[-1, PAIRS]], channel_multiplier=1).then_inc(s["picks_made"], 1)
            pool.wait_ge(s["picks_made"], 4)
            g.affine_select(out=pick_b, in_=pick_b, compare_op=ALU.is_ge, fill=0.0, base=PAIRS - 1,
                            pattern=[[PAIRS, 2], [0, S]], channel_multiplier=-1).then_inc(s["picks_made"], 1)
            g.affine_select(out=pick_k, in_=pick_k, compare_op=ALU.not_equal, fill=1.0, base=-PAIRS,
                            pattern=[[-1, PAIRS]], channel_multiplier=1).then_inc(s["picks_made"], 1)

            def context_halves(i, k, part):
                nb, chunks = 2 * i + k, slice(PC * part, PC * part + PC)
                need(pool, f"ctx_in{k}", 16 * (i + 1))
                need(pool, "weighted", CH * (nb - 1))
                g.tensor_tensor(ctx_hi[k][:, chunks, :], ctx_in[k][:, chunks, :], ones[0:CR, None, :].to_broadcast((CR, PC, D)), ALU.mult).then_inc(s["ctx_hi_done"], 1)
                need(pool, "ctx_hi_done", CP * nb + part + 1)
                g.tensor_tensor(ctx_lo[k][:, chunks, :], ctx_in[k][:, chunks, :], ctx_hi[k][:, chunks, :].bitcast(F32),
                                ALU.subtract).then_inc(s["ctx_lo_done"], 1)

            for part in range(CP):
                context_halves(0, 0, part)
            for q in range(GROUPS):
                tiles = slice(G4 * q, G4 * q + G4)
                pool.wait_ge(s["norm_in"], q + 1)
                g.tensor_tensor(wsum[:, tiles], wsum[:, tiles], minus_half[:, tiles], ALU.pow).then_inc(s["norm_done"], 1)
            powers(2)
            need(pool, "ln_done", 2 * GROUPS)
            g.tensor_tensor(resid_k, resid_k, bO_b[:, None, :].to_broadcast((TOK, PAIRS, D)), ALU.add).then_inc(s["bO_added"], 1)

            def period(i, k):
                b = 2 * i + k
                for j in range(1, CH):
                    need(pool, "prob_done", CH * b + j + 1)
                    summed = prob_sum[:, :, k, :]
                    chunk = [probs[n].rearrange("p a (h q) -> p (a h) q", h=HB) for n in range(3)]
                    if j == 1:
                        if k == 0:
                            need(pool, "sums_ps", i)
                        g.tensor_tensor(summed, chunk[0], chunk[1], ALU.add).then_inc(s["prob_added"], 1)
                    else:
                        need(pool, "prob_added", (CH - 1) * b + j - 1)
                        g.tensor_tensor(summed, summed, chunk[j % 3], ALU.add).then_inc(s["prob_added"], 1)
                    if j % 2 == 0 and j // 2 <= CP and not (isinstance(i, int) and i == PAIRS - 1 and k == 1):
                        context_halves(i + k, 1 - k, j // 2 - 1)

            sequence(pool, period)

            powers(3)
            for n in range(GROUPS):
                pool.wait_ge(s["y_var"], n + 1)
                g.tensor_tensor(rstd[:, G4 * n:G4 * n + G4], veps[:, G4 * n:G4 * n + G4], minus_half[:, 0:G4],
                                ALU.pow).then_inc(s["y_pow"], 1)

        @block.tensor
        def _(pe):
            mm, tr = nc.tensor.matmul, nc.tensor.transpose

            pe.wait_ge(s["identity_made"], 2)
            pe.wait_ge(s["lstm_w_in"], 64)
            tr(ps[:, 3, 0:4 * PE], w_in[0:4 * PE, :], ident[0:4 * PE, 0:4 * PE])
            tr(ps[0:PE, 3, 128:128 + 4 * PE], w_hh_in[0:4 * PE, :], ident[0:4 * PE, 0:4 * PE])
            tr(ps[0:PE, 3, 256:256 + NB + 1], w_head_in[0:NB + 1, :], ident[0:NB + 1, 0:NB + 1]).then_inc(s["lstm_w_ps"], 1)

            def turn_tokens(banks, count, q):
                pe.wait_ge(s["ln_done"], GROUPS * (count - 1) + q + 1)
                for t in range(G4):
                    m = tr(ps[:, banks[q], t * TOK:(t + 1) * TOK], xnorm[:, G4 * q + t, :], ident[0:TOK, 0:TOK])
                m.then_inc(s["xT_ps"], 1)

            for q in range(GROUPS):
                turn_tokens(TOKEN_BANKS[0], 1, q)

            GATE = (0, 1, 3, 2)
            xT_steps = xT[:].rearrange("d k (b t) -> d t b k", b=2)
            pe.wait_ge(s["xT_sb"], 4)
            pe.wait_ge(s["lstm_w_sb"], 3)
            pe.wait_ge(s["bias_in"], 64)
            pe.wait_ge(s["zeros_made"], 3)

            def input_part(bank, gate, t0):
                mm(ps[0:PE, bank, gate * 128:(gate + 1) * 128], wihT[:, GATE[gate] * PE:(GATE[gate] + 1) * PE],
                   xT_steps[:, bass.ds(t0, G4), :, :], start=(gate == 0), stop=False, skip_group_check=True)

            def head(it, u):
                return mm(ps[0:B, 2, bass.ds((U8 * it + u) * (NB + 1), NB + 1)], lstm_h[:, u, :], headT, start=True, stop=True)

            def lstm_steps(it, beside=None):
                first, last = isinstance(it, int) and it == 0, isinstance(it, int) and it == ITERS - 1
                for u in range(U8):
                    bank, v = u // G4, u % G4
                    need(pe, "h_ready", U8 * it + u)
                    for gate in range(4):
                        m = mm(ps[0:PE, bank, gate * 128 + v * B:gate * 128 + (v + 1) * B],
                               whhT[:, GATE[gate] * PE:(GATE[gate] + 1) * PE], lstm_h[:, (u - 1) % U8, :],
                               start=False, stop=True, skip_group_check=True)
                    m.then_inc(s["gates_ready"], 1)
                    if u:
                        head(it, u - 1)
                    elif not first:
                        head(it - 1, U8 - 1)
                    if bank == 0:
                        input_part(1, v, U8 * it + G4)
                    elif not last:
                        input_part(0, v, U8 * it + U8)
                    if beside:
                        beside(u)

            def turn_weights(f):
                if f == 0:
                    pe.wait_ge(s["attn_w_in"], 80)
                need(pe, "turned_w_sb", f - 1)
                for n, w in enumerate((wq_raw, wk_raw, wv_raw)):
                    m = tr(ps[:, SIDE + f % 2, n * D:(n + 1) * D], w[:, f * D:(f + 1) * D], ident[:])
                m.then_inc(s["turned_w"], 1)

            def fold(f):
                need(pe, "turned_w_sb", f + 1)
                need(pe, "folded_sb", 2 * f)
                for n in range(2):
                    part = slice(DK * n, DK * n + DK)
                    mm(ps[:, FOLD_BANK + n, 0:D], wT_sb[part, f % 2, 0, :], wT_sb[part, f % 2, 1, :], start=True, stop=True)
                    m = mm(ps[:, FOLD_BANK + n, D:2 * D], wT_sb[part, f % 2, 2, :], wo_raw[part, f, :], start=True, stop=True)
                m.then_inc(s["folded"], 1)

            def side(what, which, bank, i, k):
                nk, nb = 1 - k, 2 * i + k + 1
                if what == "turn":
                    if which == 0:
                        need(pe, f"ctx_in{k}", 16 * (i + 2))
                    for c in range(TG):
                        m = tr(ps[:, bank, c * CR:(c + 1) * CR], ctx_in[k][:, which * TG + c, :], ident[0:CR, 0:CR])
                    m.then_inc(s["ctxT_ps"], 1)
                elif what == "max":
                    block_, part = which // MP, which % MP
                    if which == 0:
                        need(pe, "q_hi_done", nb + 1)
                    if which < MP:
                        need(pe, "ctxT_hi_done", MP * nb + part + 1)
                    mm(ps[:, bank, 0:MC], q_hi[nk][:, block_ * 128:(block_ + 1) * 128], ctxT_hi[nk][:, part * MC:(part + 1) * MC],
                       start=True, stop=True).then_inc(s["max_ps"], 1)
                elif what == "spread":
                    if which == 0:
                        need(pe, "diag_done", nb + 1)
                    mm(ps[:, bank, 0:HALF], ones_r[:], max_diag[:, which * HALF:(which + 1) * HALF],
                       start=True, stop=True).then_inc(s["spread_ps"], 1)
                elif what == "sums":
                    need(pe, "prob_added", (CH - 1) * (nb - 1))
                    for h in range(H):
                        m = mm(ps[0:TOK, bank, h:h + 1], prob_sum[:, h].rearrange("p b q -> p (b q)"), ones[0:CR, 0:1], start=True, stop=True)
                    m.then_inc(s["sums_ps"], 1)
                elif what == "project":
                    if which == 0:
                        need(pe, "u_act", nb - 1)
                        need(pe, "u_dve", nb - 1)
                    for n in range(4):
                        h = 4 * which + n
                        m = mm(ps[0:TOK, bank, n * D:(n + 1) * D], u_sum[:, h].rearrange("p b q -> p (b q)"), vo_w[:, h, :], start=True, stop=True)
                    m.then_inc(s["projected"], 1)
                elif what == "query":
                    for n in range(4):
                        m = mm(ps[:, bank, n * TOK:(n + 1) * TOK], qk_w[:, 4 * which + n, :],
                               xT[:, bass.ds(i + 1, 1), :].rearrange("p k t -> p (k t)"), start=True, stop=True)
                    m.then_inc(s["q_ps"], 1)

            def beside_first(u):
                turn_weights(u)
                if u:
                    fold(u - 1)

            def beside_last(u):
                if u == 0:
                    fold(H // 2 - 1)
                elif u >= 2:
                    need(pe, "ctxT_lo_done", u - 3)
                    side("turn", (u - 2) % MP, SIDE + u % 2, -1, (u - 2) // MP)

            for gate in range(4):
                input_part(0, gate, 0)
            lstm_steps(0, beside_first)
            with pe.Fori(1, ITERS - 1) as it:
                lstm_steps(it)
            lstm_steps(ITERS - 1, beside_last)
            need(pe, "h_ready", S)
            head(ITERS - 1, U8 - 1).then_inc(s["head_ready"], 1)

            pe.wait_ge(s["rows_picked"], 1)
            pe.wait_ge(s["picks_made"], 6)
            mm(ps[0:TOK, 3, 0:PAIRS], mu_l.rearrange("p b j -> p (b j)"), pick_k, start=True, stop=True)
            mm(ps[0:TOK, 3, PAIRS:2 * PAIRS], inv_l.rearrange("p b j -> p (b j)"), pick_k, start=True, stop=True)
            mm(ps[0:TOK, 3, 128:128 + D], ones[0:1, 0:TOK], bO_row[:], start=True, stop=True).then_inc(s["pick_ps"], 1)

            def turn_gauss(q):
                pe.wait_ge(s["gauss_ready"], q + 1)
                for t in range(G4):
                    m = tr(ps[0:TOK, q, t * TOK:(t + 1) * TOK], gauss_w[:, G4 * q + t, :], ident[0:TOK, 0:TOK])
                m.then_inc(s["gaussT_ps"], 1)

            def self_attention(q):
                pe.wait_ge(s["gaussT_sb"], q + 1)
                for t in range(G4):
                    m = mm(ps[0:TOK, SELF_BANK[q], t * D:(t + 1) * D], gauss_wT[:, G4 * q + t, :], xnorm[:, G4 * q + t, :], start=True, stop=True)
                m.then_inc(s["self_attn_ps"], 1)

            for q in range(GROUPS + 1):
                if q < GROUPS:
                    turn_gauss(q)
                if q:
                    self_attention(q - 1)

            turn_tokens(TOKEN_BANKS[1], 2, 0)
            pe.wait_ge(s["xT_sb"], GROUPS + 1)
            for u in range(4):
                need(pe, "ctxT_lo_done", 2 * MP)
                if u > 1:
                    need(pe, "q_staged", u - 1)
                side("query", u, SIDE + u % 2, -1, 0)
            for q in range(1, GROUPS):
                turn_tokens(TOKEN_BANKS[1], 2, q)
            pe.wait_ge(s["xT_sb"], 2 * GROUPS)
            for bank in range(4):
                m = mm(ps[0:CR, bank, :], ones[:, 0:CR], xT[:].rearrange("d k t -> d (k t)")[:, 0:512], start=True, stop=True)
            m.then_inc(s["bits_set"], 1)
            for n in range(RB * MP):
                if n < 2:
                    need(pe, "q_staged", 4)
                else:
                    need(pe, "max_read", n - 1)
                side("max", n, SIDE + n % 2, -1, 1)
            for n in range(2):
                need(pe, "max_read", RB * MP)
                side("spread", n, SIDE + (n + 1) % 2, -1, 1)

            def scores(b, k, j, half):
                if half == 0:
                    if j == 0:
                        need(pe, "q_lo_done", b + 1)
                        need(pe, "ctxT_lo_done", MP * (b + 1))
                    need(pe, "seeded", CH * b + j + 1)
                rows, cols = slice(j * CR, (j + 1) * CR), slice(half * HALF, (half + 1) * HALF)
                for cx, q in ((ctxT_hi, q_hi), (ctxT_hi, q_lo), (ctxT_lo, q_hi)):
                    m = mm(score_ps[j % 2][:, half, :], cx[k][:, rows], q[k][:, cols], start=False, stop=True, skip_group_check=True)
                if half == 1:
                    m.then_inc(s["scored"], 1)

            def weigh(b, k, j, half):
                if half == 0:
                    if j == 0:
                        need(pe, "u_act", b)
                        need(pe, "u_dve", b)
                        need(pe, "ctx_lo_done", CP * (b + 1))
                    need(pe, "prob_lo_done", CH * b + j + 1)
                for n, (cx, p) in enumerate(((ctx_hi, p_hi), (ctx_hi, p_lo), (ctx_lo, p_hi))):
                    m = mm(usum_ps[:, half, :], cx[k][:, j, :], p[j % 3][:, half, :], start=(j == 0 and n == 0), stop=(j == CH - 1 and n == 2))
                if half == 1:
                    m.then_inc(s["weighted"], 1)

            for half in range(2):
                scores(0, 0, 0, half)

            def period(i, k):
                b = 2 * i + k
                first = isinstance(i, int) and i == 0 and k == 0
                last = isinstance(i, int) and i == PAIRS - 1 and k == 1
                work = {(j, p): row for (j, p), *row in side_banks(i, k)}

                def beside(j, p):
                    if (j, p) in work:
                        what, which, bank, (name, value) = work[j, p]
                        need(pe, name, value)
                        side(what, which, bank, i, k)

                for j in range(CH):
                    ahead = (b, k, j + 1) if j + 1 < CH else (b + 1, 1 - k, 0)
                    behind = (b, k, j - 1) if j else (b - 1, 1 - k, CH - 1)
                    for half in range(2):
                        if j + 1 < CH or not last:
                            scores(*ahead, half)
                        beside(j, half)
                    for half in range(2):
                        if j or not first:
                            weigh(*behind, half)
                        beside(j, 2 + half)

            sequence(pe, period)
            for half in range(2):
                weigh(B - 1, 1, CH - 1, half)

            side("sums", 0, SIDE, PAIRS, 0)
            for n in range(4):
                if n == 1:
                    need(pe, "recip_done", PAIRS)
                elif n > 1:
                    need(pe, "head_added", H * (PAIRS - 1) + 4 * (n - 1))
                side("project", n, SIDE + (n + 1) % 2, PAIRS, 0)

            pe.wait_ge(s["ffn_w_in"], 16 * 7)
            mm(ps[0:TOK, 5, 0:3 * D], ones[0:1, 0:TOK], rows_sb[:].rearrange("p n d -> p (n d)"), start=True, stop=True).then_inc(s["rows_ps"], 1)
            for q in range(GROUPS):
                turn_tokens(TOKEN_BANKS[2], 3, q)
            for t in range(PAIRS):
                if t % G4 == 0:
                    pe.wait_ge(s["xT_sb"], 8 + t // G4 + 1)
                m = mm(ps[0:TOK, 4, t * E:(t + 1) * E], xT[:, t, :], wr_sb[:], start=True, stop=True)
            m.then_inc(s["logit_ps"], 1)
            pe.wait_ge(s["onehot_step"], ONEHOT_STEPS)
            for q in range(GROUPS):
                for t in range(G4):
                    m = tr(ps[0:E, q, t * TOK:(t + 1) * TOK], onehot[:, (G4 * q + t) * E:(G4 * q + t + 1) * E], ident[0:TOK, 0:TOK])
                m.then_inc(s["onehotT_ps"], 1)

            def turn_experts(n):
                for t in range(G4):
                    tile = G4 * n + t
                    need(pe, "masked", tile + 1)
                    need(pe, "expT_sb", tile - 1)
                    for e in range(E):
                        m = tr(ps[:, SIDE + t % 2, e * TOK:(e + 1) * TOK], experts_in[:, t % 2, e, :], ident[0:TOK, 0:TOK])
                    m.then_inc(s["expT_ps"], 1)

            turn_experts(0)
            pe.wait_ge(s["onehotT_sb"], GROUPS)
            for n in range(GROUPS):
                if n + 1 < GROUPS:
                    turn_experts(n + 1)
                need(pe, "expT_sb", G4 * (n + 1))
                for m_ in range(MB):
                    need(pe, "hid_act", MB * (n - 1) + m_ + 1)
                    o_ps, cols = ps[:, m_, 0:GT], slice(m_ * 128, (m_ + 1) * 128)
                    mm(o_ps, b1_sb[:, cols], onehotT[:, n * GT:(n + 1) * GT], start=True, stop=False)
                    for e in range(E):
                        m = mm(o_ps, w1_sb[:, e, cols], expertsT[n % 2][:, e].rearrange("p k t -> p (k t)"), start=False, stop=(e == E - 1))
                    m.then_inc(s["hid_ps"], 1)
                need(pe, "y_added", n - 1)
                for t in range(G4):
                    for m_ in range(MB):
                        if t == 0:
                            need(pe, "hid_act", MB * n + m_ + 1)
                        m = mm(ps[0:TOK, 4 + n % 2, t * D:(t + 1) * D], inter[n % 2][:, m_, t * TOK:(t + 1) * TOK], wo_sb[:, m_, :],
                               start=(m_ == 0), stop=(m_ == MB - 1))
                m.then_inc(s["y_ps"], 1)

        @block.scalar
        def _(act):
            a = nc.scalar.activation
            ctx_pairs = ctx_1024.rearrange("(i n) (p c) d -> n p i (c d)", n=2, p=CR)

            def load_context(i, k):
                need(act, "ctx_lo_done", CP * (2 * i + k + 1))
                need(act, "ctxT_ps", MP * (2 * i + k + 1))
                act.dma_start(ctx_raw[k][0:CR, :], ctx_pairs[k, :, bass.ds(i + 1, 1), :].rearrange("p i c -> p (i c)")).then_inc(
                    s[f"ctx_in{k}"], 16)

            def copy_tokens(banks, count, q):
                need(act, "xT_ps", GROUPS * (count - 1) + q + 1)
                a(xT[:, G4 * q:G4 * q + G4, :].rearrange("d k t -> d (k t)"), ps[:, banks[q], 0:GT], ACT.Copy).then_inc(s["xT_sb"], 1)

            act.wait_ge(s["lstm_w_ps"], 1)
            need(act, "biased_cleared", 2)
            a(wihT, ps[:, 3, 0:4 * PE], ACT.Copy).then_inc(s["lstm_w_sb"], 1)
            a(whhT[0:PE, :], ps[0:PE, 3, 128:128 + 4 * PE], ACT.Copy).then_inc(s["lstm_w_sb"], 1)
            a(headT[0:PE, :], ps[0:PE, 3, 256:256 + NB + 1], ACT.Copy).then_inc(s["lstm_w_sb"], 1)
            act.wait_ge(s["ones_made"], 1)
            a(ones_r[:], ones[:], ACT.Copy).then_inc(s["ones_r_made"], 1)
            for q in range(GROUPS):
                copy_tokens(TOKEN_BANKS[0], 1, q)

            def lstm_steps(it, beside=None):
                for u in range(U8):
                    t = U8 * it + u
                    gates = ps[0:PE, u // G4, :].rearrange("p (g t b) -> p g t b", g=4, t=G4)[:, :, u % G4, :]
                    need(act, "gates_ready", t + 1)
                    a(gate_act[:, 0:3, :], gates[:, 0:3, :], ACT.Sigmoid).then_inc(s["sig_ready"], 1)
                    a(gate_act[:, 3, :], gates[:, 3, :], ACT.Tanh).then_inc(s["tanhg_ready"], 1)
                    need(act, "cell_step", 3 * t + 3)
                    a(cell_t, cell, ACT.Tanh).then_inc(s["tanhc_ready"], 1)
                    if beside:
                        beside(u)

            def copy_turned(f):
                need(act, "turned_w", f + 1)
                need(act, "folded", f - 1)
                a(wT_sb[:, f % 2].rearrange("p n d -> p (n d)"), ps[:, SIDE + f % 2, 0:3 * D], ACT.Copy).then_inc(s["turned_w_sb"], 1)

            def fold_out(f):
                need(act, "folded", f + 1)
                for side_, w in enumerate((qk_w, vo_w)):
                    a(w[:, 2 * f:2 * f + 2, :], ps[:, FOLD_BANK:FOLD_BANK + 2, side_ * D:(side_ + 1) * D], ACT.Copy).then_inc(s["folded_sb"], 1)

            def turned_hi(i, k, which, bank):
                tb = 2 * (i + 1) + k
                need(act, "ctxT_ps", MP * tb + which + 1)
                a(ctxT_hi[k][:, which * MC:(which + 1) * MC], ps[:, bank, 0:MC], ACT.Copy).then_inc(s["ctxT_hi_done"], 1)

            def beside_first(u):
                copy_turned(u)
                if u:
                    fold_out(u - 1)

            def beside_last(u):
                if u == 1:
                    fold_out(H // 2 - 1)
                elif u >= 2:
                    turned_hi(-1, (u - 2) // MP, (u - 2) % MP, SIDE + u % 2)

            lstm_steps(0, beside_first)
            with act.Fori(1, ITERS - 1) as it:
                lstm_steps(it)
            lstm_steps(ITERS - 1, beside_last)

            act.wait_ge(s["head_read"], 1)
            a(sig, ps[0:B, 2, 0:S * (NB + 1)].rearrange("p (t n) -> p t n", n=NB + 1)[:, :, NB], ACT.Sigmoid).then_inc(s["sigma_done"], 1)

            def tiles(q):
                return slice(G4 * q, G4 * q + G4)

            def gauss_square(q):
                act.wait_ge(s["gauss_diff"], q + 1)
                a(gauss_w[:, tiles(q), :], gauss_d[:, tiles(q), :], ACT.Square).then_inc(s["gauss_sq"], 1)

            def gauss_exponential(q):
                act.wait_ge(s["gauss_arg"], q + 1)
                a(gauss_w[:, tiles(q), :], gauss_d[:, tiles(q), :], ACT.Exp, scale=-1.0).then_inc(s["gauss_exp"], 1)

            def gauss_weight_square(q):
                act.wait_ge(s["gauss_ready"], q + 1)
                a(gauss_d[:, tiles(q), :], gauss_w[:, tiles(q), :], ACT.Square).then_inc(s["gauss_w2"], 1)

            def copy_gauss(q):
                act.wait_ge(s["gaussT_ps"], q + 1)
                a(gauss_wT[:, tiles(q), :].rearrange("p k t -> p (k t)"), ps[0:TOK, q, 0:GT], ACT.Copy).then_inc(s["gaussT_sb"], 1)

            for n in range(GROUPS + 3):
                if n < GROUPS:
                    gauss_square(n)
                if 0 <= n - 1 < GROUPS:
                    gauss_exponential(n - 1)
                if 0 <= n - 2 < GROUPS:
                    gauss_weight_square(n - 2)
                if n >= 3:
                    copy_gauss(n - 3)

            def stage_query(i, which, bank):
                need(act, "q_ps", 4 * (i + 1) + which + 1)
                need(act, "q_lo_done", 2 * (i + 1))
                a(q_stage[:, :, 4 * which:4 * which + 4, :], ps[:, bank, 0:4 * TOK].rearrange("p (h b q) -> p b h q", h=4, b=2),
                  ACT.Copy).then_inc(s["q_staged"], 1)

            def query_hi(i, k):
                need(act, "q_staged", 4 * (i + 2))
                need(act, "scored", CH * (2 * i + k + 1))
                a(q_hi[k][:].rearrange("p (h q) -> p h q", h=H), q_stage[:, k], ACT.Copy).then_inc(s["q_hi_done"], 1)

            def negate_max(i, k, which, bank):
                nk, nb = 1 - k, 2 * i + k + 1
                need(act, "spread_ps", 2 * nb + which + 1)
                need(act, "seeded", CH * (nb - 1))
                a(neg_max[nk][:, which, :], ps[:, bank, 0:HALF], ACT.Copy, scale=-1.0).then_inc(s["neg_done"], 1)

            def seed(b, k, j):
                need(act, "prob_hi_done", CH * b + j - 1)
                need(act, "neg_done", 2 * (b + 1))
                a(score_ps[j % 2], neg_max[k][0:CR], ACT.Copy).then_inc(s["seeded"], 1)

            copy_tokens(TOKEN_BANKS[1], 2, 0)
            for u in range(4):
                stage_query(-1, u, SIDE + u % 2)
            query_hi(-1, 0)
            for q in range(1, GROUPS):
                copy_tokens(TOKEN_BANKS[1], 2, q)
            query_hi(-1, 1)
            for n in range(2):
                negate_max(-1, 1, n, SIDE + (n + 1) % 2)
            act.wait_ge(s["bits_set"], 1)
            seed(0, 0, 0)
            seed(0, 0, 1)

            def take_u(i, k):
                need(act, "weighted", CH * (2 * i + k))
                if k == 1:
                    need(act, "projected", 4 * i)
                a(u_sum[:, 0:HB, 1 - k, :], usum_ps[:, 0, :].rearrange("p (h q) -> p h q", h=HB), ACT.Copy).then_inc(s["u_act"], 1)

            def period(i, k):
                b = 2 * i + k
                first = isinstance(i, int) and i == 0 and k == 0
                last = isinstance(i, int) and i == PAIRS - 1 and k == 1
                for j in range(CH):
                    c = CH * b + j
                    need(act, "scored", c + 1)
                    need(act, "prob_lo_done", c - 2)
                    need(act, "prob_added", (CH - 1) * b + (max(j - 3, 1) if j >= 3 else j - 2))
                    a(probs[j % 3], score_ps[j % 2], ACT.Exp, scale=SCALE).then_inc(s["prob_done"], 1)
                    need(act, "weighted", c - 2)
                    a(p_hi[j % 3][:], score_ps[j % 2], ACT.Exp, scale=SCALE).then_inc(s["prob_hi_done"], 1)
                    if j == 1 and not first:
                        take_u(i, k)
                    if j + 2 < CH:
                        seed(b, k, j + 2)
                    elif not last:
                        need(act, "prob_hi_done", c + 1)
                        seed(b + 1, 1 - k, j + 2 - CH)
                    if j == 2 and not (isinstance(i, int) and i == PAIRS - 1):
                        load_context(i, k)
                    for what, which, bank in slot_work(i, k, j):
                        if what == "turn":
                            turned_hi(i, k, which, bank)
                        elif what == "spread":
                            negate_max(i, k, which, bank)
                        elif what == "query":
                            stage_query(i, which, bank)
                    if j == CH - 1 and not (isinstance(i, int) and i == PAIRS - 1):
                        query_hi(i, k)

            sequence(act, period)
            take_u(PAIRS, 0)

            for q in range(GROUPS):
                copy_tokens(TOKEN_BANKS[2], 3, q)
            for q in range(GROUPS):
                need(act, "onehotT_ps", q + 1)
                a(onehotT[:, q * GT:(q + 1) * GT], ps[0:E, q, 0:GT], ACT.Copy).then_inc(s["onehotT_sb"], 1)

            def copy_experts(n):
                need(act, "hid_ps", MB * (n - 1))
                for t in range(G4):
                    need(act, "expT_ps", G4 * n + t + 1)
                    a(expertsT[n % 2][:, :, t, :], ps[:, SIDE + t % 2, 0:E * TOK].rearrange("p (e t) -> p e t", e=E),
                      ACT.Copy).then_inc(s["expT_sb"], 1)

            copy_experts(0)
            for n in range(GROUPS):
                if n + 1 < GROUPS:
                    copy_experts(n + 1)
                need(act, "y_ps", n - 1)
                for m_ in range(MB):
                    need(act, "hid_ps", MB * n + m_ + 1)
                    a(inter[n % 2][:, m_, :], ps[:, m_, 0:GT], ACT.Gelu).then_inc(s["hid_act"], 1)

        @block.vector
        def _(dve):
            v = nc.vector

            ln_steps = [0]

            def norm_step(m):
                ln_steps[0] += 1
                m.then_inc(s["ln_step"], 1)
                dve.wait_ge(s["ln_step"], ln_steps[0])

            def layer_norm(count, before=None):
                def moments(q):
                    if before:
                        before(q)
                    group = range(G4 * q, G4 * q + G4)
                    for t in group:
                        m = v.bn_stats(stats[:, t, :], resid_k[:, t, :])
                    norm_step(m)
                    for t in group:
                        m = v.bn_aggr(meanvar[:, t, :], stats[:, t, :])
                    norm_step(m)
                    v.tensor_scalar(veps[:, G4 * q:G4 * q + G4], meanvar[:, G4 * q:G4 * q + G4, 1], 1e-5, None, ALU.add).then_inc(s["ln_var"], 1)

                def scale(q):
                    dve.wait_ge(s["rstd_done"], GROUPS * (count - 1) + q + 1)
                    for t in range(G4 * q, G4 * q + G4):
                        m = v.tensor_scalar(xnorm[:, t, :], resid_k[:, t, :], meanvar[:, t, 0:1], rstd[:, t:t + 1], ALU.subtract, ALU.mult)
                    m.then_inc(s["ln_done"], 1)

                moments(0)
                for q in range(1, GROUPS):
                    moments(q)
                    scale(q - 1)
                scale(GROUPS - 1)

            dve.wait_ge(s["x_in"], 16)
            layer_norm(1)

            gauss_count = [0]

            def then(m):
                gauss_count[0] += 1
                m.then_inc(s["gauss_step"], 1)
                dve.wait_ge(s["gauss_step"], gauss_count[0])

            dve.wait_ge(s["indices_made"], 3)
            v.tensor_copy(jp1, jp1_int)
            v.tensor_copy(i_idx, idx_int)
            then(v.tensor_copy(pos[:, 0:1], p_int))
            dve.wait_ge(s["rel_made"], 2)
            then(v.tensor_tensor(pos[:, 2:3], pos[:, 0:1], pos[:, 1:2], ALU.add))
            then(v.reciprocal(pos[:, 3:4], pos[:, 2:3]))
            then(v.tensor_scalar(rel, i_idx, pos[:, 3:4], None, ALU.mult))

            dve.wait_ge(s["zeros_made"], 3)

            def turned_lo(i, k, which, bank):
                tb = 2 * (i + 1) + k
                part = slice(which * MC, (which + 1) * MC)
                need(dve, "ctxT_hi_done", MP * tb + which + 1)
                v.tensor_tensor(ctxT_lo[k][:, part], ps[:, bank, 0:MC], ctxT_hi[k][:, part].bitcast(F32), ALU.subtract).then_inc(s["ctxT_lo_done"], 1)

            def lstm_steps(it, beside=None):
                for u in range(U8):
                    t = U8 * it + u
                    need(dve, "sig_ready", t + 1)
                    need(dve, "cell_step", 3 * t)
                    v.tensor_tensor(cell_f, gate_act[:, 1, :], cell, ALU.mult).then_inc(s["cell_step"], 1)
                    need(dve, "tanhg_ready", t + 1)
                    v.tensor_tensor(cell_i, gate_act[:, 0, :], gate_act[:, 3, :], ALU.mult).then_inc(s["cell_step"], 1)
                    need(dve, "cell_step", 3 * t + 2)
                    v.tensor_tensor(cell, cell_f, cell_i, ALU.add).then_inc(s["cell_step"], 1)
                    need(dve, "tanhc_ready", t + 1)
                    v.tensor_tensor(lstm_h[0:PE, u, :], gate_act[:, 2, :], cell_t, ALU.mult).then_inc(s["h_ready"], 1)
                    if beside:
                        beside(u)

            def beside_last(u):
                if u >= 3:
                    turned_lo(-1, (u - 3) // MP, (u - 3) % MP, SIDE + (u - 1) % 2)

            lstm_steps(0)
            with dve.Fori(1, ITERS - 1) as it:
                lstm_steps(it)
            lstm_steps(ITERS - 1, beside_last)

            heads = ps[0:B, 2, 0:S * (NB + 1)].rearrange("p (t n) -> p n t", n=NB + 1)
            dve.wait_ge(s["head_ready"], 1)
            v.tensor_scalar(mu_w, heads[:, 0:NB, :], 0.0, None, ALU.max).then_inc(s["head_read"], 1)
            dve.wait_ge(s["head_read"], 1)
            then(v.scalar_tensor_tensor(mu_t, mu_w[:, 2, :], 1.0 / S, jp1, ALU.mult, ALU.mult))
            then(v.scalar_tensor_tensor(mu_b, mu_w[:, 1, :], 1.0 / S, mu_t, ALU.mult, ALU.add))
            then(v.tensor_tensor_scan(mu, mu_w[:, 0, :], mu_b, 0.0, ALU.mult, ALU.add))

            def over_b(ap):
                return ap[:, None, :].to_broadcast((B, 2, S))

            dve.wait_ge(s["sigma_done"], 1)
            dve.wait_ge(s["picks_made"], 6)
            v.tensor_tensor(mu_l, over_b(mu), pick_b, ALU.mult)
            then(v.scalar_tensor_tensor(sig2, sig, 2.0, sig, ALU.mult, ALU.mult))
            then(v.reciprocal(inv2s, sig2))
            v.tensor_tensor(inv_l, over_b(inv2s), pick_b, ALU.mult).then_inc(s["rows_picked"], 1)
            turned_lo(-1, 1, MP - 1, SIDE + 1)
            dve.wait_ge(s["pick_ps"], 1)
            v.tensor_copy(bO_b[:], ps[0:TOK, 3, 128:128 + D]).then_inc(s["picks_read"], 1)
            then(v.tensor_copy(mu_tok.rearrange("p a k -> p (a k)"), ps[0:TOK, 3, 0:2 * PAIRS]))

            def tiles(q):
                return slice(G4 * q, G4 * q + G4)

            def over_k(ap):
                return ap[:, None, :].to_broadcast((TOK, G4, TOK))

            def over_i(ap, q):
                return ap[:, tiles(q), None].to_broadcast((TOK, G4, TOK))

            def gauss_difference(q):
                v.tensor_tensor(gauss_d[:, tiles(q), :], over_k(rel), over_i(mu_tok[:, 0, :], q), ALU.subtract).then_inc(s["gauss_diff"], 1)

            def gauss_argument(q):
                dve.wait_ge(s["gauss_sq"], q + 1)
                v.tensor_tensor(gauss_d[:, tiles(q), :], gauss_w[:, tiles(q), :], over_i(mu_tok[:, 1, :], q), ALU.mult).then_inc(s["gauss_arg"], 1)

            def gauss_mask(q):
                dve.wait_ge(s["gauss_exp"], q + 1)
                v.tensor_tensor(gauss_w[:, tiles(q), :], gauss_w[:, tiles(q), :], over_k(causal), ALU.mult).then_inc(s["gauss_ready"], 1)

            def gauss_norm(q):
                dve.wait_ge(s["gauss_w2"], q + 1)
                then(v.tensor_reduce(wsum[:, tiles(q)], gauss_d[:, tiles(q), :], AX.X, ALU.add))
                v.tensor_scalar(wsum[:, tiles(q)], wsum[:, tiles(q)], 1e-24, None, ALU.max).then_inc(s["norm_in"], 1)

            dve.wait_ge(s["causal_made"], 3)
            for n in range(GROUPS + 3):
                if n < GROUPS:
                    gauss_difference(n)
                if 0 <= n - 1 < GROUPS:
                    gauss_argument(n - 1)
                if 0 <= n - 2 < GROUPS:
                    gauss_mask(n - 2)
                if n >= 3:
                    gauss_norm(n - 3)

            def add_self_attention(q):
                dve.wait_ge(s["norm_done"], q + 1)
                dve.wait_ge(s["self_attn_ps"], q + 1)
                for t in range(G4):
                    tile = G4 * q + t
                    m = v.scalar_tensor_tensor(resid_k[:, tile, :], ps[0:TOK, SELF_BANK[q], t * D:(t + 1) * D], wsum[:, tile:tile + 1],
                                               resid_k[:, tile, :], ALU.mult, ALU.add)
                m.then_inc(s["x1_done"], 1)
                dve.wait_ge(s["x1_done"], q + 1)

            layer_norm(2, add_self_attention)

            def query_lo(i, k):
                need(dve, "q_hi_done", 2 * (i + 1) + k + 1)
                v.tensor_tensor(q_lo[k][:].rearrange("p (h q) -> p h q", h=H), q_stage[:, k],
                                q_hi[k][:].bitcast(F32).rearrange("p (h q) -> p h q", h=H), ALU.subtract).then_inc(s["q_lo_done"], 1)

            def read_max(i, k, which, bank):
                nb = 2 * i + k + 1
                need(dve, "max_ps", RB * MP * nb + which + 1)
                if which == 0:
                    need(dve, "max_found", nb)
                v.tensor_reduce(max_parts[:, which:which + 1], ps[:, bank, 0:MC], AX.X, ALU.max).then_inc(s["max_read"], 1)
                if which == RB * MP - 1:
                    need(dve, "max_read", RB * MP * (nb + 1))
                    need(dve, "diag_done", nb)
                    v.tensor_reduce(max_all[:], max_parts[:].rearrange("p (r m) -> p r m", m=MP), AX.X, ALU.max).then_inc(s["max_found"], 1)
                    need(dve, "max_found", nb + 1)
                    need(dve, "spread_ps", 2 * nb)
                    v.tensor_tensor(max_diag[:].rearrange("p (r c) -> p r c", r=RB), ident[:, None, :].to_broadcast((128, RB, 128)),
                                    max_all[:, :, None].to_broadcast((128, RB, 128)), ALU.mult).then_inc(s["diag_done"], 1)

            def take_u(i, k):
                need(dve, "weighted", CH * (2 * i + k))
                if k == 1:
                    need(dve, "projected", 4 * i)
                v.tensor_copy(u_sum[:, HB:H, 1 - k, :], usum_ps[:, 1, :].rearrange("p (h q) -> p h q", h=HB)).then_inc(s["u_dve"], 1)

            def invert_sums(pair, bank):
                need(dve, "sums_ps", pair + 1)
                v.reciprocal(sum_recip[:], ps[0:TOK, bank, 0:H]).then_inc(s["recip_done"], 1)

            def add_heads(pair, which, bank):
                tile = resid[:, bass.ds(pair * D, D)]
                need(dve, "projected", 4 * pair + which + 1)
                if which == 0:
                    need(dve, "recip_done", pair + 1)
                for n in range(4):
                    h = 4 * which + n
                    product, scale = ps[0:TOK, bank, n * D:(n + 1) * D], sum_recip[:, h:h + 1]
                    if h >= 2:
                        need(dve, "head_added", H * pair + h - 1)
                    if h == 1:
                        m = v.tensor_scalar(odd_heads[:], product, scale, None, ALU.mult)
                    elif h % 2:
                        m = v.scalar_tensor_tensor(odd_heads[:], product, scale, odd_heads[:], ALU.mult, ALU.add)
                    else:
                        m = v.scalar_tensor_tensor(tile, product, scale, tile, ALU.mult, ALU.add)
                    m.then_inc(s["head_added"], 1)
                if which == 3:
                    need(dve, "head_added", H * (pair + 1))
                    v.tensor_tensor(tile, tile, odd_heads[:], ALU.add).then_inc(s["x2_done"], 1)

            query_lo(-1, 0)
            for n in range(RB * MP):
                read_max(-1, 1, n, SIDE + n % 2)
            query_lo(-1, 1)
            need(dve, "bO_added", 1)

            def period(i, k):
                b = 2 * i + k
                first = isinstance(i, int) and i == 0 and k == 0
                last = isinstance(i, int) and i == PAIRS - 1 and k == 1
                for j in range(CH):
                    c = CH * b + j
                    if j == 1 and not first:
                        take_u(i, k)
                    need(dve, "prob_hi_done", c + 1)
                    need(dve, "weighted", c - 2)
                    v.tensor_tensor(p_lo[j % 3][:], probs[j % 3], p_hi[j % 3][:].bitcast(F32), ALU.subtract).then_inc(s["prob_lo_done"], 1)
                    for what, which, bank in slot_work(i, k, j):
                        if what == "turn":
                            turned_lo(i, k, which, bank)
                        elif what == "max":
                            read_max(i, k, which, bank)
                        elif what == "sums":
                            invert_sums(i - 1, bank)
                        elif what == "project":
                            add_heads(i - 1, which, bank)
                    if j == CH - 1 and not (isinstance(i, int) and i == PAIRS - 1):
                        query_lo(i, k)

            sequence(dve, period)
            take_u(PAIRS, 0)
            invert_sums(PAIRS - 1, SIDE)
            for n in range(4):
                add_heads(PAIRS - 1, n, SIDE + (n + 1) % 2)

            need(dve, "x2_done", PAIRS)
            dve.wait_ge(s["rows_ps"], 1)
            v.tensor_copy(rows_b.rearrange("p n d -> p (n d)"), ps[0:TOK, 5, 0:3 * D]).then_inc(s["rows_copied"], 1)
            layer_norm(3)
            route_count = [0]

            def route(m):
                route_count[0] += 1
                m.then_inc(s["onehot_step"], 1)
                dve.wait_ge(s["onehot_step"], route_count[0])

            dve.wait_ge(s["logit_ps"], 1)
            route(v.tensor_copy(logits.rearrange("p k e -> p (k e)"), ps[0:TOK, 4, 0:PAIRS * E]))
            route(v.tensor_reduce(best, logits, AX.X, ALU.max))
            route(v.tensor_tensor(is_best, logits, best[:, :, None].to_broadcast((TOK, PAIRS, E)), ALU.is_equal))
            route(v.tensor_copy(seen, is_best[:, :, 0]))
            route(v.tensor_copy(onehot_k[:, :, 0], is_best[:, :, 0]))
            for e in range(1, E):
                route(v.scalar_tensor_tensor(onehot_k[:, :, e], seen, 0.5, is_best[:, :, e], ALU.is_lt, ALU.mult))
                if e + 1 < E:
                    route(v.tensor_tensor(seen, seen, is_best[:, :, e], ALU.max))
            assert route_count[0] == ONEHOT_STEPS

            def mask_experts(n):
                for t in range(G4):
                    tile = G4 * n + t
                    need(dve, "expT_ps", tile - 1)
                    v.tensor_tensor(experts_in[:, t % 2], xnorm[:, tile, None, :].to_broadcast((TOK, E, D)),
                                    onehot_k[:, tile, :, None].to_broadcast((TOK, E, D)), ALU.mult).then_inc(s["masked"], 1)

            y_count = [0]

            def step(m):
                y_count[0] += 1
                m.then_inc(s["y_step"], 1)
                dve.wait_ge(s["y_step"], y_count[0])

            def over_t(n):
                return rows_b[:, n, None, :].to_broadcast((TOK, G4, D))

            dve.wait_ge(s["rows_copied"], 1)
            mask_experts(0)
            for n in range(GROUPS):
                if n + 1 < GROUPS:
                    mask_experts(n + 1)
                tiles = slice(G4 * n, G4 * n + G4)
                y, o = y_sb[:, n % 2], o_sb[:, n % 2]
                need(dve, "y_ps", n + 1)
                v.tensor_tensor(y, ps[0:TOK, 4 + n % 2, :].rearrange("p (k d) -> p k d", k=G4), xnorm[:, tiles, :], ALU.add).then_inc(s["y_added"], 1)
                dve.wait_ge(s["y_added"], n + 1)
                step(v.tensor_tensor(y, y, over_t(0), ALU.add))
                for t in range(G4):
                    m = v.bn_stats(stats[:, t, :], y[:, t, :])
                step(m)
                for t in range(G4):
                    m = v.bn_aggr(meanvar[:, t, :], stats[:, t, :])
                step(m)
                v.tensor_scalar(veps[:, tiles], meanvar[:, 0:G4, 1], 1e-12, None, ALU.add).then_inc(s["y_var"], 1)
                dve.wait_ge(s["y_pow"], n + 1)
                for t in range(G4):
                    m = v.tensor_scalar(y[:, t, :], y[:, t, :], meanvar[:, t, 0:1], rstd[:, G4 * n + t:G4 * n + t + 1], ALU.subtract, ALU.mult)
                step(m)
                step(v.tensor_tensor(y, y, over_t(1), ALU.mult))
                step(v.tensor_tensor(y, y, over_t(2), ALU.add))
                need(dve, f"out_stored{n % 2}", 16 * (n // 2))
                v.tensor_tensor(o, y, resid_k[:, tiles, :], ALU.add).then_inc(s["out_made"], 1)


_INS = ["x", "ctx_1024", "L0_attn_W_ih", "L0_attn_W_hh", "L0_attn_b_ih", "L0_attn_b_hh", "L0_attn_W_mu", "L0_attn_b_mu",
        "L0_attn_W_sig", "L0_attn_b_sig", "L0_xattn_WQ", "L0_xattn_WK", "L0_xattn_WV", "L0_xattn_WO", "L0_xattn_bO",
        "L0_ffn_W_router", "L0_ffn_W1", "L0_ffn_b1", "L0_ffn_Wo", "L0_ffn_bo", "L0_ffn_ln_gamma", "L0_ffn_ln_beta"]


def kernel(**inputs):
    import numpy as _np
    import concourse.bacc as _bacc
    from concourse import mybir as _mybir
    from concourse.bass_utils import run_bass_kernel_spmd as _run

    nc = _bacc.Bacc("TRN2", target_bir_lowering=False, num_devices=1)
    arrays, args = {}, []
    for name in _INS:
        a = _np.ascontiguousarray(inputs[name])
        arrays[f"in_{name}_dram"] = a
        args.append(nc.dram_tensor(f"in_{name}_dram", a.shape, _mybir.dt.from_np(a.dtype), kind="ExternalInput").ap())
    out = nc.dram_tensor("out_0_dram", inputs["x"].shape, _mybir.dt.float32, kind="ExternalOutput").ap()
    decoder_layer(nc, *args, out)
    r = _run(nc, [arrays], core_ids=[0])
    return r.results[0]["out_0_dram"]
```

```python
from contextlib import ExitStack

import concourse.bass as bass
from concourse import mybir

F32 = mybir.dt.float32
F32R = mybir.dt.float32r
I32 = mybir.dt.int32
ALU = mybir.AluOpType
ACT = mybir.ActivationFunctionType
AX = mybir.AxisListType


def decoder_layer(nc, x, ctx_1024, W_ih, W_hh, b_ih, b_hh, W_mu, b_mu, W_sig, b_sig,
                  WQ, WK, WV, WO, bO, W_router, W1, b1, Wo, bo, ln_gamma, ln_beta, out):
    B, S, D = x.shape
    L = ctx_1024.shape[1]
    PE = W_hh.shape[1]
    NB = W_mu.shape[0]
    E, _, FF = W1.shape
    DK = 64
    H = WQ.shape[1] // DK
    TOK = 2 * S
    PAIRS = B // 2
    CH = 12
    CR = L // CH
    HQ = H * S
    HALF = HQ // 2
    HB = H // 2
    RB = HQ // 128
    MP = 3
    MC = L // MP
    TG = CH // MP
    SCALE = 1.0 / DK ** 0.5
    G4 = 4
    MB = FF // 128
    GROUPS = PAIRS // G4
    GT = G4 * TOK
    U8 = 2 * G4
    ITERS = S // U8
    assert CR * CH == L and RB * 128 == HQ and PAIRS % G4 == 0 and S % U8 == 0

    with ExitStack() as stack:
        def sb(name, shape, dt=F32):
            return stack.enter_context(nc.sbuf_tensor(name, shape, dt))

        ps = stack.enter_context(nc.psum_tensor("ps", [128, 8, 512], F32))
        score_ps = [ps[0:CR, 2 * n:2 * n + 2, 0:HALF] for n in range(2)]
        usum_ps = ps[:, 4:6, 0:HALF]
        SIDE = 6

        resid = sb("resid", [TOK, PAIRS * D])
        resid_k = resid[:].rearrange("p (k d) -> p k d", k=PAIRS)
        xnorm = sb("xnorm", [TOK, PAIRS, D])
        xT = sb("xT", [D, PAIRS, TOK])
        ident = sb("ident", [128, 128])
        ones = sb("ones", [128, 128])
        ones_r = sb("ones_r", [128, 128], F32R)
        qk_w = sb("qk_w", [D, H, D])
        vo_w = sb("vo_w", [D, H, D])
        bO_row = sb("bO_row", [1, D])
        w1_sb = sb("w1_sb", [D, E, FF])
        b1_sb = sb("b1_sb", [E, FF])
        wo_sb = sb("wo_sb", [128, MB, D])
        rows_sb = sb("rows_sb", [1, 2, D])
        bo_sb = sb("bo_sb", [D, 1])
        pick_e = sb("pick_e", [E, E, 128], F32R)
        wr_sb = sb("wr_sb", [D, E])
        stats = sb("stats", [TOK, PAIRS, 6])
        meanvar = sb("meanvar", [TOK, PAIRS, 2])
        veps = sb("veps", [TOK, PAIRS])
        rstd = sb("rstd", [TOK, PAIRS])
        minus_half = sb("minus_half", [TOK, PAIRS])

        ctx_raw = [sb(f"ctx_raw{n}", [128, CH * D]) for n in range(2)]
        ctx_in = [r[0:CR, :].rearrange("p (c d) -> p c d", c=CH) for r in ctx_raw]
        ctx_hi = [sb(f"ctx_hi{n}", [CR, CH, D], F32R) for n in range(2)]
        ctx_lo = [sb(f"ctx_lo{n}", [CR, CH, D], F32R) for n in range(2)]
        ctxT_hi = [sb(f"ctxT_hi{n}", [D, L], F32R) for n in range(2)]
        ctxT_lo = [sb(f"ctxT_lo{n}", [D, L], F32R) for n in range(2)]
        q_hi = [sb(f"q_hi{n}", [D, HQ], F32R) for n in range(2)]
        q_lo = [sb(f"q_lo{n}", [D, HQ], F32R) for n in range(2)]
        p_hi = [sb(f"p_hi{n}", [CR, 2, HALF], F32R) for n in range(3)]
        p_lo = [sb(f"p_lo{n}", [CR, 2, HALF], F32R) for n in range(3)]
        max_diag = sb("max_diag", [128, HQ], F32R)
        max_parts = sb("max_parts", [128, RB * MP])
        max_all = sb("max_all", [128, RB])
        sum_recip = sb("sum_recip", [TOK, H])
        odd_heads = sb("odd_heads", [TOK, D])
        bO_b = sb("bO_b", [TOK, D])
        wo_raw = sb("wo_raw", [128, H // 2, D])

        ARENA = 12 * HQ
        arena = sb("arena", [128, ARENA])
        at = [0]

        def cut(size, parts=128):
            at[0] += size
            assert at[0] <= ARENA
            return arena[0:parts, at[0] - size:at[0]]

        neg_max = [cut(HQ).rearrange("p (a b) -> p a b", a=2) for n in range(2)]
        probs = [cut(HQ, CR).rearrange("p (a b) -> p a b", a=2) for n in range(3)]
        prob_sum = cut(2 * HQ, CR).rearrange("p (h b q) -> p h b q", h=H, b=2)
        u_sum = cut(2 * HQ).rearrange("p (h b q) -> p h b q", h=H, b=2)
        q_stage = cut(2 * HQ).rearrange("p (b h q) -> p b h q", b=2, h=H)
        first_sum = q_stage[0:CR, 0]

        at[0] = 0
        W = PAIRS * TOK
        gauss_d = cut(W, TOK).rearrange("p (k i) -> p k i", k=PAIRS)
        gauss_w = cut(W, TOK).rearrange("p (k i) -> p k i", k=PAIRS)
        gauss_wT = cut(W, TOK).rearrange("p (k j) -> p k j", k=PAIRS)
        lstm_h = cut(U8 * B).rearrange("p (u b) -> p u b", u=U8)
        w_in = cut(D)
        w_hh_in = cut(PE)
        w_head_in = cut(PE)
        wihT = cut(4 * PE)
        whhT = cut(4 * PE)
        headT = cut(NB + 1)
        gate_act = cut(4 * B, PE).rearrange("p (g b) -> p g b", g=4)
        cell = cut(B, PE)
        cell_f = cut(B, PE)
        cell_i = cut(B, PE)
        cell_t = cut(B, PE)
        mu_w = cut(NB * S, B).rearrange("p (n t) -> p n t", n=NB)
        mu_t = cut(S, B)
        mu_b = cut(S, B)
        mu = cut(S, B)
        sig = cut(S, B)
        sig2 = cut(S, B)
        inv2s = cut(S, B)
        jp1 = cut(S, B)
        pick_b = cut(TOK, B).rearrange("p (b j) -> p b j", b=2)
        pick_k = cut(PAIRS, B)
        mu_l = cut(TOK, B).rearrange("p (b j) -> p b j", b=2)
        inv_l = cut(TOK, B).rearrange("p (b j) -> p b j", b=2)
        mu_tok = cut(2 * PAIRS, TOK).rearrange("p (a k) -> p a k", a=2)
        rel = cut(TOK, TOK)
        causal = cut(TOK, TOK)
        i_idx = cut(TOK, TOK)
        pos = cut(4, TOK)
        wsum = cut(PAIRS, TOK)
        pick_e_in = cut(E * 128, E).rearrange("p (e c) -> p e c", e=E)
        jp1_int = cut(S, B).bitcast(I32)
        idx_int = cut(TOK, TOK).bitcast(I32)
        p_int = cut(1, TOK).bitcast(I32)

        wq_raw = ctx_raw[1][:, 0:H * DK]
        wk_raw = w1_sb[:].rearrange("p e f -> p (e f)")[:, 0:H * DK]
        wv_raw = w1_sb[:].rearrange("p e f -> p (e f)")[:, H * DK:2 * H * DK]
        wT_sb = sb("wT_sb", [128, 2, 3, D])

        at[0] = 0
        inter = [cut(MB * GT).rearrange("p (m t) -> p m t", m=MB) for n in range(2)]
        at[0] = 9 * HQ
        yT_sb = [cut(GT) for n in range(2)]
        at[0] = 11 * HQ
        seen = cut(PAIRS, TOK)
        best = cut(PAIRS, TOK)
        logits = cut(PAIRS * E, TOK).rearrange("p (k e) -> p k e", e=E)
        is_best = cut(PAIRS * E, TOK).rearrange("p (k e) -> p k e", e=E)
        onehot = cut(PAIRS * E, TOK)
        onehot_k = onehot.rearrange("p (k e) -> p k e", e=E)
        rows_b = cut(2 * D, TOK).rearrange("p (n d) -> p n d", n=2)
        y_sb = ctx_raw[0][0:TOK, 0:2 * G4 * D].rearrange("p (n k d) -> p n k d", n=2, k=G4)
        o_sb = ctx_raw[1][0:TOK, 0:2 * G4 * D].rearrange("p (n k d) -> p n k d", n=2, k=G4)
        w1_hi = [ctxT_hi[e // 2][:, e % 2 * FF:(e % 2 + 1) * FF] for e in range(E)]
        w1_lo = [ctxT_lo[e // 2][:, e % 2 * FF:(e % 2 + 1) * FF] for e in range(E)]
        b1_r = ctx_hi[0][0:E, 0:8, :].rearrange("p c d -> p (c d)").rearrange("p (n f) -> p n f", n=2)
        onehotT = [ctx_lo[0][0:E, :, :].rearrange("p c d -> p (c d)")[:, q * GT:(q + 1) * GT] for q in range(GROUPS - 1)] + [
            ctx_hi[0][0:E, 8:CH, :].rearrange("p c d -> p (c d)")[:, 0:GT]]
        xT_halves = max_diag[:].rearrange("p (n t) -> p n t", n=2)
        expert_x = [t[:].rearrange("p (n t) -> p n t", n=2) for t in (*q_hi, *q_lo)]

        s = {name: stack.enter_context(nc.semaphore("s_" + name)) for name in (
            "x_in lstm_w_in bias_in attn_w_in ffn_w_in ctx_in0 ctx_in1 out_stored0 out_stored1 "
            "identity_made ones_made minus_made indices_made rel_made causal_made picks_made zeros_made "
            "biased_cleared table_loaded lstm_w_ps lstm_w_sb "
            "ln_step ln_var rstd_done ln_done xT_ps xT_sb ones_r_made "
            "gates_ready sig_ready tanhg_ready cell_step tanhc_ready h_ready head_ready head_read "
            "sigma_done pick_ps picks_read gauss_step rows_picked gauss_diff gauss_sq gauss_arg gauss_exp gauss_ready gauss_w2 "
            "norm_in norm_done gaussT_ps gaussT_sb self_attn_ps x1_done bO_added "
            "turned_w turned_w_sb folded folded_sb bits_set "
            "ctx_hi_done ctx_lo_done ctxT_ps ctxT_hi_done ctxT_lo_done q_ps q_staged q_hi_done q_lo_done "
            "max_ps max_read max_found diag_done spread_ps neg_done seeded scored prob_done prob_hi_done prob_hi_dve "
            "prob_lo_done prob_added weighted u_act u_dve sums_ps recip_done projected head_added x2_done "
            "pick_e_made pick_e_sb rows_ps rows_copied logit_ps logits_read onehot_step onehot_made onehotT_ps onehotT_sb "
            "w1_hi_done w1_lo_done b1_hi_done b1_lo_done xT_hi_done xT_lo_done mask_ps masked expert_used hid_ps hid_act "
            "yT_ps yT_sb y_ps y_step y_var y_pow beta_added out_made"
        ).split()}

        def need(eng, name, value):
            if not isinstance(value, int) or value > 0:
                eng.wait_ge(s[name], value)

        PLACES = ("m..m mssm ssmm mmpm .mpm mmpm mmpm mqmm mqqt ..dd qt.. t...",
                  "m..m mm.m mm.m mm.m m.m. m.m. m.mt m.m. m.mt ..dd .... .t..")
        LAST_POWERS = (1, 2, 4)
        LAST_PLACES = ".... .... .x.. .x.. .... .x.l .l.. .l.. .... .o.o o... ..kk"
        PIECES = {"k": "mask", "x": "tokens", "l": "logits", "o": "onehot", "m": "max", "d": "spread", "t": "turn", "s": "sums", "p": "project", "q": "query"}
        DVE_HI = (9, 10, 11)

        def hi_count(b, j):
            return (CH - len(DVE_HI)) * b + sum(n not in DVE_HI for n in range(j + 1))

        CP = 6
        PART_SLOTS = (1, 3, 5, 6, 8, 9)
        PC = CH // CP

        def mask_bank(e):
            pieces = sum(letter != "." for letter in LAST_PLACES.split("k")[0] if letter != " ")
            return SIDE + (pieces + e) % 2

        def side_work(i, k):
            first = isinstance(i, int) and i == 0
            last = isinstance(i, int) and i == PAIRS - 1
            skipped = ""
            words = LAST_PLACES if last and k == 1 else PLACES[k]
            if last:
                skipped += "tq"
            if first:
                skipped += "sp"
            rows, count = [], dict.fromkeys(PIECES, 0)
            for slot, word in enumerate(words.split()):
                for place, letter in enumerate(word):
                    if letter != "." and letter not in skipped:
                        rows.append(((slot, place), PIECES[letter], count[letter], SIDE + len(rows) % 2))
                        count[letter] += 1
            return rows

        def bank_read(what, which, i, k):
            nb = 2 * i + k + 1
            return {"turn": ("ctxT_lo_done", MP * (nb + 1) + which + 1), "max": ("max_read", RB * MP * nb + which + 1),
                    "spread": ("neg_done", 2 * nb + which + 1), "sums": ("recip_done", 4 * (i - 1) + which + 1),
                    "project": ("head_added", H * (i - 1) + 4 * (which + 1)), "query": ("q_staged", 4 * (i + 1) + which + 1),
                    "tokens": ("xT_sb", 2 * GROUPS + which + 1), "logits": ("logits_read", which + 1),
                    "onehot": ("onehotT_sb", which + 1), "mask": ("masked", which + 1)}[what]

        def side_banks(i, k):
            if isinstance(i, int) and i == 0 and k == 0:
                before = {SIDE + 1: ("neg_done", 1), SIDE: ("neg_done", 2)}
            else:
                pi, pk = (i, 0) if k else (i - 1, 1)
                before = {bank: bank_read(what, which, pi, pk) for _, what, which, bank in side_work(pi, pk)}
            rows = []
            for place, what, which, bank in side_work(i, k):
                rows.append((place, what, which, bank, before[bank]))
                before[bank] = bank_read(what, which, i, k)
            return rows

        def slot_work(i, k, j, places=range(4)):
            return [(what, which, bank) for (slot, place), what, which, bank in side_work(i, k) if slot == j and place in places]

        def sequence(eng, period):
            for k in range(2):
                period(0, k)
            with eng.Fori(1, PAIRS - 1) as i:
                for k in range(2):
                    period(i, k)
            for k in range(2):
                period(PAIRS - 1, k)

        Y_STEPS, Y_READ = 4, 3
        YT_BANK, Y_BANK = 4, 5
        WARM = 256
        FOLD_BANK = 4
        SELF_BANK = (4, 5, 0, 1)
        TOKEN_BANKS = ((4, 5, 6, 7), (2, 3, 4, 5), (0, 1, 2, 3))

        block = stack.enter_context(nc.Block())

        @block.sync
        def _(sp):
            sp.dma_start(resid_k, x.rearrange("b s d -> (b s) d").rearrange("(k p) d -> p k d", p=TOK)).then_inc(s["x_in"], 16)
            sp.dma_start(w_in[0:4 * PE, :], W_ih).then_inc(s["lstm_w_in"], 16)
            sp.dma_start(w_hh_in[0:4 * PE, :], W_hh).then_inc(s["lstm_w_in"], 16)
            sp.dma_start(w_head_in[0:NB, :], W_mu).then_inc(s["lstm_w_in"], 16)
            sp.dma_start(w_head_in[NB:NB + 1, :], W_sig).then_inc(s["lstm_w_in"], 16)
            need(sp, "biased_cleared", 2)
            sp.dma_start(headT[PE:PE + 1, 0:NB], b_mu.rearrange("(a n) -> a n", a=1)).then_inc(s["bias_in"], 16)
            sp.dma_start(headT[PE:PE + 1, NB:NB + 1], b_sig.rearrange("(a n) -> a n", a=1)).then_inc(s["bias_in"], 16)
            sp.dma_start(whhT[PE:PE + 1, :], b_ih.rearrange("(a n) -> a n", a=1)).then_inc(s["bias_in"], 16)
            sp.dma_start(whhT[PE + 1:PE + 2, :], b_hh.rearrange("(a n) -> a n", a=1)).then_inc(s["bias_in"], 16)
            sp.dma_start(wq_raw, WQ).then_inc(s["attn_w_in"], 16)
            sp.dma_start(wk_raw, WK).then_inc(s["attn_w_in"], 16)
            sp.dma_start(wv_raw, WV).then_inc(s["attn_w_in"], 16)
            sp.dma_start(wo_raw[:], WO.rearrange("(c p) n -> p c n", p=128)).then_inc(s["attn_w_in"], 16)
            sp.dma_start(bO_row[:], bO.rearrange("(a n) -> a n", a=1)).then_inc(s["attn_w_in"], 16)
            sp.dma_start(ctx_in[0], ctx_1024[0].rearrange("(p c) d -> p c d", p=CR)).then_inc(s["ctx_in0"], 16)
            sp.dma_start(b1_sb[:], b1).then_inc(s["ffn_w_in"], 16)
            sp.dma_start(wo_sb[:], Wo.rearrange("(m p) n -> p m n", p=128)).then_inc(s["ffn_w_in"], 16)
            sp.dma_start(wr_sb[:], W_router).then_inc(s["ffn_w_in"], 16)
            for n, row in enumerate((ln_gamma, ln_beta)):
                sp.dma_start(rows_sb[:, n, :], row.rearrange("(a n) -> a n", a=1)).then_inc(s["ffn_w_in"], 16)
            sp.dma_start(bo_sb[:], bo.rearrange("(d a) -> d a", a=1)).then_inc(s["ffn_w_in"], 16)
            need(sp, "turned_w", H // 2)
            sp.dma_start(ctx_in[1], ctx_1024[1].rearrange("(p c) d -> p c d", p=CR)).then_inc(s["ctx_in1"], 16)
            sp.dma_start(w1_sb[:], W1.rearrange("e h i -> h e i")).then_inc(s["ffn_w_in"], 16)
            out_k = out.rearrange("b s d -> (b s) d").rearrange("(k p) d -> p k d", p=TOK)
            for g in range(GROUPS):
                need(sp, "out_made", g + 1)
                sp.dma_start(out_k[:, G4 * g:G4 * g + G4, :], o_sb[:, g % 2]).then_inc(s[f"out_stored{g % 2}"], 16)
            for n in range(2):
                sp.wait_ge(s[f"out_stored{n}"], 16 * (GROUPS // 2))

        @block.gpsimd
        def _(pool):
            g = nc.gpsimd
            g.memset(headT, 0.0).then_inc(s["biased_cleared"], 1)
            g.memset(whhT, 0.0).then_inc(s["biased_cleared"], 1)
            g.memset(lstm_h, 1.0).then_inc(s["zeros_made"], 1)
            g.memset(cell, 0.0).then_inc(s["zeros_made"], 1)
            pool.wait_ge(s["zeros_made"], 1)
            g.memset(lstm_h[0:PE, U8 - 1, :], 0.0).then_inc(s["zeros_made"], 1)
            g.memset(ident[:], 0.0).then_inc(s["identity_made"], 1)
            pool.wait_ge(s["identity_made"], 1)
            g.affine_select(out=ident[:], in_=ident[:], compare_op=ALU.not_equal, fill=1.0, base=0,
                            pattern=[[-1, 128]], channel_multiplier=1).then_inc(s["identity_made"], 1)
            g.memset(ones[:], 1.0).then_inc(s["ones_made"], 1)
            g.memset(minus_half[:], -0.5).then_inc(s["minus_made"], 1)

            def power(count, q):
                tiles = slice(G4 * q, G4 * q + G4)
                pool.wait_ge(s["ln_var"], GROUPS * (count - 1) + q + 1)
                g.tensor_tensor(rstd[:, tiles], veps[:, tiles], minus_half[:, tiles], ALU.pow).then_inc(s["rstd_done"], 1)

            pool.wait_ge(s["minus_made"], 1)
            for q in range(GROUPS):
                power(1, q)
            g.iota(jp1_int, [[1, S]], base=1, channel_multiplier=0).then_inc(s["indices_made"], 1)
            g.iota(idx_int.rearrange("p (b i) -> p b i", b=2), [[0, 2], [1, S]], base=0, channel_multiplier=0).then_inc(s["indices_made"], 1)
            g.iota(p_int, [[0, 1]], base=1, channel_multiplier=1).then_inc(s["indices_made"], 1)
            g.memset(pos[:, 1:2], -float(S)).then_inc(s["rel_made"], 1)
            pool.wait_ge(s["rel_made"], 1)
            g.affine_select(out=pos[:, 1:2], in_=pos[:, 1:2], compare_op=ALU.is_ge, fill=0.0, base=-S,
                            pattern=[[0, 1]], channel_multiplier=1).then_inc(s["rel_made"], 1)
            causal_v = causal.rearrange("p (b i) -> p b i", b=2)
            g.memset(causal, 1.0).then_inc(s["causal_made"], 1)
            pool.wait_ge(s["causal_made"], 1)
            g.affine_select(out=causal_v, in_=causal_v, compare_op=ALU.is_ge, fill=0.0, base=0,
                            pattern=[[-S, 2], [-1, S]], channel_multiplier=1).then_inc(s["causal_made"], 1)
            pool.wait_ge(s["causal_made"], 2)
            g.affine_select(out=causal_v, in_=causal_v, compare_op=ALU.is_ge, fill=0.0, base=S - 1,
                            pattern=[[S, 2], [0, S]], channel_multiplier=-1).then_inc(s["causal_made"], 1)
            g.memset(pick_b, 1.0).then_inc(s["picks_made"], 1)
            g.memset(pick_k, 0.0).then_inc(s["picks_made"], 1)
            pool.wait_ge(s["picks_made"], 2)
            g.affine_select(out=pick_b, in_=pick_b, compare_op=ALU.is_ge, fill=0.0, base=0,
                            pattern=[[-PAIRS, 2], [0, S]], channel_multiplier=1).then_inc(s["picks_made"], 1)
            g.affine_select(out=pick_k, in_=pick_k, compare_op=ALU.not_equal, fill=1.0, base=0,
                            pattern=[[-1, PAIRS]], channel_multiplier=1).then_inc(s["picks_made"], 1)
            pool.wait_ge(s["picks_made"], 4)
            g.affine_select(out=pick_b, in_=pick_b, compare_op=ALU.is_ge, fill=0.0, base=PAIRS - 1,
                            pattern=[[PAIRS, 2], [0, S]], channel_multiplier=-1).then_inc(s["picks_made"], 1)
            g.affine_select(out=pick_k, in_=pick_k, compare_op=ALU.not_equal, fill=1.0, base=-PAIRS,
                            pattern=[[-1, PAIRS]], channel_multiplier=1).then_inc(s["picks_made"], 1)

            g.memset(pick_e_in, 0.0).then_inc(s["pick_e_made"], 1)
            pool.wait_ge(s["pick_e_made"], 1)
            g.affine_select(out=pick_e_in, in_=pick_e_in, compare_op=ALU.not_equal, fill=1.0, base=0,
                            pattern=[[-1, E], [0, 128]], channel_multiplier=1).then_inc(s["pick_e_made"], 1)

            def context_halves(i, k, part):
                nb, chunks = 2 * i + k, slice(PC * part, PC * part + PC)
                need(pool, f"ctx_in{k}", 16 * (i + 1))
                need(pool, "weighted", CH * (nb - 1))
                g.tensor_tensor(ctx_hi[k][:, chunks, :], ctx_in[k][:, chunks, :], ones[0:CR, None, :].to_broadcast((CR, PC, D)), ALU.mult).then_inc(s["ctx_hi_done"], 1)
                need(pool, "ctx_hi_done", CP * nb + part + 1)
                g.tensor_tensor(ctx_lo[k][:, chunks, :], ctx_in[k][:, chunks, :], ctx_hi[k][:, chunks, :].bitcast(F32),
                                ALU.subtract).then_inc(s["ctx_lo_done"], 1)

            for part in range(CP):
                context_halves(0, 0, part)
            for q in range(GROUPS):
                tiles = slice(G4 * q, G4 * q + G4)
                pool.wait_ge(s["norm_in"], q + 1)
                g.tensor_tensor(wsum[:, tiles], wsum[:, tiles], minus_half[:, tiles], ALU.pow).then_inc(s["norm_done"], 1)
            for q in range(GROUPS):
                power(2, q)
            need(pool, "ln_done", 2 * GROUPS)
            g.tensor_tensor(resid_k, resid_k, bO_b[:, None, :].to_broadcast((TOK, PAIRS, D)), ALU.add).then_inc(s["bO_added"], 1)

            def expert_halves(e):
                need(pool, "scored", CH * (B - 1 + e // 2))
                g.tensor_tensor(w1_hi[e], w1_sb[:, e, :], ones[:, None, :].to_broadcast((128, MB, 128)), ALU.mult).then_inc(s["w1_hi_done"], 1)
                need(pool, "w1_hi_done", e + 1)
                g.tensor_tensor(w1_lo[e], w1_sb[:, e, :], w1_hi[e].bitcast(F32), ALU.subtract).then_inc(s["w1_lo_done"], 1)

            def period(i, k):
                b = 2 * i + k
                for j in range(1, CH):
                    need(pool, "prob_done", CH * b + j + 1)
                    summed = prob_sum[:, :, k, :]
                    chunk = [probs[n].rearrange("p a (h q) -> p (a h) q", h=HB) for n in range(3)]
                    if j == 1:
                        if k == 0:
                            need(pool, "q_lo_done", 2 * i + 1)
                        g.tensor_tensor(first_sum if k == 0 else summed, chunk[0], chunk[1], ALU.add).then_inc(s["prob_added"], 1)
                    else:
                        need(pool, "prob_added", (CH - 1) * b + j - 1)
                        if j == 2 and k == 0:
                            need(pool, "sums_ps", 4 * i)
                        g.tensor_tensor(summed, first_sum if j == 2 and k == 0 else summed, chunk[j % 3], ALU.add).then_inc(s["prob_added"], 1)
                    if j in PART_SLOTS and not (isinstance(i, int) and i == PAIRS - 1 and k == 1):
                        context_halves(i + k, 1 - k, PART_SLOTS.index(j))
                    if isinstance(i, int) and i == PAIRS - 1 and k == 1:
                        if j in LAST_POWERS:
                            power(3, LAST_POWERS.index(j))
                        elif j == 7:
                            pool.wait_ge(s["ffn_w_in"], 16 * 7)
                            expert_halves(0)
                        elif j == 9:
                            expert_halves(1)

            sequence(pool, period)

            expert_halves(2)
            expert_halves(3)
            power(3, GROUPS - 1)
            pool.wait_ge(s["rows_copied"], 1)
            pool.wait_ge(s["ln_done"], 3 * GROUPS)
            for n in range(GROUPS):
                tiles = resid_k[:, G4 * n:G4 * n + G4, :]
                g.tensor_tensor(tiles, tiles, rows_b[:, 1, None, :].to_broadcast((TOK, G4, D)), ALU.add).then_inc(s["beta_added"], 1)
            for n in range(GROUPS):
                tiles = slice(G4 * n, G4 * n + G4)
                pool.wait_ge(s["y_var"], n + 1)
                g.tensor_tensor(rstd[:, tiles], veps[:, tiles], minus_half[:, 0:G4], ALU.pow).then_inc(s["y_pow"], 1)

        @block.tensor
        def _(pe):
            mm, tr = nc.tensor.matmul, nc.tensor.transpose

            pe.wait_ge(s["identity_made"], 2)
            pe.wait_ge(s["lstm_w_in"], 64)
            tr(ps[:, 3, 0:4 * PE], w_in[0:4 * PE, :], ident[0:4 * PE, 0:4 * PE])
            tr(ps[0:PE, 3, 128:128 + 4 * PE], w_hh_in[0:4 * PE, :], ident[0:4 * PE, 0:4 * PE])
            tr(ps[0:PE, 3, 256:256 + NB + 1], w_head_in[0:NB + 1, :], ident[0:NB + 1, 0:NB + 1]).then_inc(s["lstm_w_ps"], 1)

            def turn_tokens(banks, count, q):
                pe.wait_ge(s["ln_done"], GROUPS * (count - 1) + q + 1)
                for t in range(G4):
                    m = tr(ps[:, banks[q], t * TOK:(t + 1) * TOK], xnorm[:, G4 * q + t, :], ident[0:TOK, 0:TOK])
                m.then_inc(s["xT_ps"], 1)

            for q in range(GROUPS):
                turn_tokens(TOKEN_BANKS[0], 1, q)

            GATE = (0, 1, 3, 2)
            xT_steps = xT[:].rearrange("d k (b t) -> d t b k", b=2)
            pe.wait_ge(s["xT_sb"], 4)
            pe.wait_ge(s["lstm_w_sb"], 3)
            pe.wait_ge(s["bias_in"], 64)
            pe.wait_ge(s["zeros_made"], 3)

            def input_part(bank, gate, t0):
                mm(ps[0:PE, bank, gate * 128:(gate + 1) * 128], wihT[:, GATE[gate] * PE:(GATE[gate] + 1) * PE],
                   xT_steps[:, bass.ds(t0, G4), :, :], start=(gate == 0), stop=False, skip_group_check=True)

            def head(it, u):
                return mm(ps[0:B, 2, bass.ds((U8 * it + u) * (NB + 1), NB + 1)], lstm_h[:, u, :], headT, start=True, stop=True)

            def lstm_steps(it, beside=None):
                first, last = isinstance(it, int) and it == 0, isinstance(it, int) and it == ITERS - 1
                for u in range(U8):
                    bank, v = u // G4, u % G4
                    need(pe, "h_ready", U8 * it + u)
                    for gate in range(4):
                        m = mm(ps[0:PE, bank, gate * 128 + v * B:gate * 128 + (v + 1) * B],
                               whhT[:, GATE[gate] * PE:(GATE[gate] + 1) * PE], lstm_h[:, (u - 1) % U8, :],
                               start=False, stop=True, skip_group_check=True)
                    m.then_inc(s["gates_ready"], 1)
                    if u:
                        head(it, u - 1)
                    elif not first:
                        head(it - 1, U8 - 1)
                    if bank == 0:
                        input_part(1, v, U8 * it + G4)
                    elif not last:
                        input_part(0, v, U8 * it + U8)
                    if beside:
                        beside(u)
                    else:
                        mm(ps[:, 3, 0:WARM], ident[:], xT[:].rearrange("d k t -> d (k t)")[:, 0:WARM], start=True, stop=True)

            def turn_weights(f):
                if f == 0:
                    pe.wait_ge(s["attn_w_in"], 80)
                need(pe, "turned_w_sb", f - 1)
                for n, w in enumerate((wq_raw, wk_raw, wv_raw)):
                    m = tr(ps[:, SIDE + f % 2, n * D:(n + 1) * D], w[:, f * D:(f + 1) * D], ident[:])
                m.then_inc(s["turned_w"], 1)

            def fold(f):
                need(pe, "turned_w_sb", f + 1)
                need(pe, "folded_sb", 2 * f)
                for n in range(2):
                    part = slice(DK * n, DK * n + DK)
                    mm(ps[:, FOLD_BANK + n, 0:D], wT_sb[part, f % 2, 0, :], wT_sb[part, f % 2, 1, :], start=True, stop=True)
                    m = mm(ps[:, FOLD_BANK + n, D:2 * D], wT_sb[part, f % 2, 2, :], wo_raw[part, f, :], start=True, stop=True)
                m.then_inc(s["folded"], 1)

            def router_logits(q, bank):
                if q == 0:
                    pe.wait_ge(s["ffn_w_in"], 16 * 7)
                pe.wait_ge(s["xT_sb"], 2 * GROUPS + q + 1)
                for t in range(G4):
                    m = mm(ps[0:TOK, bank, t * E:(t + 1) * E], xT[:, G4 * q + t, :], wr_sb[:], start=True, stop=True)
                m.then_inc(s["logit_ps"], 1)

            def turn_onehot(q, bank):
                pe.wait_ge(s["onehot_made"], GROUPS - 1 if q < GROUPS - 1 else GROUPS)
                for t in range(G4):
                    m = tr(ps[0:E, bank, t * TOK:(t + 1) * TOK], onehot[:, (G4 * q + t) * E:(G4 * q + t + 1) * E], ident[0:TOK, 0:TOK])
                m.then_inc(s["onehotT_ps"], 1)

            def spread_mask(n, e):
                need(pe, "masked", E * n + e - 1)
                if e == 0:
                    pe.wait_ge(s["onehotT_sb"], max(n + 1, GROUPS - 1))
                mm(ps[:, mask_bank(e), 0:GT], pick_e[:, e, :], onehotT[n], start=True, stop=True).then_inc(s["mask_ps"], 1)

            def side(what, which, bank, i, k):
                nk, nb = 1 - k, 2 * i + k + 1
                if what == "turn":
                    if which == 0:
                        need(pe, f"ctx_in{k}", 16 * (i + 2))
                    for c in range(TG):
                        m = tr(ps[:, bank, c * CR:(c + 1) * CR], ctx_in[k][:, which * TG + c, :], ident[0:CR, 0:CR])
                    m.then_inc(s["ctxT_ps"], 1)
                elif what == "max":
                    block_, part = which // MP, which % MP
                    if which == 0:
                        need(pe, "q_hi_done", nb + 1)
                    if which < MP:
                        need(pe, "ctxT_hi_done", MP * nb + part + 1)
                    mm(ps[:, bank, 0:MC], q_hi[nk][:, block_ * 128:(block_ + 1) * 128], ctxT_hi[nk][:, part * MC:(part + 1) * MC],
                       start=True, stop=True).then_inc(s["max_ps"], 1)
                elif what == "spread":
                    if which == 0:
                        need(pe, "diag_done", nb + 1)
                    mm(ps[:, bank, 0:HALF], ones_r[:], max_diag[:, which * HALF:(which + 1) * HALF],
                       start=True, stop=True).then_inc(s["spread_ps"], 1)
                elif what == "sums":
                    if which == 0:
                        need(pe, "prob_added", (CH - 1) * (nb - 1))
                    for n in range(4):
                        m = mm(ps[0:TOK, bank, n:n + 1], prob_sum[:, 4 * which + n].rearrange("p b q -> p (b q)"), ones[0:CR, 0:1], start=True, stop=True)
                    m.then_inc(s["sums_ps"], 1)
                elif what == "project":
                    if which == 0:
                        need(pe, "u_act", nb - 1)
                        need(pe, "u_dve", nb - 1)
                    for n in range(4):
                        h = 4 * which + n
                        m = mm(ps[0:TOK, bank, n * D:(n + 1) * D], u_sum[:, h].rearrange("p b q -> p (b q)"), vo_w[:, h, :], start=True, stop=True)
                    m.then_inc(s["projected"], 1)
                elif what == "tokens":
                    turn_tokens((bank,) * GROUPS, 3, which)
                elif what == "logits":
                    router_logits(which, bank)
                elif what == "onehot":
                    turn_onehot(which, bank)
                elif what == "mask":
                    spread_mask(0, which)
                elif what == "query":
                    for n in range(4):
                        m = mm(ps[:, bank, n * TOK:(n + 1) * TOK], qk_w[:, 4 * which + n, :],
                               xT[:, bass.ds(i + 1, 1), :].rearrange("p k t -> p (k t)"), start=True, stop=True)
                    m.then_inc(s["q_ps"], 1)

            def beside_first(u):
                turn_weights(u)
                if u:
                    fold(u - 1)

            def beside_last(u):
                if u == 0:
                    fold(H // 2 - 1)
                elif u >= 2:
                    need(pe, "ctxT_lo_done", u - 3)
                    side("turn", (u - 2) % MP, SIDE + u % 2, -1, (u - 2) // MP)

            for gate in range(4):
                input_part(0, gate, 0)
            lstm_steps(0, beside_first)
            with pe.Fori(1, ITERS - 1) as it:
                lstm_steps(it)
            lstm_steps(ITERS - 1, beside_last)
            need(pe, "h_ready", S)
            head(ITERS - 1, U8 - 1).then_inc(s["head_ready"], 1)

            pe.wait_ge(s["rows_picked"], 1)
            pe.wait_ge(s["picks_made"], 6)
            mm(ps[0:TOK, 3, 0:PAIRS], mu_l.rearrange("p b j -> p (b j)"), pick_k, start=True, stop=True)
            mm(ps[0:TOK, 3, PAIRS:2 * PAIRS], inv_l.rearrange("p b j -> p (b j)"), pick_k, start=True, stop=True)
            mm(ps[0:TOK, 3, 128:128 + D], ones[0:1, 0:TOK], bO_row[:], start=True, stop=True).then_inc(s["pick_ps"], 1)

            def turn_gauss(q):
                pe.wait_ge(s["gauss_ready"], q + 1)
                for t in range(G4):
                    m = tr(ps[0:TOK, q, t * TOK:(t + 1) * TOK], gauss_w[:, G4 * q + t, :], ident[0:TOK, 0:TOK])
                m.then_inc(s["gaussT_ps"], 1)

            def self_attention(q):
                pe.wait_ge(s["gaussT_sb"], q + 1)
                for t in range(G4):
                    m = mm(ps[0:TOK, SELF_BANK[q], t * D:(t + 1) * D], gauss_wT[:, G4 * q + t, :], xnorm[:, G4 * q + t, :], start=True, stop=True)
                m.then_inc(s["self_attn_ps"], 1)

            for q in range(GROUPS + 1):
                if q < GROUPS:
                    turn_gauss(q)
                if q:
                    self_attention(q - 1)

            turn_tokens(TOKEN_BANKS[1], 2, 0)
            pe.wait_ge(s["xT_sb"], GROUPS + 1)
            for u in range(4):
                need(pe, "ctxT_lo_done", 2 * MP)
                if u > 1:
                    need(pe, "q_staged", u - 1)
                side("query", u, SIDE + u % 2, -1, 0)
            for q in range(1, GROUPS):
                turn_tokens(TOKEN_BANKS[1], 2, q)
            for n in range(RB * MP):
                if n < 2:
                    need(pe, "q_staged", 4)
                else:
                    need(pe, "max_read", n - 1)
                side("max", n, SIDE + n % 2, -1, 1)
            pe.wait_ge(s["xT_sb"], 2 * GROUPS)
            for bank in range(4):
                m = mm(ps[0:CR, bank, 0:HALF], ones_r[:, 0:CR], q_hi[0][:, 0:HALF], start=True, stop=True)
            m.then_inc(s["bits_set"], 1)
            for n in range(2):
                need(pe, "max_read", RB * MP)
                side("spread", n, SIDE + (n + 1) % 2, -1, 1)

            def scores(b, k, j, half):
                if half == 0:
                    if j == 0:
                        need(pe, "q_lo_done", b + 1)
                        need(pe, "ctxT_lo_done", MP * (b + 1))
                    need(pe, "seeded", CH * b + j + 1)
                rows, cols = slice(j * CR, (j + 1) * CR), slice(half * HALF, (half + 1) * HALF)
                for cx, q in ((ctxT_hi, q_hi), (ctxT_hi, q_lo), (ctxT_lo, q_hi)):
                    m = mm(score_ps[j % 2][:, half, :], cx[k][:, rows], q[k][:, cols], start=False, stop=True, skip_group_check=True)
                if half == 1:
                    m.then_inc(s["scored"], 1)

            def weigh(b, k, j, half):
                if half == 0:
                    if j == 0:
                        need(pe, "u_act", b)
                        need(pe, "u_dve", b)
                        need(pe, "ctx_lo_done", CP * (b + 1))
                    need(pe, "prob_lo_done", CH * b + j + 1)
                for n, (cx, p) in enumerate(((ctx_hi, p_hi), (ctx_hi, p_lo), (ctx_lo, p_hi))):
                    m = mm(usum_ps[:, half, :], cx[k][:, j, :], p[j % 3][:, half, :], start=(j == 0 and n == 0), stop=(j == CH - 1 and n == 2))
                if half == 1:
                    m.then_inc(s["weighted"], 1)

            for half in range(2):
                scores(0, 0, 0, half)

            def period(i, k):
                b = 2 * i + k
                first = isinstance(i, int) and i == 0 and k == 0
                last = isinstance(i, int) and i == PAIRS - 1 and k == 1
                work = {(j, p): row for (j, p), *row in side_banks(i, k)}

                def beside(j, p):
                    if (j, p) in work:
                        what, which, bank, (name, value) = work[j, p]
                        need(pe, name, value)
                        side(what, which, bank, i, k)

                for j in range(CH):
                    ahead = (b, k, j + 1) if j + 1 < CH else (b + 1, 1 - k, 0)
                    behind = (b, k, j - 1) if j else (b - 1, 1 - k, CH - 1)
                    for half in range(2):
                        if j + 1 < CH or not last:
                            scores(*ahead, half)
                        beside(j, half)
                    for half in range(2):
                        if j or not first:
                            weigh(*behind, half)
                        beside(j, 2 + half)

            sequence(pe, period)
            for half in range(2):
                weigh(B - 1, 1, CH - 1, half)

            def hidden(n, e):
                need(pe, "masked", E * n + e + 1)
                if n == 0:
                    need(pe, "w1_lo_done", e + 1)
                for m_ in range(MB):
                    cols, o_ps = slice(m_ * 128, (m_ + 1) * 128), ps[:, m_, 0:GT]
                    if e == 0:
                        need(pe, "hid_act", MB * (n - 1) + m_ + 1)
                        for half in range(2):
                            mm(o_ps, b1_r[:, half, cols], onehotT[n], start=(half == 0), stop=False)
                    for w, x_half in ((w1_hi[e], 0), (w1_lo[e], 0), (w1_hi[e], 1)):
                        last = e == E - 1 and x_half == 1
                        m = mm(o_ps, w[:, cols], expert_x[e][:, x_half, :], start=False, stop=last)
                    if e == E - 1:
                        m.then_inc(s["hid_ps"], 1)
                    elif m_ == MB - 1:
                        m.then_inc(s["expert_used"], 1)

            def output(n):
                if n == 0:
                    pe.wait_ge(s["xT_sb"], 3 * GROUPS)
                need(pe, "yT_sb", n)
                for m_ in range(MB):
                    need(pe, "hid_act", MB * n + m_ + 1)
                    m = mm(ps[:, YT_BANK, 0:GT], wo_sb[:, m_, :], inter[n % 2][:, m_, :], start=(m_ == 0), stop=(m_ == MB - 1))
                m.then_inc(s["yT_ps"], 1)

            def turn_output(n):
                need(pe, "yT_sb", n + 1)
                if n == 0:
                    pe.wait_ge(s["onehotT_sb"], GROUPS)
                else:
                    need(pe, "y_step", Y_STEPS * (n - 1) + Y_READ)
                for t in range(G4):
                    m = tr(ps[0:TOK, Y_BANK, t * D:(t + 1) * D], yT_sb[n % 2][:, t * TOK:(t + 1) * TOK], ident[:])
                m.then_inc(s["y_ps"], 1)

            def last_sums(n):
                if n < 2:
                    need(pe, "u_act", B)
                    need(pe, "u_dve", B)
                else:
                    need(pe, "recip_done", 4 * (PAIRS - 1) + n - 1)
                side("sums", n, YT_BANK + n % 2, PAIRS, 0)

            def last_project(n):
                if n < 2:
                    need(pe, "recip_done", 4 * (PAIRS - 1) + n + 3)
                else:
                    need(pe, "head_added", H * (PAIRS - 1) + 4 * (n - 1))
                side("project", n, YT_BANK + n % 2, PAIRS, 0)

            def spread_rows():
                need(pe, "head_added", H * PAIRS)
                mm(ps[0:TOK, Y_BANK, 0:2 * D], ones[0:1, 0:TOK], rows_sb[:].rearrange("p n d -> p (n d)"), start=True, stop=True).then_inc(s["rows_ps"], 1)

            def last_tokens():
                turn_tokens((YT_BANK,) * GROUPS, 3, GROUPS - 1)

            def last_logits():
                pe.wait_ge(s["rows_copied"], 1)
                router_logits(GROUPS - 1, Y_BANK)

            def last_onehot():
                pe.wait_ge(s["logits_read"], GROUPS)
                turn_onehot(GROUPS - 1, Y_BANK)

            after = {(0, 0): [(last_sums, 0), (last_sums, 1)], (0, 1): [(last_sums, 2), (last_sums, 3)],
                     (0, 2): [(last_project, 0), (last_project, 1)], (0, 3): [(last_project, 2), (last_project, 3)],
                     (1, 0): [(spread_rows,)], (1, 1): [(last_tokens,)], (1, 2): [(last_logits,)], (1, 3): [(output, 0)],
                     (2, 0): [(last_onehot,)], (2, 1): [(turn_output, 0)], (2, 3): [(output, 1)],
                     (3, 0): [(turn_output, 1)], (3, 1): [(output, 2)],
                     (3, 3): [(turn_output, 2), (output, 3), (turn_output, 3)]}
            pe.wait_ge(s["b1_lo_done"], 1)
            pe.wait_ge(s["prob_done"], CH * B)
            for n in range(GROUPS):
                for e in range(E):
                    hidden(n, e)
                    u = E * n + e + 2
                    if u < E * GROUPS:
                        spread_mask(u // E, u % E)
                    for piece, *args in after.get((n, e), ()):
                        piece(*args)

        @block.scalar
        def _(act):
            a = nc.scalar.activation
            ctx_pairs = ctx_1024.rearrange("(i n) (p c) d -> n p i (c d)", n=2, p=CR)

            def load_context(i, k):
                need(act, "ctx_lo_done", CP * (2 * i + k + 1))
                need(act, "ctxT_ps", MP * (2 * i + k + 1))
                act.dma_start(ctx_raw[k][0:CR, :], ctx_pairs[k, :, bass.ds(i + 1, 1), :].rearrange("p i c -> p (i c)")).then_inc(
                    s[f"ctx_in{k}"], 16)

            def copy_tokens(banks, count, q):
                need(act, "xT_ps", GROUPS * (count - 1) + q + 1)
                a(xT[:, G4 * q:G4 * q + G4, :].rearrange("d k t -> d (k t)"), ps[:, banks[q], 0:GT], ACT.Copy).then_inc(s["xT_sb"], 1)

            need(act, "zeros_made", 3)
            a(cell_t, cell, ACT.Sigmoid).then_inc(s["table_loaded"], 1)
            act.wait_ge(s["lstm_w_ps"], 1)
            need(act, "biased_cleared", 2)
            a(wihT, ps[:, 3, 0:4 * PE], ACT.Copy).then_inc(s["lstm_w_sb"], 1)
            a(whhT[0:PE, :], ps[0:PE, 3, 128:128 + 4 * PE], ACT.Copy).then_inc(s["lstm_w_sb"], 1)
            a(headT[0:PE, :], ps[0:PE, 3, 256:256 + NB + 1], ACT.Copy).then_inc(s["lstm_w_sb"], 1)
            for q in range(GROUPS):
                copy_tokens(TOKEN_BANKS[0], 1, q)

            def lstm_steps(it, beside=None):
                for u in range(U8):
                    t = U8 * it + u
                    gates = ps[0:PE, u // G4, :].rearrange("p (g t b) -> p g t b", g=4, t=G4)[:, :, u % G4, :]
                    need(act, "gates_ready", t + 1)
                    a(gate_act[:, 0:3, :], gates[:, 0:3, :], ACT.Sigmoid).then_inc(s["sig_ready"], 1)
                    a(gate_act[:, 3, :], gates[:, 3, :], ACT.Tanh).then_inc(s["tanhg_ready"], 1)
                    need(act, "cell_step", 3 * t + 3)
                    a(cell_t, cell, ACT.Tanh).then_inc(s["tanhc_ready"], 1)
                    if beside:
                        beside(u)

            def copy_turned(f):
                need(act, "turned_w", f + 1)
                need(act, "folded", f - 1)
                a(wT_sb[:, f % 2].rearrange("p n d -> p (n d)"), ps[:, SIDE + f % 2, 0:3 * D], ACT.Copy).then_inc(s["turned_w_sb"], 1)

            def fold_out(f):
                need(act, "folded", f + 1)
                for side_, w in enumerate((qk_w, vo_w)):
                    a(w[:, 2 * f:2 * f + 2, :], ps[:, FOLD_BANK:FOLD_BANK + 2, side_ * D:(side_ + 1) * D], ACT.Copy).then_inc(s["folded_sb"], 1)

            def turned_hi(i, k, which, bank):
                tb = 2 * (i + 1) + k
                need(act, "ctxT_ps", MP * tb + which + 1)
                a(ctxT_hi[k][:, which * MC:(which + 1) * MC], ps[:, bank, 0:MC], ACT.Copy).then_inc(s["ctxT_hi_done"], 1)

            def beside_first(u):
                copy_turned(u)
                if u:
                    fold_out(u - 1)

            def beside_last(u):
                if u == 1:
                    fold_out(H // 2 - 1)
                elif u >= 2:
                    turned_hi(-1, (u - 2) // MP, (u - 2) % MP, SIDE + u % 2)

            lstm_steps(0, beside_first)
            act.wait_ge(s["pick_e_made"], 2)
            a(pick_e[:], pick_e_in, ACT.Copy).then_inc(s["pick_e_sb"], 1)
            act.wait_ge(s["ones_made"], 1)
            a(ones_r[:], ones[:], ACT.Copy).then_inc(s["ones_r_made"], 1)
            with act.Fori(1, ITERS - 1) as it:
                lstm_steps(it)
            lstm_steps(ITERS - 1, beside_last)

            act.wait_ge(s["head_read"], 1)
            a(sig, ps[0:B, 2, 0:S * (NB + 1)].rearrange("p (t n) -> p t n", n=NB + 1)[:, :, NB], ACT.Sigmoid).then_inc(s["sigma_done"], 1)

            def tiles(q):
                return slice(G4 * q, G4 * q + G4)

            def gauss_square(q):
                act.wait_ge(s["gauss_diff"], q + 1)
                a(gauss_w[:, tiles(q), :], gauss_d[:, tiles(q), :], ACT.Square).then_inc(s["gauss_sq"], 1)

            def gauss_exponential(q):
                act.wait_ge(s["gauss_arg"], q + 1)
                a(gauss_w[:, tiles(q), :], gauss_d[:, tiles(q), :], ACT.Exp, scale=-1.0).then_inc(s["gauss_exp"], 1)

            def gauss_weight_square(q):
                act.wait_ge(s["gauss_ready"], q + 1)
                a(gauss_d[:, tiles(q), :], gauss_w[:, tiles(q), :], ACT.Square).then_inc(s["gauss_w2"], 1)

            def copy_gauss(q):
                act.wait_ge(s["gaussT_ps"], q + 1)
                a(gauss_wT[:, tiles(q), :].rearrange("p k t -> p (k t)"), ps[0:TOK, q, 0:GT], ACT.Copy).then_inc(s["gaussT_sb"], 1)

            for n in range(GROUPS + 3):
                if n < GROUPS:
                    gauss_square(n)
                if 0 <= n - 1 < GROUPS:
                    gauss_exponential(n - 1)
                if 0 <= n - 2 < GROUPS:
                    gauss_weight_square(n - 2)
                if n >= 3:
                    copy_gauss(n - 3)

            def stage_query(i, which, bank):
                need(act, "q_ps", 4 * (i + 1) + which + 1)
                need(act, "q_lo_done", 2 * (i + 1))
                a(q_stage[:, :, 4 * which:4 * which + 4, :], ps[:, bank, 0:4 * TOK].rearrange("p (h b q) -> p b h q", h=4, b=2),
                  ACT.Copy).then_inc(s["q_staged"], 1)

            def query_hi(i, k):
                need(act, "q_staged", 4 * (i + 2))
                need(act, "scored", CH * (2 * i + k + 1))
                a(q_hi[k][:].rearrange("p (h q) -> p h q", h=H), q_stage[:, k], ACT.Copy).then_inc(s["q_hi_done"], 1)

            def negate_max(i, k, which, bank):
                nk, nb = 1 - k, 2 * i + k + 1
                need(act, "spread_ps", 2 * nb + which + 1)
                need(act, "seeded", CH * (nb - 1))
                a(neg_max[nk][:, which, :], ps[:, bank, 0:HALF], ACT.Copy, scale=-1.0).then_inc(s["neg_done"], 1)

            def seed(b, k, j):
                lb, lj = (b, j - 2) if j >= 2 else (b - 1, CH + j - 2)
                if lj in DVE_HI:
                    need(act, "prob_done", CH * lb + lj + 1)
                else:
                    need(act, "prob_hi_done", hi_count(lb, lj))
                need(act, "neg_done", 2 * (b + 1))
                a(score_ps[j % 2], neg_max[k][0:CR], ACT.Copy).then_inc(s["seeded"], 1)

            copy_tokens(TOKEN_BANKS[1], 2, 0)
            for u in range(4):
                stage_query(-1, u, SIDE + u % 2)
            query_hi(-1, 0)
            for q in range(1, GROUPS):
                copy_tokens(TOKEN_BANKS[1], 2, q)
            query_hi(-1, 1)
            for n in range(2):
                negate_max(-1, 1, n, SIDE + (n + 1) % 2)
            act.wait_ge(s["bits_set"], 1)
            seed(0, 0, 0)
            seed(0, 0, 1)

            def take_u(i, k):
                need(act, "weighted", CH * (2 * i + k))
                if k == 1:
                    need(act, "projected", 4 * i)
                a(u_sum[:, 0:HB, 1 - k, :], usum_ps[:, 0, :].rearrange("p (h q) -> p h q", h=HB), ACT.Copy).then_inc(s["u_act"], 1)

            def group_halves(n):
                if n == 0:
                    need(act, "spread_ps", 2 * B)
                need(act, "masked", E * n)
                a(xT_halves[:, 0, :], xT[:, G4 * n:G4 * n + G4, :].rearrange("d k t -> d (k t)"), ACT.Copy).then_inc(s["xT_hi_done"], 1)

            def copy_onehot(q, bank):
                need(act, "onehotT_ps", q + 1)
                a(onehotT[q], ps[0:E, bank, 0:GT], ACT.Copy).then_inc(s["onehotT_sb"], 1)

            def side_copies(i, k, j):
                for what, which, bank in slot_work(i, k, j):
                    if what == "turn":
                        turned_hi(i, k, which, bank)
                    elif what == "spread":
                        negate_max(i, k, which, bank)
                    elif what == "query":
                        stage_query(i, which, bank)
                    elif what == "tokens":
                        copy_tokens((bank,) * GROUPS, 3, which)
                    elif what == "onehot":
                        copy_onehot(which, bank)

            def period(i, k):
                b = 2 * i + k
                first = isinstance(i, int) and i == 0 and k == 0
                last = isinstance(i, int) and i == PAIRS - 1 and k == 1
                for j in range(CH):
                    c = CH * b + j
                    need(act, "scored", c + 1)
                    need(act, "prob_lo_done", c - 2)
                    need(act, "prob_added", (CH - 1) * b + (max(j - 3, 1) if j >= 3 else j - 2))
                    a(probs[j % 3], score_ps[j % 2], ACT.Exp, scale=SCALE).then_inc(s["prob_done"], 1)
                    if j or not first:
                        side_copies(*((i, k, j - 1) if j else (i, 0, CH - 1) if k else (i - 1, 1, CH - 1)))
                    if j == 1 and not first:
                        take_u(i, k)
                    if j not in DVE_HI:
                        need(act, "weighted", c - 2)
                        a(p_hi[j % 3][:], score_ps[j % 2], ACT.Exp, scale=SCALE).then_inc(s["prob_hi_done"], 1)
                    if j + 2 < CH:
                        seed(b, k, j + 2)
                    elif not last:
                        seed(b + 1, 1 - k, j + 2 - CH)
                    if j == 2 and not (isinstance(i, int) and i == PAIRS - 1):
                        load_context(i, k)
                    if last and j == 9:
                        group_halves(0)
                    if last and j == 6:
                        act.wait_ge(s["ffn_w_in"], 16 * 7)
                        need(act, "weighted", CH * (B - 1))
                        a(b1_r[:, 0, :], b1_sb[:], ACT.Copy).then_inc(s["b1_hi_done"], 1)
                    if j == CH - 1 and not (isinstance(i, int) and i == PAIRS - 1):
                        query_hi(i, k)

            sequence(act, period)
            take_u(PAIRS, 0)

            def activate(n):
                need(act, "yT_ps", n - 1)
                for m_ in range(MB):
                    need(act, "hid_ps", MB * n + m_ + 1)
                    a(inter[n % 2][:, m_, :], ps[:, m_, 0:GT], ACT.Gelu).then_inc(s["hid_act"], 1)

            group_halves(1)
            activate(0)
            copy_tokens((YT_BANK,) * GROUPS, 3, GROUPS - 1)
            group_halves(2)
            activate(1)
            copy_onehot(GROUPS - 1, Y_BANK)
            group_halves(3)
            activate(2)
            activate(3)

        @block.vector
        def _(dve):
            v = nc.vector

            ln_steps = [0]

            def norm_step(m):
                ln_steps[0] += 1
                m.then_inc(s["ln_step"], 1)
                dve.wait_ge(s["ln_step"], ln_steps[0])

            def moments(count, q):
                group = range(G4 * q, G4 * q + G4)
                for t in group:
                    m = v.bn_stats(stats[:, t, :], resid_k[:, t, :])
                norm_step(m)
                for t in group:
                    m = v.bn_aggr(meanvar[:, t, :], stats[:, t, :])
                norm_step(m)
                v.tensor_scalar(veps[:, G4 * q:G4 * q + G4], meanvar[:, G4 * q:G4 * q + G4, 1], 1e-5, None, ALU.add).then_inc(s["ln_var"], 1)

            def scale(count, q):
                dve.wait_ge(s["rstd_done"], GROUPS * (count - 1) + q + 1)
                for t in range(G4 * q, G4 * q + G4):
                    m = v.tensor_scalar(xnorm[:, t, :], resid_k[:, t, :], meanvar[:, t, 0:1], rstd[:, t:t + 1], ALU.subtract, ALU.mult)
                m.then_inc(s["ln_done"], 1)

            def layer_norm(count, before=None):
                for q in range(GROUPS):
                    if before:
                        before(q)
                    moments(count, q)
                    if q:
                        scale(count, q - 1)
                scale(count, GROUPS - 1)

            dve.wait_ge(s["x_in"], 16)
            layer_norm(1)

            gauss_count = [0]

            def then(m):
                gauss_count[0] += 1
                m.then_inc(s["gauss_step"], 1)
                dve.wait_ge(s["gauss_step"], gauss_count[0])

            dve.wait_ge(s["indices_made"], 3)
            v.tensor_copy(jp1, jp1_int)
            v.tensor_copy(i_idx, idx_int)
            then(v.tensor_copy(pos[:, 0:1], p_int))
            dve.wait_ge(s["rel_made"], 2)
            then(v.tensor_tensor(pos[:, 2:3], pos[:, 0:1], pos[:, 1:2], ALU.add))
            then(v.reciprocal(pos[:, 3:4], pos[:, 2:3]))
            then(v.tensor_scalar(rel, i_idx, pos[:, 3:4], None, ALU.mult))

            dve.wait_ge(s["zeros_made"], 3)

            def turned_lo(i, k, which, bank):
                tb = 2 * (i + 1) + k
                part = slice(which * MC, (which + 1) * MC)
                need(dve, "ctxT_hi_done", MP * tb + which + 1)
                v.tensor_tensor(ctxT_lo[k][:, part], ps[:, bank, 0:MC], ctxT_hi[k][:, part].bitcast(F32), ALU.subtract).then_inc(s["ctxT_lo_done"], 1)

            def lstm_steps(it, beside=None):
                for u in range(U8):
                    t = U8 * it + u
                    need(dve, "sig_ready", t + 1)
                    need(dve, "cell_step", 3 * t)
                    v.tensor_tensor(cell_f, gate_act[:, 1, :], cell, ALU.mult).then_inc(s["cell_step"], 1)
                    need(dve, "tanhg_ready", t + 1)
                    v.tensor_tensor(cell_i, gate_act[:, 0, :], gate_act[:, 3, :], ALU.mult).then_inc(s["cell_step"], 1)
                    need(dve, "cell_step", 3 * t + 2)
                    v.tensor_tensor(cell, cell_f, cell_i, ALU.add).then_inc(s["cell_step"], 1)
                    need(dve, "tanhc_ready", t + 1)
                    v.tensor_tensor(lstm_h[0:PE, u, :], gate_act[:, 2, :], cell_t, ALU.mult).then_inc(s["h_ready"], 1)
                    if beside:
                        beside(u)

            def beside_last(u):
                if u >= 3:
                    turned_lo(-1, (u - 3) // MP, (u - 3) % MP, SIDE + (u - 1) % 2)

            lstm_steps(0)
            with dve.Fori(1, ITERS - 1) as it:
                lstm_steps(it)
            lstm_steps(ITERS - 1, beside_last)

            heads = ps[0:B, 2, 0:S * (NB + 1)].rearrange("p (t n) -> p n t", n=NB + 1)
            dve.wait_ge(s["head_ready"], 1)
            v.tensor_scalar(mu_w, heads[:, 0:NB, :], 0.0, None, ALU.max).then_inc(s["head_read"], 1)
            dve.wait_ge(s["head_read"], 1)
            then(v.scalar_tensor_tensor(mu_t, mu_w[:, 2, :], 1.0 / S, jp1, ALU.mult, ALU.mult))
            then(v.scalar_tensor_tensor(mu_b, mu_w[:, 1, :], 1.0 / S, mu_t, ALU.mult, ALU.add))
            then(v.tensor_tensor_scan(mu, mu_w[:, 0, :], mu_b, 0.0, ALU.mult, ALU.add))

            def over_b(ap):
                return ap[:, None, :].to_broadcast((B, 2, S))

            dve.wait_ge(s["sigma_done"], 1)
            dve.wait_ge(s["picks_made"], 6)
            v.tensor_tensor(mu_l, over_b(mu), pick_b, ALU.mult)
            then(v.scalar_tensor_tensor(sig2, sig, 2.0, sig, ALU.mult, ALU.mult))
            then(v.reciprocal(inv2s, sig2))
            v.tensor_tensor(inv_l, over_b(inv2s), pick_b, ALU.mult).then_inc(s["rows_picked"], 1)
            turned_lo(-1, 1, MP - 1, SIDE + 1)
            dve.wait_ge(s["pick_ps"], 1)
            v.tensor_copy(bO_b[:], ps[0:TOK, 3, 128:128 + D]).then_inc(s["picks_read"], 1)
            then(v.tensor_copy(mu_tok.rearrange("p a k -> p (a k)"), ps[0:TOK, 3, 0:2 * PAIRS]))

            def tiles(q):
                return slice(G4 * q, G4 * q + G4)

            def over_k(ap):
                return ap[:, None, :].to_broadcast((TOK, G4, TOK))

            def over_i(ap, q):
                return ap[:, tiles(q), None].to_broadcast((TOK, G4, TOK))

            def gauss_difference(q):
                v.tensor_tensor(gauss_d[:, tiles(q), :], over_k(rel), over_i(mu_tok[:, 0, :], q), ALU.subtract).then_inc(s["gauss_diff"], 1)

            def gauss_argument(q):
                dve.wait_ge(s["gauss_sq"], q + 1)
                v.tensor_tensor(gauss_d[:, tiles(q), :], gauss_w[:, tiles(q), :], over_i(mu_tok[:, 1, :], q), ALU.mult).then_inc(s["gauss_arg"], 1)

            def gauss_mask(q):
                dve.wait_ge(s["gauss_exp"], q + 1)
                v.tensor_tensor(gauss_w[:, tiles(q), :], gauss_w[:, tiles(q), :], over_k(causal), ALU.mult).then_inc(s["gauss_ready"], 1)

            def gauss_norm(q):
                dve.wait_ge(s["gauss_w2"], q + 1)
                then(v.tensor_reduce(wsum[:, tiles(q)], gauss_d[:, tiles(q), :], AX.X, ALU.add))
                v.tensor_scalar(wsum[:, tiles(q)], wsum[:, tiles(q)], 1e-24, None, ALU.max).then_inc(s["norm_in"], 1)

            dve.wait_ge(s["causal_made"], 3)
            for n in range(GROUPS + 3):
                if n < GROUPS:
                    gauss_difference(n)
                if 0 <= n - 1 < GROUPS:
                    gauss_argument(n - 1)
                if 0 <= n - 2 < GROUPS:
                    gauss_mask(n - 2)
                if n >= 3:
                    gauss_norm(n - 3)

            def add_self_attention(q):
                dve.wait_ge(s["norm_done"], q + 1)
                dve.wait_ge(s["self_attn_ps"], q + 1)
                for t in range(G4):
                    tile = G4 * q + t
                    m = v.scalar_tensor_tensor(resid_k[:, tile, :], ps[0:TOK, SELF_BANK[q], t * D:(t + 1) * D], wsum[:, tile:tile + 1],
                                               resid_k[:, tile, :], ALU.mult, ALU.add)
                m.then_inc(s["x1_done"], 1)
                dve.wait_ge(s["x1_done"], q + 1)

            layer_norm(2, add_self_attention)

            def query_lo(i, k):
                need(dve, "q_hi_done", 2 * (i + 1) + k + 1)
                v.tensor_tensor(q_lo[k][:].rearrange("p (h q) -> p h q", h=H), q_stage[:, k],
                                q_hi[k][:].bitcast(F32).rearrange("p (h q) -> p h q", h=H), ALU.subtract).then_inc(s["q_lo_done"], 1)

            def read_max(i, k, which, bank):
                nb = 2 * i + k + 1
                need(dve, "max_ps", RB * MP * nb + which + 1)
                if which == 0:
                    need(dve, "max_found", nb)
                v.tensor_reduce(max_parts[:, which:which + 1], ps[:, bank, 0:MC], AX.X, ALU.max).then_inc(s["max_read"], 1)
                if which == RB * MP - 1:
                    need(dve, "max_read", RB * MP * (nb + 1))
                    need(dve, "diag_done", nb)
                    v.tensor_reduce(max_all[:], max_parts[:].rearrange("p (r m) -> p r m", m=MP), AX.X, ALU.max).then_inc(s["max_found"], 1)
                    need(dve, "max_found", nb + 1)
                    need(dve, "spread_ps", 2 * nb)
                    v.tensor_tensor(max_diag[:].rearrange("p (r c) -> p r c", r=RB), ident[:, None, :].to_broadcast((128, RB, 128)),
                                    max_all[:, :, None].to_broadcast((128, RB, 128)), ALU.mult).then_inc(s["diag_done"], 1)

            def take_u(i, k):
                need(dve, "weighted", CH * (2 * i + k))
                if k == 1:
                    need(dve, "projected", 4 * i)
                v.tensor_copy(u_sum[:, HB:H, 1 - k, :], usum_ps[:, 1, :].rearrange("p (h q) -> p h q", h=HB)).then_inc(s["u_dve"], 1)

            def invert_sums(pair, which, bank):
                need(dve, "sums_ps", 4 * pair + which + 1)
                v.reciprocal(sum_recip[:, 4 * which:4 * which + 4], ps[0:TOK, bank, 0:4]).then_inc(s["recip_done"], 1)

            def add_heads(pair, which, bank):
                tile = resid[:, bass.ds(pair * D, D)]
                need(dve, "projected", 4 * pair + which + 1)
                if which == 0:
                    need(dve, "recip_done", 4 * (pair + 1))
                for n in range(4):
                    h = 4 * which + n
                    product, scale = ps[0:TOK, bank, n * D:(n + 1) * D], sum_recip[:, h:h + 1]
                    if h >= 2:
                        need(dve, "head_added", H * pair + h - 1)
                    if h == 1:
                        m = v.tensor_scalar(odd_heads[:], product, scale, None, ALU.mult)
                    elif h % 2:
                        m = v.scalar_tensor_tensor(odd_heads[:], product, scale, odd_heads[:], ALU.mult, ALU.add)
                    else:
                        m = v.scalar_tensor_tensor(tile, product, scale, tile, ALU.mult, ALU.add)
                    m.then_inc(s["head_added"], 1)
                if which == 3:
                    need(dve, "head_added", H * (pair + 1))
                    v.tensor_tensor(tile, tile, odd_heads[:], ALU.add).then_inc(s["x2_done"], 1)

            route_count = [0]

            def route(m):
                route_count[0] += 1
                m.then_inc(s["onehot_step"], 1)
                dve.wait_ge(s["onehot_step"], route_count[0])

            def choose_experts(lo, hi):
                x, k = slice(lo, hi), hi - lo
                dve.wait_ge(s["logits_read"], hi // G4)
                route(v.tensor_reduce(best[:, x], logits[:, x, :], AX.X, ALU.max))
                route(v.tensor_tensor(is_best[:, x, :], logits[:, x, :], best[:, x, None].to_broadcast((TOK, k, E)), ALU.is_equal))
                v.tensor_copy(seen[:, x], is_best[:, x, 0])
                route(v.tensor_copy(onehot_k[:, x, 0], is_best[:, x, 0]))
                for e in range(1, E):
                    m = v.scalar_tensor_tensor(onehot_k[:, x, e], seen[:, x], 0.5, is_best[:, x, e], ALU.is_lt, ALU.mult)
                    if e + 1 < E:
                        route(m)
                        route(v.tensor_tensor(seen[:, x], seen[:, x], is_best[:, x, e], ALU.max))
                m.then_inc(s["onehot_made"], hi // G4 - lo // G4)

            def read_logits(q, bank):
                dve.wait_ge(s["logit_ps"], q + 1)
                v.tensor_copy(logits[:, G4 * q:G4 * q + G4, :].rearrange("p k e -> p (k e)"), ps[0:TOK, bank, 0:G4 * E]).then_inc(s["logits_read"], 1)

            def low_tokens(n):
                dve.wait_ge(s["xT_hi_done"], n + 1)
                v.tensor_tensor(xT_halves[:, 1, :], xT[:, G4 * n:G4 * n + G4, :].rearrange("d k t -> d (k t)"),
                                xT_halves[:, 0, :].bitcast(F32), ALU.subtract).then_inc(s["xT_lo_done"], 1)
                dve.wait_ge(s["xT_lo_done"], n + 1)

            def mask_tokens(n, e):
                if e == 0:
                    low_tokens(n)
                dve.wait_ge(s["mask_ps"], E * n + e + 1)
                if n == 0 and e % 2:
                    dve.wait_ge(s["scored"], CH * B)
                if n and e < E - 1:
                    dve.wait_ge(s["expert_used"], (E - 1) * (n - 1) + e + 1)
                elif n:
                    dve.wait_ge(s["hid_ps"], MB * n)
                v.tensor_tensor(expert_x[e], xT_halves.bitcast(F32), ps[:, mask_bank(e), None, 0:GT].to_broadcast((128, 2, GT)), ALU.mult).then_inc(s["masked"], 1)

            def beside_last_batch(j):
                if j == 0:
                    need(dve, "x2_done", PAIRS - 1)
                    moments(3, 0)
                elif j == 1:
                    moments(3, 1)
                    scale(3, 0)
                elif j == 2:
                    scale(3, 1)
                elif j == 3:
                    moments(3, 2)
                elif j == 4:
                    scale(3, 2)
                elif j == 6:
                    dve.wait_ge(s["b1_hi_done"], 1)
                    v.tensor_tensor(b1_r[:, 1, :], b1_sb[:], b1_r[:, 0, :].bitcast(F32), ALU.subtract).then_inc(s["b1_lo_done"], 1)
                elif j == 8:
                    choose_experts(0, G4 * (GROUPS - 1))
                elif j == 11:
                    mask_tokens(0, 0)
                    mask_tokens(0, 1)

            def late_turns(i, k, j):
                for what, which, bank in slot_work(i, k, j):
                    if what == "turn":
                        turned_lo(i, k, which, bank)

            def side_reads(i, k, j, places):
                for what, which, bank in slot_work(i, k, j, places):
                    if what == "max":
                        read_max(i, k, which, bank)
                    elif what == "sums":
                        invert_sums(i - 1, which, bank)
                    elif what == "project":
                        add_heads(i - 1, which, bank)
                    elif what == "logits":
                        read_logits(which, bank)

            query_lo(-1, 0)
            for n in range(RB * MP):
                read_max(-1, 1, n, SIDE + n % 2)
            query_lo(-1, 1)
            need(dve, "bO_added", 1)

            def period(i, k):
                b = 2 * i + k
                first = isinstance(i, int) and i == 0 and k == 0
                last = isinstance(i, int) and i == PAIRS - 1 and k == 1
                for j in range(CH):
                    c = CH * b + j
                    if j == 1 and not first:
                        take_u(i, k)
                    side_reads(i, k, j, (0,))
                    if j or not first:
                        late_turns(*((i, k, j - 1) if j else (i, 0, CH - 1) if k else (i - 1, 1, CH - 1)))
                    side_reads(i, k, j, (1,))
                    need(dve, "weighted", c - 2)
                    if j in DVE_HI:
                        need(dve, "prob_done", c + 1)
                        v.tensor_copy(p_hi[j % 3][:], probs[j % 3]).then_inc(s["prob_hi_dve"], 1)
                        need(dve, "prob_hi_dve", len(DVE_HI) * b + DVE_HI.index(j) + 1)
                    else:
                        need(dve, "prob_hi_done", hi_count(b, j))
                    v.tensor_tensor(p_lo[j % 3][:], probs[j % 3], p_hi[j % 3][:].bitcast(F32), ALU.subtract).then_inc(s["prob_lo_done"], 1)
                    side_reads(i, k, j, (2, 3))
                    if last:
                        beside_last_batch(j)
                    if j == CH - 1 and not (isinstance(i, int) and i == PAIRS - 1):
                        query_lo(i, k)

            sequence(dve, period)
            take_u(PAIRS, 0)
            y_count = [0]

            def step(m):
                y_count[0] += 1
                m.then_inc(s["y_step"], 1)
                dve.wait_ge(s["y_step"], y_count[0])

            def over_t(n):
                return rows_b[:, n, None, :].to_broadcast((TOK, G4, D))

            def take_output(n):
                dve.wait_ge(s["yT_ps"], n + 1)
                need(dve, "y_ps", n - 1)
                v.scalar_tensor_tensor(yT_sb[n % 2], ps[:, YT_BANK, 0:GT], bo_sb[:, 0:1], xT[:, G4 * n:G4 * n + G4, :].rearrange("d k t -> d (k t)"),
                                       ALU.add, ALU.add).then_inc(s["yT_sb"], 1)

            def output_tiles(n):
                return ps[0:TOK, Y_BANK, :].rearrange("p (k d) -> p k d", k=G4), slice(G4 * n, G4 * n + G4)

            def output_moments(n):
                y_ps, tiles = output_tiles(n)
                dve.wait_ge(s["y_ps"], n + 1)
                for t in range(G4):
                    m = v.bn_stats(stats[:, t, :], y_ps[:, t, :])
                step(m)
                for t in range(G4):
                    m = v.bn_aggr(meanvar[:, t, :], stats[:, t, :])
                step(m)
                v.tensor_scalar(veps[:, tiles], meanvar[:, 0:G4, 1], 1e-12, None, ALU.add).then_inc(s["y_var"], 1)

            def scale_output(n):
                y_ps, tiles = output_tiles(n)
                y = y_sb[:, n % 2]
                dve.wait_ge(s["y_pow"], n + 1)
                for t in range(G4):
                    m = v.tensor_scalar(y[:, t, :], y_ps[:, t, :], meanvar[:, t, 0:1], rstd[:, G4 * n + t:G4 * n + t + 1], ALU.subtract, ALU.mult)
                step(m)
                assert y_count[0] == Y_STEPS * n + Y_READ

            def add_output(n):
                y_ps, tiles = output_tiles(n)
                y, o = y_sb[:, n % 2], o_sb[:, n % 2]
                step(v.tensor_tensor(y, y, over_t(0), ALU.mult))
                assert y_count[0] == Y_STEPS * (n + 1)
                dve.wait_ge(s["beta_added"], n + 1)
                need(dve, f"out_stored{n % 2}", 16 * (n // 2))
                v.tensor_tensor(o, y, resid_k[:, tiles, :], ALU.add).then_inc(s["out_made"], 1)

            last_group = GROUPS - 1
            mask_tokens(0, 2)
            invert_sums(PAIRS - 1, 0, YT_BANK)
            invert_sums(PAIRS - 1, 1, Y_BANK)
            mask_tokens(0, 3)
            invert_sums(PAIRS - 1, 2, YT_BANK)
            invert_sums(PAIRS - 1, 3, Y_BANK)
            mask_tokens(1, 0)
            add_heads(PAIRS - 1, 0, YT_BANK)
            add_heads(PAIRS - 1, 1, Y_BANK)
            mask_tokens(1, 1)
            add_heads(PAIRS - 1, 2, YT_BANK)
            add_heads(PAIRS - 1, 3, Y_BANK)
            need(dve, "x2_done", PAIRS)
            moments(3, last_group)
            mask_tokens(1, 2)
            scale(3, last_group)
            dve.wait_ge(s["rows_ps"], 1)
            v.tensor_copy(rows_b.rearrange("p n d -> p (n d)"), ps[0:TOK, Y_BANK, 0:2 * D]).then_inc(s["rows_copied"], 1)
            mask_tokens(1, 3)
            mask_tokens(2, 0)
            read_logits(last_group, Y_BANK)
            choose_experts(G4 * last_group, PAIRS)
            mask_tokens(2, 1)
            take_output(0)
            mask_tokens(2, 2)
            mask_tokens(2, 3)
            mask_tokens(3, 0)
            output_moments(0)
            mask_tokens(3, 1)
            dve.wait_ge(s["rows_copied"], 1)
            scale_output(0)
            add_output(0)
            take_output(1)
            mask_tokens(3, 2)
            output_moments(1)
            mask_tokens(3, 3)
            take_output(2)
            scale_output(1)
            add_output(1)
            output_moments(2)
            scale_output(2)
            take_output(3)
            add_output(2)
            output_moments(3)
            scale_output(3)
            add_output(3)


_INS = ["x", "ctx_1024", "L0_attn_W_ih", "L0_attn_W_hh", "L0_attn_b_ih", "L0_attn_b_hh", "L0_attn_W_mu", "L0_attn_b_mu",
        "L0_attn_W_sig", "L0_attn_b_sig", "L0_xattn_WQ", "L0_xattn_WK", "L0_xattn_WV", "L0_xattn_WO", "L0_xattn_bO",
        "L0_ffn_W_router", "L0_ffn_W1", "L0_ffn_b1", "L0_ffn_Wo", "L0_ffn_bo", "L0_ffn_ln_gamma", "L0_ffn_ln_beta"]


def kernel(**inputs):
    import numpy as _np
    import concourse.bacc as _bacc
    from concourse import mybir as _mybir
    from concourse.bass_utils import run_bass_kernel_spmd as _run

    nc = _bacc.Bacc("TRN2", target_bir_lowering=False, num_devices=1)
    arrays, args = {}, []
    for name in _INS:
        a = _np.ascontiguousarray(inputs[name])
        arrays[f"in_{name}_dram"] = a
        args.append(nc.dram_tensor(f"in_{name}_dram", a.shape, _mybir.dt.from_np(a.dtype), kind="ExternalInput").ap())
    out = nc.dram_tensor("out_0_dram", inputs["x"].shape, _mybir.dt.float32, kind="ExternalOutput").ap()
    decoder_layer(nc, *args, out)
    r = _run(nc, [arrays], core_ids=[0])
    return r.results[0]["out_0_dram"]
```
